# Optimizing a Trainium2 kernel written in Bass

```python
import numpy as np
import jax
import jax.numpy as jnp

def _softmax(x, axis=-1):
    return jax.nn.softmax(x, axis=axis)

def _gelu(x):
    return jax.nn.gelu(x, approximate=True)

def _silu(x):
    return jax.nn.silu(x)

def _sigmoid(x):
    return jax.nn.sigmoid(x)

def _layernorm(x, axis=-1, eps=1e-05):
    m = jnp.mean(x, axis=axis, keepdims=True)
    v = jnp.var(x, axis=axis, keepdims=True)
    return (x - m) / jnp.sqrt(v + eps)

def _scatter_add(tgt, idx, src, axis=0):
    return tgt.at[idx].add(src)

def _segment_sum(src, seg, n):
    return jax.ops.segment_sum(src, seg, n)
kernel_name = 'mk_adj_ffn_d2_adj_r2_d09faa'

def setup_inputs(seed: int=0):
    np.random.seed(seed)
    _w = jnp.asarray

    def _rec_inputs():
        import jax
        import jax.numpy as jnp
        _gk = jax.random.key(seed)
        x = -0.0005207 + 1.001 * jax.random.normal(jax.random.fold_in(_gk, 1), (8192, 128), jnp.float32)
        _w = (1.0 + jnp.arange(8192, dtype=jnp.float32)) ** (-0.5)
        _w = _w / _w.mean()
        _pij = jnp.clip(0.000976562 * _w[:, None] * _w[None, :], 0.0, 1.0)
        _a = jax.random.uniform(jax.random.fold_in(_gk, 2), (8192, 8192)) < _pij
        _a = jnp.logical_or(_a, jnp.eye(8192, dtype=bool))
        _af = _a.astype(jnp.float32)
        _af = _af * jax.random.uniform(jax.random.fold_in(_gk, 3), (8192, 8192), jnp.float32, 0.05, 1)
        adj = _af
        return (x, adj)
    x, adj = _rec_inputs()

    def _L0_gnn_setup():
        import jax, jax.numpy as jnp
        import numpy as np
        N, F_IN, F_OUT = (4096, 128, 128)
        key = jax.random.key(seed)
        k1, k2, k3, k4 = jax.random.split(key, 4)
        X = jax.random.normal(k1, (N, F_IN), dtype=jnp.float32)
        A = jax.random.uniform(k2, (N, N), dtype=jnp.float32)
        W = jax.random.normal(k3, (F_OUT, F_IN), dtype=jnp.float32) * (1.0 / np.sqrt(F_IN))
        b = jax.random.normal(k4, (F_OUT,), dtype=jnp.float32) * 0.01
        return {'X': X, 'A': A, 'W': W, 'b': b}
    _L0_gnn_all = _L0_gnn_setup()
    _L0_gnn_in = {k: v for k, v in _L0_gnn_all.items() if k in ('W', 'b')}
    del _L0_gnn_all

    def _L0_ffn_setup():
        import jax, jax.numpy as jnp
        import numpy as np
        TOP_K = 2
        LN_EPS = 1e-05
        key = jax.random.key(seed)
        ks = jax.random.split(key, 8)
        B, S, D, E, H = (16, 512, 128, 8, 512)
        x = jax.random.normal(ks[0], (B, S, D), dtype=jnp.float32)
        Wr = jax.random.normal(ks[1], (D, E), dtype=jnp.float32) * 0.1
        br = jnp.zeros((E,), dtype=jnp.float32)
        ln_g = jnp.ones((E, D), dtype=jnp.float32)
        ln_b = jnp.zeros((E, D), dtype=jnp.float32)
        W1 = jax.random.normal(ks[2], (E, D, H), dtype=jnp.float32) * (1.0 / np.sqrt(D))
        b1 = jnp.zeros((E, H), dtype=jnp.float32)
        W2 = jax.random.normal(ks[3], (E, H, D), dtype=jnp.float32) * (1.0 / np.sqrt(H))
        b2 = jnp.zeros((E, D), dtype=jnp.float32)
        return {'x': x, 'Wr': Wr, 'br': br, 'ln_g': ln_g, 'ln_b': ln_b, 'W1': W1, 'b1': b1, 'W2': W2, 'b2': b2}
    _L0_ffn_all = _L0_ffn_setup()
    _L0_ffn_in = {k: v for k, v in _L0_ffn_all.items() if k in ('Wr', 'br', 'ln_g', 'ln_b', 'W1', 'b1', 'W2', 'b2')}
    del _L0_ffn_all

    def _L1_gnn_setup():
        import jax, jax.numpy as jnp
        import numpy as np
        N = 4096
        IN_F = 128
        OUT_F = 128
        ALPHA = 0.2
        key = jax.random.key(seed)
        k_x, k_adj, k_w, k_as, k_ad = jax.random.split(key, 5)
        x = jax.random.normal(k_x, (N, IN_F), dtype=jnp.float32)
        adj = (jax.random.uniform(k_adj, (N, N)) < 0.01).astype(jnp.float32)
        lim_w = float(np.sqrt(6.0 / (IN_F + OUT_F)))
        W = jax.random.uniform(k_w, (OUT_F, IN_F), minval=-lim_w, maxval=lim_w, dtype=jnp.float32)
        lim_a = float(np.sqrt(6.0 / (1 + OUT_F)))
        attn_src = jax.random.uniform(k_as, (1, OUT_F), minval=-lim_a, maxval=lim_a, dtype=jnp.float32)
        attn_dst = jax.random.uniform(k_ad, (1, OUT_F), minval=-lim_a, maxval=lim_a, dtype=jnp.float32)
        return {'x': x, 'adj': adj, 'W': W, 'attn_src': attn_src, 'attn_dst': attn_dst}
    _L1_gnn_all = _L1_gnn_setup()
    _L1_gnn_in = {k: v for k, v in _L1_gnn_all.items() if k in ('W', 'attn_src', 'attn_dst')}
    del _L1_gnn_all

    def _L1_ffn_setup():
        import jax, jax.numpy as jnp
        import numpy as np
        B, N, D = (16, 2048, 128)
        NUM_EXPERTS, TOP_K, HEADS = (4, 2, 4)
        N_EDGES = 524288
        LN_EPS = 1e-05

        def _layernorm(x, g, b):
            mu = x.mean(-1, keepdims=True)
            var = ((x - mu) ** 2).mean(-1, keepdims=True)
            return (x - mu) * jax.lax.rsqrt(var + LN_EPS) * g + b

        def _forward(x, edge_index, W_gat, att_src, att_dst, b_gat, ln_gamma, ln_beta, W1, b1, W2, b2):
            Bc, Nc, Dc = x.shape
            M = Bc * Nc
            x_flat = x.reshape(M, Dc)
            h = (x_flat @ W_gat).reshape(M, HEADS, NUM_EXPERTS)
            loops = jnp.arange(M, dtype=edge_index.dtype)
            src = jnp.concatenate([edge_index[0], loops])
            dst = jnp.concatenate([edge_index[1], loops])
            a_src = (h * att_src).sum(-1)
            a_dst = (h * att_dst).sum(-1)
            e = jax.nn.leaky_relu(a_src[src] + a_dst[dst], negative_slope=0.2)
            e_max = jax.ops.segment_max(e, dst, num_segments=M)
            ee = jnp.exp(e - e_max[dst])
            denom = jax.ops.segment_sum(ee, dst, num_segments=M)
            alpha = ee / (denom[dst] + 1e-16)
            msg = h[src] * alpha[:, :, None]
            agg = jax.ops.segment_sum(msg, dst, num_segments=M).reshape(M, HEADS * NUM_EXPERTS) + b_gat
            scores = _layernorm(agg, ln_gamma, ln_beta).reshape(M, HEADS, NUM_EXPERTS).mean(1)
            scores = scores.reshape(Bc, Nc, NUM_EXPERTS)
            topk_s, topk_i = jax.lax.top_k(scores, TOP_K)
            w = jax.nn.softmax(topk_s, axis=-1)
            out = jnp.zeros_like(x)
            for ei in range(NUM_EXPERTS):
                g = jnp.where(topk_i == ei, w, 0.0).sum(-1)
                hh = jax.nn.gelu(x @ W1[ei] + b1[ei], approximate=False)
                out = out + g[..., None] * (hh @ W2[ei] + b2[ei])
            return out
        key = jax.random.key(seed)
        ks = jax.random.split(key, 8)
        s = 0.05
        return {'x': jax.random.normal(ks[0], (B, N, D), jnp.float32), 'W_gat': jax.random.normal(ks[1], (D, HEADS * NUM_EXPERTS), jnp.float32) * s, 'att_src': jax.random.normal(ks[2], (HEADS, NUM_EXPERTS), jnp.float32) * s, 'att_dst': jax.random.normal(ks[3], (HEADS, NUM_EXPERTS), jnp.float32) * s, 'b_gat': jnp.zeros((HEADS * NUM_EXPERTS,), jnp.float32), 'ln_gamma': jnp.ones((HEADS * NUM_EXPERTS,), jnp.float32), 'ln_beta': jnp.zeros((HEADS * NUM_EXPERTS,), jnp.float32), 'W1': jax.random.normal(ks[4], (NUM_EXPERTS, D, 2 * D), jnp.float32) * s, 'b1': jnp.zeros((NUM_EXPERTS, 2 * D), jnp.float32), 'W2': jax.random.normal(ks[5], (NUM_EXPERTS, 2 * D, D), jnp.float32) * s, 'b2': jnp.zeros((NUM_EXPERTS, D), jnp.float32), 'edge_index': jax.random.randint(ks[6], (2, N_EDGES), 0, B * N, jnp.int32)}
    _L1_ffn_all = _L1_ffn_setup()
    _L1_ffn_in = {k: v for k, v in _L1_ffn_all.items() if k in ('W_gat', 'att_src', 'att_dst', 'b_gat', 'ln_gamma', 'ln_beta', 'W1', 'b1', 'W2', 'b2', 'edge_index')}
    del _L1_ffn_all
    return {'x': x, 'adj': adj, 'L0_gnn_W': _L0_gnn_in['W'], 'L0_gnn_b': _L0_gnn_in['b'], 'L0_ffn_Wr': _L0_ffn_in['Wr'], 'L0_ffn_br': _L0_ffn_in['br'], 'L0_ffn_ln_g': _L0_ffn_in['ln_g'], 'L0_ffn_ln_b': _L0_ffn_in['ln_b'], 'L0_ffn_W1': _L0_ffn_in['W1'], 'L0_ffn_b1': _L0_ffn_in['b1'], 'L0_ffn_W2': _L0_ffn_in['W2'], 'L0_ffn_b2': _L0_ffn_in['b2'], 'L1_gnn_W': _L1_gnn_in['W'], 'L1_gnn_attn_src': _L1_gnn_in['attn_src'], 'L1_gnn_attn_dst': _L1_gnn_in['attn_dst'], 'L1_ffn_W_gat': _L1_ffn_in['W_gat'], 'L1_ffn_att_src': _L1_ffn_in['att_src'], 'L1_ffn_att_dst': _L1_ffn_in['att_dst'], 'L1_ffn_b_gat': _L1_ffn_in['b_gat'], 'L1_ffn_ln_gamma': _L1_ffn_in['ln_gamma'], 'L1_ffn_ln_beta': _L1_ffn_in['ln_beta'], 'L1_ffn_W1': _L1_ffn_in['W1'], 'L1_ffn_b1': _L1_ffn_in['b1'], 'L1_ffn_W2': _L1_ffn_in['W2'], 'L1_ffn_b2': _L1_ffn_in['b2'], 'L1_ffn_edge_index': _L1_ffn_in['edge_index']}

def reference(x, adj, L0_gnn_W, L0_gnn_b, L0_ffn_Wr, L0_ffn_br, L0_ffn_ln_g, L0_ffn_ln_b, L0_ffn_W1, L0_ffn_b1, L0_ffn_W2, L0_ffn_b2, L1_gnn_W, L1_gnn_attn_src, L1_gnn_attn_dst, L1_ffn_W_gat, L1_ffn_att_src, L1_ffn_att_dst, L1_ffn_b_gat, L1_ffn_ln_gamma, L1_ffn_ln_beta, L1_ffn_W1, L1_ffn_b1, L1_ffn_W2, L1_ffn_b2, L1_ffn_edge_index):
    import jax
    import jax.numpy as jnp

    def _L0_gnn_ref(X, A, W, b):
        import jax, jax.numpy as jnp
        import numpy as np
        N, F_IN, F_OUT = (4096, 128, 128)
        A_hat = A + jnp.eye(A.shape[0], dtype=A.dtype)
        deg = jnp.sum(A_hat, axis=1)
        d = jnp.where(deg > 0, jax.lax.rsqrt(deg), 0.0)
        A_norm = d[:, None] * A_hat * d[None, :]
        out = A_norm @ X
        out = out @ W.T + b
        return out

    def _L0_ffn_ref(x, Wr, br, ln_g, ln_b, W1, b1, W2, b2):
        import jax, jax.numpy as jnp
        import numpy as np
        TOP_K = 2
        LN_EPS = 1e-05
        B, S, D = x.shape
        N = B * S
        xt = x.reshape(N, D)
        logits = xt @ Wr + br
        probs = jax.nn.softmax(logits, axis=-1)
        top_p, top_idx = jax.lax.top_k(probs, TOP_K)
        weights = top_p / top_p.sum(axis=-1, keepdims=True)
        mu = xt.mean(axis=-1, keepdims=True)
        var = ((xt - mu) ** 2).mean(axis=-1, keepdims=True)
        xn = (xt - mu) * jax.lax.rsqrt(var + LN_EPS)
        xe = xn[None, :, :] * ln_g[:, None, :] + ln_b[:, None, :]
        h = jax.nn.gelu(jnp.einsum('end,edh->enh', xe, W1) + b1[:, None, :], approximate=False)
        y = jnp.einsum('enh,ehd->end', h, W2) + b2[:, None, :]
        y_tok = jnp.transpose(y, (1, 0, 2))
        sel = jnp.take_along_axis(y_tok, top_idx[:, :, None], axis=1)
        out = (weights[:, :, None] * sel).sum(axis=1)
        return out.reshape(B, S, D)

    def _L1_gnn_ref(x, adj, W, attn_src, attn_dst):
        import jax, jax.numpy as jnp
        import numpy as np
        N = 4096
        IN_F = 128
        OUT_F = 128
        ALPHA = 0.2
        h = x @ W.T
        a_src = (h * attn_src).sum(axis=-1)
        a_dst = (h * attn_dst).sum(axis=-1)
        scores = a_src[None, :] + a_dst[:, None]
        mask = (adj > 0).astype(h.dtype)
        s = jnp.where(scores > 0, scores, ALPHA * scores) * mask
        s = s - jnp.max(s, axis=1, keepdims=True)
        e = jnp.exp(s) * mask
        w = e / (jnp.sum(e, axis=1, keepdims=True) + 1e-08)
        out = w @ h
        return jax.nn.elu(out)

    def _L1_ffn_ref(x, W_gat, att_src, att_dst, b_gat, ln_gamma, ln_beta, W1, b1, W2, b2, edge_index):
        import jax, jax.numpy as jnp
        import numpy as np
        B, N, D = (16, 2048, 128)
        NUM_EXPERTS, TOP_K, HEADS = (4, 2, 4)
        N_EDGES = 524288
        LN_EPS = 1e-05

        def _layernorm(x, g, b):
            mu = x.mean(-1, keepdims=True)
            var = ((x - mu) ** 2).mean(-1, keepdims=True)
            return (x - mu) * jax.lax.rsqrt(var + LN_EPS) * g + b

        def _forward(x, edge_index, W_gat, att_src, att_dst, b_gat, ln_gamma, ln_beta, W1, b1, W2, b2):
            Bc, Nc, Dc = x.shape
            M = Bc * Nc
            x_flat = x.reshape(M, Dc)
            h = (x_flat @ W_gat).reshape(M, HEADS, NUM_EXPERTS)
            loops = jnp.arange(M, dtype=edge_index.dtype)
            src = jnp.concatenate([edge_index[0], loops])
            dst = jnp.concatenate([edge_index[1], loops])
            a_src = (h * att_src).sum(-1)
            a_dst = (h * att_dst).sum(-1)
            e = jax.nn.leaky_relu(a_src[src] + a_dst[dst], negative_slope=0.2)
            e_max = jax.ops.segment_max(e, dst, num_segments=M)
            ee = jnp.exp(e - e_max[dst])
            denom = jax.ops.segment_sum(ee, dst, num_segments=M)
            alpha = ee / (denom[dst] + 1e-16)
            msg = h[src] * alpha[:, :, None]
            agg = jax.ops.segment_sum(msg, dst, num_segments=M).reshape(M, HEADS * NUM_EXPERTS) + b_gat
            scores = _layernorm(agg, ln_gamma, ln_beta).reshape(M, HEADS, NUM_EXPERTS).mean(1)
            scores = scores.reshape(Bc, Nc, NUM_EXPERTS)
            topk_s, topk_i = jax.lax.top_k(scores, TOP_K)
            w = jax.nn.softmax(topk_s, axis=-1)
            out = jnp.zeros_like(x)
            for ei in range(NUM_EXPERTS):
                g = jnp.where(topk_i == ei, w, 0.0).sum(-1)
                hh = jax.nn.gelu(x @ W1[ei] + b1[ei], approximate=False)
                out = out + g[..., None] * (hh @ W2[ei] + b2[ei])
            return out
        return _forward(x, edge_index, W_gat, att_src, att_dst, b_gat, ln_gamma, ln_beta, W1, b1, W2, b2)
    x = x + _L0_gnn_ref(_layernorm(x, axis=-1), adj, L0_gnn_W, L0_gnn_b)
    x = x + _L0_ffn_ref(_layernorm(x, axis=-1)[None], L0_ffn_Wr, L0_ffn_br, L0_ffn_ln_g, L0_ffn_ln_b, L0_ffn_W1, L0_ffn_b1, L0_ffn_W2, L0_ffn_b2)[0]
    x = x + _L1_gnn_ref(_layernorm(x, axis=-1), adj, L1_gnn_W, L1_gnn_attn_src, L1_gnn_attn_dst)
    x = x + _L1_ffn_ref(_layernorm(x, axis=-1)[None], L1_ffn_W_gat, L1_ffn_att_src, L1_ffn_att_dst, L1_ffn_b_gat, L1_ffn_ln_gamma, L1_ffn_ln_beta, L1_ffn_W1, L1_ffn_b1, L1_ffn_W2, L1_ffn_b2, L1_ffn_edge_index)[0]
    return x

_drawn_inputs = setup_inputs


def setup_inputs(seed=0):
    import zlib

    import numpy as np

    out = dict(_drawn_inputs(seed))
    spreads = {'L0_ffn_br': (0.0, 0.1),
     'L0_ffn_ln_g': (1.0, 0.2),
     'L0_ffn_ln_b': (0.0, 0.1),
     'L0_ffn_b1': (0.0, 0.1),
     'L0_ffn_b2': (0.0, 0.1),
     'L1_ffn_b_gat': (0.0, 0.1),
     'L1_ffn_ln_gamma': (1.0, 0.6),
     'L1_ffn_ln_beta': (0.0, 0.1),
     'L1_ffn_b1': (0.0, 0.328),
     'L1_ffn_b2': (0.0, 0.1)}
    factors = {'L1_ffn_att_src': 5.444, 'L1_ffn_att_dst': 7.212}
    for name, (base, spread) in spreads.items():
        noise = np.random.default_rng([zlib.crc32(name.encode()), seed]).standard_normal(out[name].shape)
        drawn = base * np.exp(spread * noise) if base else spread * noise
        out[name] = jnp.asarray(drawn.astype(out[name].dtype))
    for name, factor in factors.items():
        out[name] = (out[name] * factor).astype(out[name].dtype)
    return out
```

```python
from contextlib import ExitStack

import concourse.bass as bass
from concourse import mybir

F32 = mybir.dt.float32
I32 = mybir.dt.int32
BF16 = mybir.dt.bfloat16
U16 = mybir.dt.uint16
ALU = mybir.AluOpType
ACT = mybir.ActivationFunctionType
AX = mybir.AxisListType

P = 128
BANK = 512
EPS = 1e-5


class Chain:

    def __init__(self, eng, sem):
        self.eng, self.sem, self.n, self.trip = eng, sem, 0, None

    def __call__(self, ins):
        self.n += 1
        ins.then_inc(self.sem, 1)
        self.eng.wait_ge(self.sem, self.n if self.trip is None else self.trip + self.n)

    def enter(self, i, per, first=0):
        self.trip, self.start, self.per = i * per, self.n, per
        self.n -= first * per

    def leave(self, trips, first=0):
        assert self.n + first * self.per - self.start == self.per, (self.n + first * self.per - self.start, self.per)
        self.trip, self.n = None, self.start + trips * self.per


def build(nc, d, out):
    N = d["x"].shape[0]
    T = N // P
    IB = 2048
    NB = N // IB
    TB = IB // P
    E0, H0 = d["W1a"].shape[1], d["W1a"].shape[2]
    E1, H1 = d["W1b"].shape[1], d["W1b"].shape[2]
    C0, C1 = H0 // P, H1 // P
    SB4 = 4
    NBLK = T // SB4
    HEADS = 4
    EX = E1
    HF = HEADS * EX
    TW = HF + HEADS

    NE = d["pairs"].shape[0]
    EC = NE // P
    GRP = 4
    GE = GRP * P
    NG = NE // GE + T
    NGP = -(-(NG + 2) // P) * P
    NQ = 4
    QL = EC // NQ
    SC = 16

    sorted_d = nc.dram_tensor("sorted_edges", (NGP * GE, 2), I32, kind="Internal").ap()
    table_d = nc.dram_tensor("node_table", (N, TW), F32, kind="Internal").ap()
    gb_d = nc.dram_tensor("group_bucket", (NGP,), I32, kind="Internal").ap()
    q_d = nc.dram_tensor("score_factors", (P, P), F32, kind="Internal").ap()

    with ExitStack() as c:
        def sb(n, s, dt=F32):
            return c.enter_context(nc.sbuf_tensor(n, s, dt))

        def sem(n):
            return c.enter_context(nc.semaphore(n))

        ps = c.enter_context(nc.psum_tensor("ps", [P, 8, BANK], F32))

        resid = sb("resid", [P, T, P])
        feat = sb("feat", [P, T * 130])
        work = sb("work", [P, 18432])
        edge = sb("edge", [P, 3 * EC])
        ident = sb("ident", [P, P])
        lower = sb("lower", [P, P])
        ones = sb("ones", [P, P])
        iota_i = sb("iota_i", [P, P], I32)
        iota = sb("iota", [P, P])
        zeros_b = sb("zeros_b", [P, BANK], BF16)
        w0t = sb("w0t", [P, P])
        wr = sb("wr", [P, E0])
        rows = sb("rows", [P, P + E0 + 5 * HF])
        b2a = sb("b2a", [E0, P])
        b2b = sb("b2b", [E1, P])
        lngb = sb("lngb", [P, 2, E0])
        b1a = sb("b1a", [P, E0 * C0])
        b1b = sb("b1b", [P, E1 * C1])
        wg = sb("wg", [P, P])
        wext = sb("wext", [P, P + 2])
        att = sb("att", [P, 2])
        wgat = sb("wgat", [P, HF + 2 * HEADS])
        stats = sb("stats", [P, 2, TB])
        deg2 = sb("deg2", [P, T, 2])
        dinv = sb("dinv", [P, T])
        dmask = sb("dmask", [P, T])
        gates = sb("gates", [P, T, 8])
        gst = sb("gst", [P, SB4, 8])
        top = sb("top", [P, SB4, 8])
        topi = sb("topi", [P, SB4, 8], mybir.dt.uint32)
        tops = sb("tops", [P, 4, T])
        wts = sb("wts", [P, 2, T])
        gts = sb("gts", [8, BANK])
        small = sb("small", [P, 16])
        asd = sb("asd", [P, 2, T])
        fac = sb("fac", [P, 5, T])
        cnt = sb("cnt", [P, T])
        ngi = sb("ngi", [P, T], I32)
        ngf = sb("ngf", [P, T])
        gend = sb("gend", [P, T])
        cur = sb("cur", [P, T])
        gid_i = sb("gid_i", [P, NGP // P], I32)
        gid = sb("gid", [P, NGP // P])
        gbf = sb("gbf", [P, NGP // P])
        gbi = sb("gbi", [P, NGP // P], I32)
        gcount = sb("gcount", [P, 1], I32)
        stg_i = sb("stg_i", [P, 2, SC], I32)
        stg_p = sb("stg_p", [P, 2, SC, 2], I32)

        bias0 = rows[:, 0:P]
        brr = rows[:, P:P + E0]
        attr = rows[:, P + E0:P + E0 + 2 * HF].rearrange("p (s h e) -> p s h e", s=2, h=HEADS)
        bgat = rows[:, P + E0 + 2 * HF:P + E0 + 3 * HF]
        gam = rows[:, P + E0 + 3 * HF:P + E0 + 4 * HF]
        bet = rows[:, P + E0 + 4 * HF:P + E0 + 5 * HF]

        pairs = edge[:, 0:2 * EC].bitcast(I32).rearrange("p (e two) -> p e two", two=2)
        pos = edge[:, 2 * EC:3 * EC].bitcast(I32)
        NS1 = 3
        HALF = N // 2
        arow = [work[:, r * HALF:(r + 1) * HALF] for r in range(NS1)]
        ew = NS1 * HALF
        dh = work[:, ew:ew + EC // 2].bitcast(BF16)
        junk = work[:, ew + EC // 2:ew + EC].bitcast(BF16)
        mk = work[:, ew + EC:ew + EC + QL // 2].bitcast(BF16)
        ones_b = work[:, ew + EC + QL // 2:ew + EC + QL].bitcast(BF16)
        sc = work[:, ew + EC + QL:ew + EC + 2 * QL].bitcast(I32)
        assert ew + EC + 2 * QL <= 18432
        lnw = edge[:, 0:0]
        NS2 = 4
        at2 = [work[:, r * IB:(r + 1) * IB] for r in range(NS2)]
        agg = work[:, NS2 * IB:(NS2 + 1) * IB]
        xs = work[:, (NS2 + 1) * IB:(NS2 + 1) * IB + NS2 * P].rearrange("p (r f) -> p r f", r=NS2)
        assert (NS2 + 1) * IB + NS2 * P <= ew
        featp = feat[:, 0:T * P].rearrange("p (t f) -> p t f", t=T)
        feath = feat[:, :].rearrange("p (t f) -> p t f", t=T)
        featT = feat[:, 0:N]
        w1 = work[:, 0:4096]
        w2 = work[:, 4096:8192]
        w1av = w1.rearrange("p (e h) -> p e h", e=E0)
        w2av = w2.rearrange("p (e c f) -> p e c f", e=E0, c=C0)
        w1bv = w1[:, 0:E1 * H1].rearrange("p (e h) -> p e h", e=E1)
        w2bv = w2[:, 0:E1 * C1 * P].rearrange("p (e c f) -> p e c f", e=E1, c=C1)
        hid = [work[:, 8192 + r * 2048:8192 + (r + 1) * 2048].rearrange("p (c n) -> p c n", n=BANK) for r in range(2)]
        u4 = work[:, 12288:12288 + BANK].rearrange("p (t f) -> p t f", t=SB4)
        n4 = work[:, 12800:12800 + BANK].rearrange("p (t f) -> p t f", t=SB4)
        uT = work[:, 13312:13312 + BANK]
        sq4 = work[:, 13824:13824 + BANK].rearrange("p (t f) -> p t f", t=SB4)
        NS6 = 5
        at6 = [work[:, r * IB:(r + 1) * IB] for r in range(NS6)]
        prod = [work[:, (NS6 + r) * IB:(NS6 + r + 1) * IB] for r in range(2)]
        qb = work[:, (NS6 + 2) * IB:(NS6 + 4) * IB].rearrange("p (k n) -> p k n", k=2)
        rden = stats[:, 0, :]
        oh = work[:, 0:2 * GRP * P].rearrange("p (r c n) -> p r c n", r=2, c=GRP)
        oht = work[:, 2 * GRP * P:4 * GRP * P].rearrange("p (r c n) -> p r c n", r=2, c=GRP)
        o = 4 * GRP * P
        gt = work[:, o:o + 2 * GRP * TW].rearrange("p (r c k) -> p r c k", r=2, c=GRP)
        o += 2 * GRP * TW
        vals = work[:, o:o + 2 * GRP * TW].rearrange("p (r c k) -> p r c k", r=2, c=GRP)
        o += 2 * GRP * TW
        pt = work[:, o:o + 4 * GRP].bitcast(I32).rearrange("p (r c k) -> p r c k", r=2, c=GRP)
        o += 4 * GRP
        dlf = work[:, o:o + 2 * GRP].rearrange("p (r c) -> p r c", r=2)
        o += 2 * GRP
        zt = work[:, o:o + GRP * HEADS].rearrange("p (c k) -> p c k", c=GRP)
        o += GRP * HEADS
        assert o <= 8192
        gb = work[0:1, 8192:8192 + NGP].bitcast(I32)
        o = 0
        ntab = edge[:, o:o + T * 24].rearrange("p (t k) -> p t k", t=T)
        o += T * 24
        dtab = edge[:, o:o + T * 8].rearrange("p (t k) -> p t k", t=T)
        o += T * 8
        acc = edge[:, o:o + T * TW].rearrange("p (t k) -> p t k", t=T)
        o += T * TW
        ee = edge[:, o:o + T * HEADS].rearrange("p (t k) -> p t k", t=T)
        o += T * HEADS
        ag = edge[:, o:o + T * HF].rearrange("p (t k) -> p t k", t=T)
        o += T * HF
        ag2 = edge[:, o:o + T * HF].rearrange("p (t k) -> p t k", t=T)
        o += T * HF
        lg8 = edge[:, o:o + T * 8].rearrange("p (t k) -> p t k", t=T)
        o += T * 8
        lst = edge[:, o:o + 2 * T].rearrange("p (s t) -> p s t", s=2)
        o += 2 * T
        gcmp = edge[:, 0:1]
        fillt = feat[:, 0:2 * NGP * GE // P // 8].bitcast(I32)
        assert 2 * NGP * GE // P // 8 <= T * 130

        const = sem("const"); fill_made = sem("fill_made"); filled = sem("filled")
        pairs_in = sem("pairs_in"); x_in = sem("x_in"); small_in = sem("small_in")
        arow_in = [sem(f"arow_in{r}") for r in range(NS1)]
        row_summed = sem("row_summed")
        dve_c = sem("dve_c"); act_c = sem("act_c")
        var_ready = sem("var_ready"); std_ready = sem("std_ready")
        counts = sem("counts"); offs = sem("offs"); cur_moved = sem("cur_moved"); pos_ready = sem("pos_ready")
        scat = [sem("scat0"), sem("scat1")]; staged = sem("staged"); slot_open = sem("slot_open"); slot_taken = sem("slot_taken"); sorting = sem("sorting")
        gbi_ready = sem("gbi_ready"); gb_out = sem("gb_out"); gb_in = sem("gb_in"); scattered = sem("scattered")
        feats0 = sem("feats0")
        at_in = [sem(f"at_in{r}") for r in range(NS2)]
        staged_x = sem("staged_x"); tile_used = sem("tile_used"); agg_ready = sem("agg_ready")
        agg_copied = sem("agg_copied"); lin_ready = sem("lin_ready"); x1_ready = sem("x1_ready")
        w1_in = sem("w1_in"); wa_ready = sem("wa_ready"); b1_ready = sem("b1_ready"); b1_done = sem("b1_done")
        ln_ready = sem("ln_ready"); tr_ready = sem("tr_ready"); tr_copied = sem("tr_copied")
        lg_ready = sem("lg_ready"); tops_done = sem("tops_done"); exp_ready = sem("exp_ready"); gates_ready = sem("gates_ready")
        gst_ready = sem("gst_ready"); gt_ready = sem("gt_ready"); gts_ready = sem("gts_ready"); bt_ready = sem("bt_ready")
        h_ready = sem("h_ready"); hid_ready = sem("hid_ready"); y_ready = sem("y_ready"); y_added = sem("y_added")
        hx_ready = sem("hx_ready"); hx_copied = sem("hx_copied"); wext_ready = sem("wext_ready"); wext_done = sem("wext_done")
        mx_ready = sem("mx_ready"); mxt_ready = sem("mxt_ready"); mxd_ready = sem("mxd_ready"); mxb_ready = sem("mxb_ready")
        fac_in = sem("fac_in"); fac_ready = sem("fac_ready"); qt_ready = sem("qt_ready"); qs_ready = sem("qs_ready"); q_out = sem("q_out"); q_in = sem("q_in")
        a6_in = [sem(f"a6_in{r}") for r in range(NS6)]
        p_ready = sem("p_ready"); e_ready = sem("e_ready"); e_used = sem("e_used"); att_ready = sem("att_ready")
        vpos = sem("vpos"); eneg = sem("eneg"); x3_ready = sem("x3_ready")
        block_done = sem("block_done"); ln3_ready = sem("ln3_ready"); tr3_ready = sem("tr3_ready"); tr3_copied = sem("tr3_copied"); gat_ready = sem("gat_ready"); gat_copied = sem("gat_copied")
        wgat_done = sem("wgat_done"); ntab_ready = sem("ntab_ready"); tab_out = sem("tab_out")
        emx = sem("emx"); emxt = sem("emxt"); emxd = sem("emxd"); emxb = sem("emxb")
        self_in = sem("self_in"); self_exp = sem("self_exp")
        pt_in = [sem("pt_in0"), sem("pt_in1")]; gathered = [sem("gathered0"), sem("gathered1")]
        oh_ready = sem("oh_ready"); ohp_ready = sem("ohp_ready"); oht_ready = sem("oht_ready"); dst_ready = sem("dst_ready")
        z_ready = sem("z_ready"); ez_ready = sem("ez_ready"); vals_ready = sem("vals_ready"); sum_ready = sem("sum_ready")
        grp_c = sem("grp_c")
        w1b_in = sem("w1b_in")
        out_ready = sem("out_ready"); out_done = sem("out_done")

        NW = 15
        ring = 4

        block = c.enter_context(nc.Block())

        @block.sync
        def _(sp):
            sp.dma_start(pairs[:, :, :], d["pairs"].rearrange("(p e) two -> p e two", p=P)).then_inc(pairs_in, 16)
            sp.dma_start(resid[:, :, :], d["x"].rearrange("(t p) f -> p t f", p=P)).then_inc(x_in, 16)

            def row(ap):
                return ap.rearrange("(a n) -> a n", a=1).to_broadcast([P, ap.shape[0]])

            loads = [(w0t[:, :], d["W0T"]), (wr[:, :], d["Wr"]), (bias0, row(d["b0"])), (brr, row(d["br"])),
                     (attr[:, 0].rearrange("p h e -> p (h e)"), row(d["att_src"])),
                     (attr[:, 1].rearrange("p h e -> p (h e)"), row(d["att_dst"])),
                     (bgat, row(d["b_gat"])), (gam, row(d["ln_gamma"])), (bet, row(d["ln_beta"])),
                     (b2a[:, :], d["b2a"]), (b2b[:, :], d["b2b"]),
                     (lngb[:, :, :], d["lngb"]), (b1a[:, :], d["b1a"]), (b1b[:, :], d["b1b"]),
                     (wg[:, :], d["Wg"]), (wext[:, 0:P], d["WgT"]), (att[:, :], d["attn"]),
                     (wgat[:, 0:HF], d["W_gat"])]
            for dst, src in loads:
                sp.dma_start(dst, src).then_inc(small_in, 16)

            halves = d["adj"].rearrange("(t p) (h n) -> t h p n", p=P, h=2)

            def load_half(n, r):
                sp.dma_start(arow[r], halves[n // 2, n % 2]).then_inc(arow_in[r], 16)

            for n in range(NS1):
                load_half(n, n)
            full = (2 * T - NS1) // 6
            with sp.Fori(0, full) as i:
                for k in range(6):
                    r = k % NS1
                    n = 6 * i + k
                    sp.wait_ge(row_summed, 6 * i + (k + 1))
                    m = k + NS1
                    sp.dma_start(arow[r], halves[3 * i + m // 2, m % 2]).then_inc(arow_in[r], 16)
            for n in range(6 * full + NS1, 2 * T):
                sp.wait_ge(row_summed, n - NS1 + 1)
                load_half(n, n % NS1)

            sp.wait_ge(gbi_ready, 1)
            with nc.allow_non_contiguous_dma(reason="one word per group of edges"):
                sp.dma_start(gb_d.rearrange("(k p) -> p k", p=P), gbi[:, :]).then_inc(gb_out, 16)

            tiles = d["adjT"].rearrange("k (j p) n -> (k j) p n", p=P)
            sp.wait_ge(row_summed, 2 * T)
            for r in range(NS2):
                sp.dma_start(at2[r], tiles[r]).then_inc(at_in[r], 16)
            with sp.Fori(0, NB * T // NS2 - 1) as i:
                for r in range(NS2):
                    sp.wait_ge(tile_used, i * NS2 + (NS2 + r + 1))
                    sp.dma_start(at2[r], tiles[i * NS2 + (NS2 + r)]).then_inc(at_in[r], 16)

            sp.wait_ge(x1_ready, NB)
            sp.wait_ge(pos_ready, NQ)
            sp.dma_start(w1av, d["W1a"]).then_inc(w1_in, 16)
            sp.dma_start(w2av, d["W2a"]).then_inc(w1_in, 16)

            sp.wait_ge(qs_ready, 1)
            sp.dma_start(q_d, n4[:, 0, :]).then_inc(q_out, 16)
            for r in range(NS6):
                sp.dma_start(at6[r], tiles[r]).then_inc(a6_in[r], 16)
            total = NB * T
            full = (total - NS6) // NS6
            with sp.Fori(0, full) as i:
                for r in range(NS6):
                    sp.wait_ge(e_used, i * NS6 + (r + 1))
                    sp.dma_start(at6[r], tiles[i * NS6 + (NS6 + r)]).then_inc(a6_in[r], 16)
            for n in range(full * NS6, total - NS6):
                sp.wait_ge(e_used, n + 1)
                sp.dma_start(at6[n % NS6], tiles[n + NS6]).then_inc(a6_in[n % NS6], 16)

            sp.wait_ge(ntab_ready, 1)
            sp.dma_start(table_d.rearrange("(t p) k -> p t k", p=P), ntab[:, :, 0:TW]).then_inc(tab_out, 16)
            sp.wait_ge(gb_out, 16)
            sp.dma_start(gb, gb_d.rearrange("(a g) -> a g", a=1)).then_inc(gb_in, 16)
            sp.wait_ge(scattered, 1)
            trips = sp.value_load(gcount[0:1, 0:1], min_val=1, max_val=(NG + 1) // 2)
            groups = sorted_d.rearrange("(g p r) two -> g p (r two)", p=P, r=GRP)

            def flat(r):
                return pt[:, r, :, :].rearrange("p c k -> p (c k)")

            for r in range(2):
                sp.dma_start(flat(r), groups[r]).then_inc(pt_in[r], 16)
            with sp.Fori(0, trips) as i:
                for r in range(2):
                    sp.wait_ge(gathered[r], (i + 1) * 16 * GRP)
                    sp.wait_ge(oh_ready, i * 2 + (r + 1))
                    sp.dma_start(flat(r), groups[i * 2 + (2 + r)]).then_inc(pt_in[r], 16)

            sp.wait_ge(gates_ready, 2)
            sp.dma_start(w1bv, d["W1b"]).then_inc(w1b_in, 16)
            sp.dma_start(w2bv, d["W2b"]).then_inc(w1b_in, 16)
            sp.wait_ge(out_ready, 1)
            sp.dma_start(out.rearrange("(t p) f -> p t f", p=P), resid[:, :, :]).then_inc(out_done, 16)
            sp.wait_ge(out_done, 16)

        @block.gpsimd
        def _(pool):
            pool.iota(iota_i[:, :], pattern=[[1, P]], base=0, channel_multiplier=0).then_inc(const, 1)
            pool.iota(gid_i[:, :], pattern=[[P, NGP // P]], base=0, channel_multiplier=1).then_inc(const, 1)
            pool.memset(ones[:, :], 1.0).then_inc(const, 1)
            pool.memset(ident[:, :], 0.0).then_inc(const, 1)
            pool.memset(zeros_b[:, :], 0.0).then_inc(const, 1)
            pool.memset(fillt, -1).then_inc(fill_made, 1)
            pool.wait_ge(const, 5)
            pool.affine_select(out=ident[:, :], in_=ident[:, :], compare_op=ALU.not_equal, fill=1.0, base=0,
                               pattern=[[-1, P]], channel_multiplier=1).then_inc(const, 1)
            pool.affine_select(out=lower[:, :], in_=ones[:, :], compare_op=ALU.is_gt, fill=0.0, base=0,
                               pattern=[[1, P]], channel_multiplier=-1).then_inc(const, 1)
            pool.wait_ge(fill_made, 1)
            fill_v = sorted_d.rearrange("(k p r) two -> k p (r two)", k=8, p=P)
            for k in range(8):
                pool.dma_start(fill_v[k], fillt).then_inc(filled, 16)
            slot_bound = pool.to_reg(NG * GE - 1)
            node_bound = pool.to_reg(N - 1)
            pool.wait_ge(filled, 16 * 8)

            def scatter(n, first):
                for r in range(2):
                    if not first:
                        pool.wait_ge(scat[r], n * (16 * SC))
                    pool.tensor_copy(stg_i[:, r, :], pos[:, bass.ds(n * (2 * SC) + r * SC, SC)]).then_inc(staged, 1)
                    pool.tensor_copy(stg_p[:, r, :, :], pairs[:, bass.ds(n * (2 * SC) + r * SC, SC), :]).then_inc(staged, 1)
                    pool.wait_ge(staged, n * 4 + (2 * r + 2))
                    pool.sem_inc(slot_open, 1)
                    for k in range(SC):
                        pool.indirect_dma_start(sorted_d, bass.IndirectOffsetOnAxis(ap=stg_i[:, r, k:k + 1], axis=0),
                                                stg_p[:, r, k, :], None, bounds_check=slot_bound,
                                                oob_is_err=False).then_inc(scat[r], 16)

            per = QL // (2 * SC)
            for q in range(NQ):
                pool.wait_ge(pos_ready, q + 1)
                if q == 0:
                    scatter(0, True)
                with pool.Fori(q * per + (q == 0), (q + 1) * per) as n:
                    scatter(n, False)
            for r in range(2):
                pool.wait_ge(scat[r], 16 * SC * per * NQ)
            pool.sem_inc(scattered, 1)

            pool.wait_ge(tab_out, 16)
            trips = pool.value_load(gcount[0:1, 0:1], min_val=1, max_val=(NG + 1) // 2)
            with pool.Fori(0, trips) as i:
                for r in range(2):
                    pool.wait_ge(pt_in[r], (i + 1) * 16)
                    pool.wait_ge(vals_ready, i * 2 + (r + 1))
                    pool.sem_inc(slot_open, 1)
                    for k in range(GRP):
                        pool.indirect_dma_start(gt[:, r, k, :], None, table_d,
                                                bass.IndirectOffsetOnAxis(ap=pt[:, r, k, 0:1], axis=0),
                                                bounds_check=node_bound, oob_is_err=False).then_inc(gathered[r], 16)

        @block.vector
        def _(dve):
            link = Chain(dve, dve_c)
            nvar = [0]

            def bc(ap, shape, axis=2):
                return ap.unsqueeze(axis).to_broadcast(shape)

            def normalize(dst, src, sq, k, trip=None):
                st, sh = stats, [P, k, P]
                link(dve.tensor_reduce(st[:, 0, 0:k], src, AX.X, ALU.add))
                link(dve.tensor_scalar(st[:, 0, 0:k], st[:, 0, 0:k], 1.0 / P, None, ALU.mult))
                link(dve.tensor_tensor(dst, src, bc(st[:, 0, 0:k], sh), ALU.subtract))
                link(dve.tensor_tensor(sq, dst, dst, ALU.mult))
                link(dve.tensor_reduce(st[:, 1, 0:k], sq, AX.X, ALU.add))
                nvar[0] += 1
                dve.tensor_scalar(st[:, 1, 0:k], st[:, 1, 0:k], 1.0 / P, EPS, ALU.mult, ALU.add).then_inc(var_ready, 1)
                dve.wait_ge(std_ready, nvar[0] if trip is None else trip + nvar[0])
                link(dve.reciprocal(st[:, 1, 0:k], st[:, 1, 0:k]))
                return lambda: dve.tensor_tensor(dst, dst, bc(st[:, 1, 0:k], sh), ALU.mult)

            def buckets(q):
                qs = slice(q * QL, (q + 1) * QL)
                with dve.Fori(0, T) as b:
                    link.enter(b, 3)
                    link(dve.tensor_scalar(mk, dh[:, qs], iota[:, bass.ds(b, 1)], None, ALU.is_equal))
                    link(dve.tensor_tensor_scan(sc, ones_b, mk, cur[:, bass.ds(b, 1)], ALU.mult, ALU.add))
                    dve.tensor_scalar(cur[:, bass.ds(b, 1)], sc[:, QL - 1:QL], 0.0, None, ALU.add).then_inc(cur_moved, 1)
                    link(dve.copy_predicated(pos[:, qs], mk.bitcast(U16), sc))
                    link.leave(T)
                dve.wait_ge(cur_moved, (q + 1) * T)
                dve.sem_inc(pos_ready, 1)

            dve.wait_ge(const, 7)
            link(dve.tensor_copy(iota[:, :], iota_i[:, :]))
            link(dve.tensor_copy(gid[:, :], gid_i[:, :]))
            link(dve.memset(ones_b, 1.0))
            dve.wait_ge(pairs_in, 16)
            link(dve.tensor_scalar(pos, pairs[:, :, 1], 7, None, ALU.logical_shift_right))
            link(dve.tensor_scalar(dh, pos, float(T), None, ALU.min))
            link(dve.tensor_scalar(pairs[:, :, 1], pairs[:, :, 1], P - 1, None, ALU.bitwise_and))
            link(dve.tensor_scalar(pairs[:, :, 0], pairs[:, :, 0], float(N - 1), 0.0, ALU.min, ALU.max))
            link(dve.memset(pos, 1 << 30))
            with dve.Fori(0, T) as b:
                dve.tensor_scalar(junk, dh, iota[:, bass.ds(b, 1)], 0.0, ALU.is_equal, ALU.add,
                                  accum_out=cnt[:, bass.ds(b, 1)]).then_inc(counts, 1)
                dve.wait_ge(counts, b + 1)
            dve.wait_ge(offs, 1)
            link(dve.tensor_scalar(ngi[:, :], ps[:, 1, 0:T], float(GE - 1), None, ALU.add))
            link(dve.tensor_scalar(ngi[:, :], ngi[:, :], GE.bit_length() - 1, None, ALU.logical_shift_right))
            link(dve.tensor_scalar(ngf[:, :], ngi[:, :], 1.0, None, ALU.max))
            link(dve.tensor_tensor_scan(gend[:, :], ones_b[:, 0:T], ngf[:, :], 0.0, ALU.mult, ALU.add))
            link(dve.tensor_tensor(cur[:, :], gend[:, :], ngf[:, :], ALU.subtract))
            link(dve.tensor_scalar(cur[:, :], cur[:, :], float(GE), -1.0, ALU.mult, ALU.add))
            link(dve.tensor_tensor(cur[:, :], cur[:, :], ps[:, 0, 0:T], ALU.add))
            link(dve.tensor_scalar(gcount[:, :], gend[:, T - 1:T], 1.0, None, ALU.add))
            link(dve.tensor_scalar(gcount[:, :], gcount[:, :], 1, None, ALU.logical_shift_right))
            K = NGP // P
            gc = junk.bitcast(F32)[:, 0:K * T].rearrange("p (k b) -> p k b", k=K)
            link(dve.tensor_tensor(gc, bc(gid[:, :], [P, K, T]), bc(gend[:, :], [P, K, T], 1), ALU.is_ge))
            link(dve.tensor_reduce(gbf[:, :], gc, AX.X, ALU.add))
            dve.tensor_scalar(gbi[:, :], gbf[:, :], float(T - 1), None, ALU.min).then_inc(gbi_ready, 1)
            buckets(0)

            dve.wait_ge(x_in, 16)
            dve.wait_ge(small_in, 16 * 18)
            dve.wait_ge(filled, 16 * 8)
            for q in range(NB):
                ts = slice(q * TB, (q + 1) * TB)
                sq = junk.bitcast(F32)[:, 0:EC // 2].rearrange("p (t f) -> p t f", t=TB)
                link(normalize(featp[:, ts, :], resid[:, ts, :], sq, TB)())
            dve.wait_ge(row_summed, 2 * T)
            link(dve.tensor_tensor(dinv[:, :], deg2[:, :, 0], deg2[:, :, 1], ALU.add))
            link(dve.tensor_scalar(dinv[:, :], dinv[:, :], 1.0, None, ALU.add))
            link(dve.tensor_scalar(dmask[:, :], dinv[:, :], 0.0, None, ALU.is_gt))
            nvar[0] += 1
            dve.tensor_scalar(dinv[:, :], dinv[:, :], 1e-30, None, ALU.max).then_inc(var_ready, 1)
            dve.wait_ge(std_ready, nvar[0])
            link(dve.reciprocal(dinv[:, :], dinv[:, :]))
            link(dve.tensor_tensor(dinv[:, :], dinv[:, :], dmask[:, :], ALU.mult))
            dve.tensor_tensor(featp, featp, bc(dinv[:, :], [P, T, P]), ALU.mult).then_inc(feats0, 1)
            link(dve.tensor_tensor(resid[:, :, :], resid[:, :, :], bc(bias0, [P, T, P], 1), ALU.add))

            for k in range(NB):
                if k + 1 < NQ:
                    buckets(k + 1)
                dve.wait_ge(lin_ready, k + 1)
                kb = (k % 2) * 4
                for t in range(TB):
                    g = k * TB + t
                    ins = dve.scalar_tensor_tensor(resid[:, g, :], ps[:, kb + t // 4, (t % 4) * P:(t % 4 + 1) * P],
                                                   dinv[:, g:g + 1], resid[:, g, :], ALU.mult, ALU.add)
                ins.then_inc(x1_ready, 1)

            dve.wait_ge(x1_ready, NB)
            dve.wait_ge(w1_in, 32)
            dve.wait_ge(b1_done, 1)
            link(dve.tensor_tensor(b1a[:, :], b1a[:, :], ps[:, 7, 0:E0 * C0], ALU.add))
            dve.tensor_tensor(w1av, w1av, bc(lngb[:, 0, :], [P, E0, H0]), ALU.mult).then_inc(wa_ready, 1)
            v0 = nvar[0]
            with dve.Fori(0, NBLK) as i:
                per = 2 * 6 + 1 + 3 + 4
                link.enter(i, per)
                bt = bass.ds(i * SB4, SB4)
                link(normalize(u4, resid[:, bt, :], sq4, SB4, i * 2)())
                normalize(n4, u4, sq4, SB4, i * 2)().then_inc(ln_ready, 1)
                dve.wait_ge(lg_ready, i + 1)
                link(dve.tensor_tensor(gst[:, :, :], ps[:, 2, 0:SB4 * E0].rearrange("p (t e) -> p t e", t=SB4),
                                       bc(brr, [P, SB4, E0], 1), ALU.add))
                dve.sem_inc(sorting, 1)
                for t in range(SB4):
                    ins = dve.max(top[:, t, :], gst[:, t, :])
                link(ins)
                dve.sem_inc(sorting, 1)
                for t in range(SB4):
                    ins = dve.max_index(topi[:, t, :], top[:, t, :], gst[:, t, :])
                link(ins)
                for s in range(2):
                    link(dve.tensor_scalar(tops[:, s, bt], top[:, :, s], 0.0, None, ALU.add))
                    link(dve.tensor_scalar(tops[:, 2 + s, bt], topi[:, :, s], 0.0, None, ALU.add))
                link.leave(NBLK)
            nvar[0] = v0 + 2 * NBLK

            def two_best(first):
                dve.tensor_tensor(wts[:, 0, :], tops[:, 1, :], tops[:, 0, :], ALU.subtract).then_inc(tops_done, 1)
                dve.wait_ge(exp_ready, first)
                link(dve.tensor_scalar(wts[:, 1, :], wts[:, 0, :], 1.0, None, ALU.add))
                link(dve.reciprocal(wts[:, 1, :], wts[:, 1, :]))
                link(dve.tensor_tensor(wts[:, 0, :], wts[:, 0, :], wts[:, 1, :], ALU.mult))

            two_best(1)
            i8 = bc(iota[:, 0:8], [P, T, 8], 1)
            g2 = hid[0].rearrange("p c n -> p (c n)")[:, 0:T * 8].rearrange("p (t e) -> p t e", t=T)
            link(dve.tensor_tensor(gates[:, :, :], i8, bc(tops[:, 2, :], [P, T, 8]), ALU.is_equal))
            link(dve.tensor_tensor(gates[:, :, :], gates[:, :, :], bc(wts[:, 1, :], [P, T, 8]), ALU.mult))
            link(dve.tensor_tensor(g2, i8, bc(tops[:, 3, :], [P, T, 8]), ALU.is_equal))
            link(dve.tensor_tensor(g2, g2, bc(wts[:, 0, :], [P, T, 8]), ALU.mult))
            dve.tensor_tensor(gates[:, :, :], gates[:, :, :], g2, ALU.add).then_inc(gates_ready, 1)
            dve.wait_ge(gates_ready, 1)

            def combine(E, base_y, base_b):
                with dve.Fori(0, NBLK) as i:
                    link.enter(i, 1)
                    bt = bass.ds(i * SB4, SB4)
                    dve.tensor_scalar(gst[:, :, :], gates[:, bt, :], 0.0, None, ALU.add).then_inc(gst_ready, 1)
                    dve.wait_ge(bt_ready, i + (base_b + 1))
                    link(dve.tensor_tensor(resid[:, bt, :], resid[:, bt, :],
                                           ps[:, 7, :].rearrange("p (t f) -> p t f", t=SB4), ALU.add))
                    for e in range(E):
                        dve.wait_ge(y_ready, i * E + (base_y + e + 3))
                        for t in range(SB4):
                            g = bass.ds(i * SB4 + t, 1)
                            ins = dve.scalar_tensor_tensor(resid[:, g, :], ps[:, 4 + e % 2, t * P:(t + 1) * P].unsqueeze(1),
                                                           gates[:, g, e], resid[:, g, :], ALU.mult, ALU.add)
                        ins.then_inc(y_added, 1)
                        dve.wait_ge(y_added, i * E + (base_y + e + 3))
                    link.leave(NBLK)

            dve.sem_inc(y_added, 2)
            combine(E0, 0, 0)

            dve.wait_ge(wext_done, 1)
            link(dve.tensor_copy(wext[:, P:P + 2], ps[:, 6, 0:2]))
            dve.sem_inc(wext_ready, 1)
            link(dve.memset(feath[:, :, P:P + 1], 1.0))
            v0 = nvar[0]
            with dve.Fori(0, NBLK) as i:
                link.enter(i, 6 + 2)
                bt = bass.ds(i * SB4, SB4)
                normalize(u4, resid[:, bt, :], sq4, SB4, i)().then_inc(ln_ready, 1)
                dve.wait_ge(hx_ready, i + 1)
                hv = ps[:, 2:4, :].rearrange("p b (t w) -> p (b t) w", t=2)
                link(dve.tensor_scalar(feath[:, bt, 0:P], hv[:, :, 0:P], 0.0, None, ALU.add))
                for s in range(2):
                    ins = dve.tensor_scalar(asd[:, s, bt], hv[:, :, P + s], 0.0, None, ALU.add)
                    if s == 0:
                        link(ins)
                ins.then_inc(hx_copied, 1)
                dve.wait_ge(hx_copied, i + 1)
                link.leave(NBLK)
            nvar[0] = v0 + NBLK
            dve.tensor_reduce(small[:, 0:1], asd[:, 0, :], AX.X, ALU.max).then_inc(mx_ready, 1)
            dve.wait_ge(mxt_ready, 1)
            dve.tensor_reduce(small[0:1, 1:2], ps[0:1, 2, 0:P], AX.X, ALU.max).then_inc(mxd_ready, 1)
            dve.wait_ge(mxb_ready, 1)
            link(dve.tensor_copy(small[:, 2:3], ps[:, 3, 0:1]))
            link(dve.tensor_scalar(fac[:, 0, :], asd[:, 0, :], small[:, 2:3], None, ALU.subtract))
            link(dve.tensor_scalar(fac[:, 1, :], fac[:, 0, :], 0.2, None, ALU.mult))
            link(dve.tensor_scalar(asd[:, 1, :], asd[:, 1, :], small[:, 2:3], None, ALU.add))
            link(dve.tensor_scalar(fac[:, 2, :], asd[:, 1, :], 0.0, None, ALU.min))
            link(dve.tensor_scalar(asd[:, 0, :], asd[:, 1, :], 0.0, None, ALU.max))
            link(dve.tensor_scalar(fac[:, 4, :], asd[:, 0, :], -1.0, None, ALU.mult))
            link(dve.scalar_tensor_tensor(fac[:, 3, :], asd[:, 1, :], 0.2, asd[:, 0, :], ALU.mult, ALU.subtract))
            dve.sem_inc(fac_in, 1)
            dve.wait_ge(fac_ready, 1)
            link(dve.tensor_scalar(fac[:, 4, :], fac[:, 4, :], 1e-8, None, ALU.mult))
            dve.wait_ge(qt_ready, 1)
            dve.tensor_copy(n4[:, 0, :], ps[:, 4, 0:P]).then_inc(qs_ready, 1)

            dve.sem_inc(e_ready, 2)
            TURN = 2 * NS6
            for k in range(NB):
                dve.wait_ge(q_in, 16 * (k + 1))

                def weigh(n, loaded, r, s, j):
                    dve.wait_ge(p_ready, n + 1)
                    dve.scalar_tensor_tensor(prod[s], qb[:, 1, :], fac[:, 1, j], prod[s],
                                             ALU.mult, ALU.max).then_inc(vpos, 1)
                    dve.wait_ge(vpos, n + 1)
                    dve.wait_ge(a6_in[r], loaded)
                    dve.scalar_tensor_tensor(at6[r], at6[r], 0.0, prod[s], ALU.is_gt, ALU.mult).then_inc(e_ready, 1)

                with dve.Fori(0, T // TURN) as i:
                    for m in range(TURN):
                        n = k * T + m
                        weigh(i * TURN + n, i * 32 + 16 * (n // NS6 + 1), n % NS6, n % 2, bass.ds(i * TURN + m, 1))
                for m in range(T // TURN * TURN, T):
                    n = k * T + m
                    weigh(n, 16 * (n // NS6 + 1), n % NS6, n % 2, slice(m, m + 1))
                dve.wait_ge(att_ready, k + 1)
                vb = prod[0].rearrange("p (t f) -> p t f", t=TB)
                nb_ = prod[1].rearrange("p (t f) -> p t f", t=TB)
                for b in range(6):
                    w = min(3, TB - 3 * b)
                    accv = ps[:, b, 0:w * 129].rearrange("p (t f) -> p t f", t=w)
                    ts = slice(3 * b, 3 * b + w)
                    link(dve.tensor_tensor(rden[:, ts].unsqueeze(2), accv[:, :, P:P + 1], fac[:, 4, k * TB + 3 * b:k * TB + 3 * b + w].unsqueeze(2), ALU.add))
                link(dve.reciprocal(rden[:, 0:TB], rden[:, 0:TB]))
                for b in range(6):
                    w = min(3, TB - 3 * b)
                    accv = ps[:, b, 0:w * 129].rearrange("p (t f) -> p t f", t=w)
                    ts = slice(3 * b, 3 * b + w)
                    link(dve.tensor_tensor(vb[:, ts, :], accv[:, :, 0:P], bc(rden[:, ts], [P, w, P]), ALU.mult))
                dve.tensor_scalar(nb_, vb, 0.0, None, ALU.min).then_inc(eneg, 1)
                rs = resid[:, k * TB:(k + 1) * TB, :]
                link(dve.tensor_scalar(vb, vb, 0.0, -1.0, ALU.max, ALU.add))
                link(dve.tensor_tensor(rs, rs, vb, ALU.add))
                dve.wait_ge(x3_ready, k + 1)
                dve.tensor_tensor(rs, rs, nb_, ALU.add).then_inc(block_done, 1)
                dve.wait_ge(block_done, k + 1)

            dve.wait_ge(scattered, 1)
            tmpw = ntab[:, 0:2, 0:HF].rearrange("p s (h e) -> p s h e", h=HEADS)
            wv = wgat[:, 0:HF].rearrange("p (h e) -> p h e", h=HEADS)
            for s in range(2):
                link(dve.tensor_tensor(tmpw[:, s], wv, attr[:, s], ALU.mult))
                link(dve.tensor_reduce(wgat[:, HF + s * HEADS:HF + (s + 1) * HEADS], tmpw[:, s], AX.X, ALU.add))
            dve.sem_inc(wgat_done, 1)
            v0 = nvar[0]
            with dve.Fori(0, NBLK) as i:
                link.enter(i, 6 + 1)
                bt = bass.ds(i * SB4, SB4)
                normalize(u4, resid[:, bt, :], sq4, SB4, i)().then_inc(ln3_ready, 1)
                dve.wait_ge(gat_ready, i + 1)
                link(dve.tensor_scalar(ntab[:, bt, :], ps[:, 2, 0:SB4 * 24].rearrange("p (t k) -> p t k", t=SB4), 0.0, None, ALU.add))
                dve.sem_inc(gat_copied, 1)
                link.leave(NBLK)
            nvar[0] = v0 + NBLK
            dve.sem_inc(ntab_ready, 1)
            dve.tensor_reduce(small[:, 0:HEADS], ntab[:, :, HF:TW].rearrange("p t h -> p h t"), AX.X, ALU.max).then_inc(emx, 1)
            dve.wait_ge(emxt, 1)
            link(dve.tensor_reduce(small[0:HEADS, 4:5], ps[0:HEADS, 2, 0:P], AX.X, ALU.max))
            dve.tensor_scalar(small[0:HEADS, 8:8 + HEADS], ident[0:HEADS, 0:HEADS], small[0:HEADS, 4:5], None, ALU.mult).then_inc(emxd, 1)
            dve.wait_ge(emxb, 1)
            link(dve.tensor_copy(small[:, 12:16], ps[:, 3, 0:HEADS]))
            link(dve.tensor_copy(dtab[:, :, 0:HEADS], ntab[:, :, TW:TW + HEADS]))
            link(dve.tensor_tensor(ee, ntab[:, :, TW:TW + HEADS], bc(small[:, 12:16], [P, T, HEADS], 1), ALU.add))
            link(dve.scalar_tensor_tensor(dtab[:, :, HEADS:2 * HEADS], ee, 0.2, ee, ALU.mult, ALU.max))
            link(dve.tensor_tensor(ee, ntab[:, :, HF:TW], ntab[:, :, TW:TW + HEADS], ALU.add))
            link(dve.scalar_tensor_tensor(ee, ee, 0.2, ee, ALU.mult, ALU.max))
            link(dve.tensor_tensor(ee, ee, dtab[:, :, HEADS:2 * HEADS], ALU.subtract))
            dve.sem_inc(self_in, 1)
            dve.wait_ge(self_exp, 1)
            link(dve.tensor_copy(acc[:, :, HF:TW], ee))
            for h in range(HEADS):
                link(dve.tensor_tensor(acc[:, :, h * EX:(h + 1) * EX], ntab[:, :, h * EX:(h + 1) * EX],
                                       ee[:, :, h:h + 1].to_broadcast([P, T, EX]), ALU.mult))
            dve.sem_inc(vals_ready, 2)
            dve.wait_ge(gb_in, 16)
            trips = dve.value_load(gcount[0:1, 0:1], min_val=1, max_val=(NG + 1) // 2)

            def onehot(r):
                dve.tensor_tensor(oh[:, r, :, :], bc(iota[:, :], [P, GRP, P], 1), bc(dlf[:, r, :], [P, GRP, P]),
                                  ALU.is_equal).then_inc(oh_ready, 1)

            dve.wait_ge(pt_in[0], 16)
            dve.wait_ge(sum_ready, 2)
            link(dve.tensor_copy(dlf[:, 0, :], pt[:, 0, :, 1]))
            onehot(0)
            with dve.Fori(0, trips) as i:
                for r in range(2):
                    k = i * 10 + 5 * r
                    dve.wait_ge(pt_in[1 - r], (i + (1 + r)) * 16)
                    dve.wait_ge(sum_ready, i * 2 + (r + 2))
                    dve.tensor_copy(dlf[:, 1 - r, :], pt[:, 1 - r, :, 1]).then_inc(grp_c, 1)
                    dve.wait_ge(grp_c, k + 1)
                    onehot(1 - r)
                    dve.wait_ge(gathered[r], (i + 1) * 16 * GRP)
                    dve.wait_ge(dst_ready, i * 2 + (r + 1))
                    pd = ps[:, 4 + r, 0:GRP * 8].rearrange("p (c k) -> p c k", k=8)
                    dve.tensor_tensor(zt, gt[:, r, :, HF:TW], pd[:, :, 0:HEADS], ALU.add).then_inc(grp_c, 1)
                    dve.wait_ge(grp_c, k + 2)
                    dve.scalar_tensor_tensor(zt, zt, 0.2, zt, ALU.mult, ALU.max).then_inc(grp_c, 1)
                    dve.wait_ge(grp_c, k + 3)
                    dve.tensor_tensor(zt, zt, pd[:, :, HEADS:2 * HEADS], ALU.subtract).then_inc(grp_c, 1)
                    dve.wait_ge(grp_c, k + 4)
                    dve.tensor_scalar(zt, zt, 0.0, None, ALU.min).then_inc(z_ready, 1)
                    dve.wait_ge(ez_ready, i * 2 + (r + 1))
                    dve.tensor_tensor(vals[:, r, :, 0:HF].rearrange("p c (h e) -> p c h e", h=HEADS),
                                      gt[:, r, :, 0:HF].rearrange("p c (h e) -> p c h e", h=HEADS),
                                      vals[:, r, :, HF:TW].unsqueeze(3).to_broadcast([P, GRP, HEADS, EX]),
                                      ALU.mult).then_inc(vals_ready, 1)
                    bk = dve.value_load(gb[0:1, bass.ds(i * 2 + r, 1)], min_val=0, max_val=T - 1)
                    dve.wait_ge(sum_ready, i * 2 + (r + 3))
                    dve.tensor_tensor(acc[:, bass.ds(bk, 1), :], acc[:, bass.ds(bk, 1), :],
                                      ps[:, 6 + r, 0:TW].unsqueeze(1), ALU.add).then_inc(grp_c, 1)
                    dve.wait_ge(grp_c, k + 5)

            link(dve.tensor_scalar(ee, acc[:, :, HF:TW], 1e-16, None, ALU.add))
            link(dve.reciprocal(ee, ee))
            for h in range(HEADS):
                link(dve.tensor_tensor(ag[:, :, h * EX:(h + 1) * EX], acc[:, :, h * EX:(h + 1) * EX],
                                       ee[:, :, h:h + 1].to_broadcast([P, T, EX]), ALU.mult))
            link(dve.tensor_tensor(ag, ag, bc(bgat, [P, T, HF], 1), ALU.add))
            link(dve.tensor_reduce(lst[:, 0, :], ag, AX.X, ALU.add))
            link(dve.tensor_scalar(lst[:, 0, :], lst[:, 0, :], 1.0 / HF, None, ALU.mult))
            link(dve.tensor_tensor(ag, ag, bc(lst[:, 0, :], [P, T, HF]), ALU.subtract))
            link(dve.tensor_tensor(ag2, ag, ag, ALU.mult))
            link(dve.tensor_reduce(lst[:, 1, :], ag2, AX.X, ALU.add))
            nvar[0] += 1
            dve.tensor_scalar(lst[:, 1, :], lst[:, 1, :], 1.0 / HF, EPS, ALU.mult, ALU.add).then_inc(var_ready, 1)
            dve.wait_ge(std_ready, nvar[0])
            link(dve.reciprocal(lst[:, 1, :], lst[:, 1, :]))
            link(dve.tensor_tensor(ag, ag, bc(lst[:, 1, :], [P, T, HF]), ALU.mult))
            link(dve.tensor_tensor(ag, ag, bc(gam, [P, T, HF], 1), ALU.mult))
            link(dve.tensor_tensor(ag, ag, bc(bet, [P, T, HF], 1), ALU.add))
            link(dve.memset(lg8, -3e38))
            link(dve.tensor_reduce(lg8[:, :, 0:EX], ag.rearrange("p t (h e) -> p t e h", h=HEADS), AX.X, ALU.add))
            link(dve.tensor_scalar(lg8[:, :, 0:EX], lg8[:, :, 0:EX], 1.0 / HEADS, None, ALU.mult))
            with dve.Fori(0, NBLK) as i:
                link.enter(i, 1 + 2 + 4)
                bt = bass.ds(i * SB4, SB4)
                link(dve.tensor_scalar(gst[:, :, :], lg8[:, bt, :], 0.0, None, ALU.add))
                dve.sem_inc(sorting, 1)
                for t in range(SB4):
                    ins = dve.max(top[:, t, :], gst[:, t, :])
                link(ins)
                dve.sem_inc(sorting, 1)
                for t in range(SB4):
                    ins = dve.max_index(topi[:, t, :], top[:, t, :], gst[:, t, :])
                link(ins)
                for s in range(2):
                    link(dve.tensor_scalar(tops[:, s, bt], top[:, :, s], 0.0, None, ALU.add))
                    link(dve.tensor_scalar(tops[:, 2 + s, bt], topi[:, :, s], 0.0, None, ALU.add))
                link.leave(NBLK)
            two_best(2)
            g3 = lg8
            link(dve.tensor_tensor(gates[:, :, :], i8, bc(tops[:, 2, :], [P, T, 8]), ALU.is_equal))
            link(dve.tensor_tensor(gates[:, :, :], gates[:, :, :], bc(wts[:, 1, :], [P, T, 8]), ALU.mult))
            link(dve.tensor_tensor(g3, i8, bc(tops[:, 3, :], [P, T, 8]), ALU.is_equal))
            link(dve.tensor_tensor(g3, g3, bc(wts[:, 0, :], [P, T, 8]), ALU.mult))
            dve.tensor_tensor(gates[:, :, :], gates[:, :, :], g3, ALU.add).then_inc(gates_ready, 1)
            dve.wait_ge(gates_ready, 2)
            combine(E1, NBLK * E0, NBLK)
            dve.sem_inc(out_ready, 1)

        @block.tensor
        def _(pe):
            pe.wait_ge(const, 7)
            pe.wait_ge(counts, T)
            pe.matmul(ps[:, 0, 0:T], lower[:, :], cnt[:, :], start=True, stop=True)
            pe.matmul(ps[:, 1, 0:T], ones[:, :], cnt[:, :], start=True, stop=True).then_inc(offs, 1)
            pe.wait_ge(gbi_ready, 1)

            def clear(bank, n=BANK):
                return pe.matmul(ps[:, bank, 0:n], zeros_b[:, 0:P], zeros_b[:, 0:n], start=True, stop=False,
                                 skip_group_check=True)

            def close(bank, n=BANK):
                return pe.matmul(ps[:, bank, 0:n], zeros_b[:, 0:P], zeros_b[:, 0:n], start=False, stop=True,
                                 skip_group_check=True)

            pe.wait_ge(feats0, 1)
            pe.sem_inc(tile_used, NS2)
            pe.wait_ge(small_in, 16 * 18)
            for k in range(NB):
                kb = (k % 2) * 4
                if k >= 2:
                    pe.wait_ge(x1_ready, k - 1)
                for b in range(4):
                    clear(kb + b)
                with pe.Fori(0, T // NS2) as i:
                    for r in range(NS2):
                        pe.wait_ge(at_in[r], i * 16 + (k * (T // NS2) * 16 + 16))
                        pe.wait_ge(staged_x, i * NS2 + (k * T + r + 1))
                        for b in range(4):
                            ins = pe.matmul(ps[:, kb + b, :], xs[:, r, :], at2[r][:, b * BANK:(b + 1) * BANK],
                                            start=False, stop=False, skip_group_check=True)
                        ins.then_inc(tile_used, 1)
                for t in range(TB):
                    pe.matmul(ps[:, kb + t // 4, (t % 4) * P:(t % 4 + 1) * P], featp[:, k * TB + t, :], ident[:, :],
                              start=False, stop=False, skip_group_check=True)
                for b in range(4):
                    ins = close(kb + b)
                ins.then_inc(agg_ready, 1)
                pe.wait_ge(agg_copied, 4 * (k + 1))
                for t in range(TB):
                    ins = pe.matmul(ps[:, kb + t // 4, (t % 4) * P:(t % 4 + 1) * P], agg[:, t * P:(t + 1) * P],
                                    w0t[:, :], start=True, stop=True)
                ins.then_inc(lin_ready, 1)

            pe.wait_ge(w1_in, 32)
            pe.wait_ge(x1_ready, NB)
            for e in range(E0):
                for h in range(C0):
                    ins = pe.matmul(ps[:, 7, e * C0 + h:e * C0 + h + 1], w1av[:, e, h * P:(h + 1) * P],
                                    lngb[:, 1, e:e + 1], start=True, stop=True)
            ins.then_inc(b1_done, 1)
            with pe.Fori(0, NBLK) as i:
                pe.wait_ge(ln_ready, i + 1)
                for t in range(SB4):
                    pe.transpose(ps[:, 0, t * P:(t + 1) * P], u4[:, t, :], ident[:, :])
                for t in range(SB4):
                    ins = pe.transpose(ps[:, 1, t * P:(t + 1) * P], n4[:, t, :], ident[:, :])
                ins.then_inc(tr_ready, 1)
                pe.wait_ge(tr_copied, i + 1)
                for t in range(SB4):
                    ins = pe.matmul(ps[:, 2, t * E0:(t + 1) * E0], uT[:, t * P:(t + 1) * P], wr[:, :], start=True, stop=True)
                ins.then_inc(lg_ready, 1)

            def experts(E, C, w1v, w2v, b2, base_y, base_b, base_h):
                with pe.Fori(0, NBLK) as i:
                    def hidden(e):
                        for h in range(C):
                            pe.wait_ge(hid_ready, i * (E * C) + (base_h + C * e + h + 1))
                            bank = h if C == 4 else h + 2 * (e % 2)
                            pe.matmul(ps[:, bank, :], w1v[:, e, h * P:(h + 1) * P], featT[:, bass.ds(i * BANK, BANK)],
                                      start=True, stop=True).then_inc(h_ready, 1)

                    hidden(0)
                    pe.wait_ge(gst_ready, i + (base_b + 1))
                    for t in range(SB4):
                        ins = pe.transpose(ps[0:8, 6, t * P:(t + 1) * P], gst[:, t, :], ident[:, :])
                    ins.then_inc(gt_ready, 1)
                    pe.wait_ge(gts_ready, i + (base_b + 1))
                    for t in range(SB4):
                        ins = pe.matmul(ps[:, 7, t * P:(t + 1) * P], gts[0:E, t * P:(t + 1) * P], b2[:, :], start=True, stop=True)
                    ins.then_inc(bt_ready, 1)
                    for e in range(E):
                        if e + 1 < E:
                            hidden(e + 1)
                        pe.wait_ge(hid_ready, i * (E * C) + (base_h + C * (e + 1) + 4))
                        pe.wait_ge(y_added, i * E + (base_y + e + 1))
                        for t in range(SB4):
                            for h in range(C):
                                ins = pe.matmul(ps[:, 4 + e % 2, t * P:(t + 1) * P], hid[e % 2][:, h, t * P:(t + 1) * P],
                                                w2v[:, e, h, :], start=(h == 0), stop=(h == C - 1))
                        ins.then_inc(y_ready, 1)

            pe.sem_inc(y_ready, 2)
            pe.wait_ge(wa_ready, 1)
            pe.wait_ge(gates_ready, 1)
            experts(E0, C0, w1av, w2av, b2a, 0, 0, 0)

            pe.wait_ge(small_in, 16 * 18)
            pe.matmul(ps[:, 6, 0:2], wg[:, :], att[:, :], start=True, stop=True).then_inc(wext_done, 1)
            pe.wait_ge(wext_ready, 1)
            with pe.Fori(0, NBLK) as i:
                pe.wait_ge(ln_ready, i + (NBLK + 1))
                for t in range(SB4):
                    ins = pe.transpose(ps[:, 0, t * P:(t + 1) * P], u4[:, t, :], ident[:, :])
                ins.then_inc(tr_ready, 1)
                pe.wait_ge(tr_copied, i + (NBLK + 1))
                for t in range(SB4):
                    ins = pe.matmul(ps[:, 2 + t // 2, (t % 2) * 256:(t % 2) * 256 + P + 2], uT[:, t * P:(t + 1) * P],
                                    wext[:, :], start=True, stop=True)
                ins.then_inc(hx_ready, 1)
            pe.wait_ge(hx_copied, NBLK)
            pe.wait_ge(mx_ready, 1)
            pe.transpose(ps[0:1, 2, 0:P], small[:, 0:1], ident[:, :]).then_inc(mxt_ready, 1)
            pe.wait_ge(mxd_ready, 1)
            pe.matmul(ps[:, 3, 0:1], ones[0:1, :], small[0:1, 1:2], start=True, stop=True).then_inc(mxb_ready, 1)
            pe.wait_ge(fac_ready, 1)
            pe.transpose(ps[:, 4, 0:P], fac[:, 2:4, :].rearrange("p k t -> p (k t)"), ident[:, :]).then_inc(qt_ready, 1)
            pe.wait_ge(qs_ready, 1)

            for k in range(NB):
                if k:
                    pe.wait_ge(eneg, k)
                for b in range(6):
                    clear(b, 129 * min(3, TB - 3 * b))

                def tile6(n, r, j):
                    pe.wait_ge(e_ready, n + 3)
                    for t in range(TB):
                        ins = pe.matmul(ps[:, t // 3, (t % 3) * 129:(t % 3 + 1) * 129], at6[r][:, t * P:(t + 1) * P],
                                        feath[:, j, 0:129], start=False, stop=False, skip_group_check=True)
                    ins.then_inc(e_used, 1)

                full = T // NS6
                with pe.Fori(0, full) as i:
                    for m in range(NS6):
                        tile6(i * NS6 + (k * T + m), (k * T + m) % NS6, bass.ds(i * NS6 + m, 1))
                for m in range(full * NS6, T):
                    tile6(k * T + m, (k * T + m) % NS6, slice(m, m + 1))
                for b in range(6):
                    ins = close(b, 129 * min(3, TB - 3 * b))
                ins.then_inc(att_ready, 1)

            pe.wait_ge(wgat_done, 1)
            with pe.Fori(0, NBLK) as i:
                pe.wait_ge(ln3_ready, i + 1)
                for t in range(SB4):
                    ins = pe.transpose(ps[:, 0, t * P:(t + 1) * P], u4[:, t, :], ident[:, :])
                ins.then_inc(tr3_ready, 1)
                pe.wait_ge(tr3_copied, i + 1)
                for t in range(SB4):
                    ins = pe.matmul(ps[:, 2, t * 24:(t + 1) * 24], uT[:, t * P:(t + 1) * P], wgat[:, :], start=True, stop=True)
                ins.then_inc(gat_ready, 1)
            pe.wait_ge(gat_copied, NBLK)
            pe.wait_ge(emx, 1)
            pe.transpose(ps[0:HEADS, 2, 0:P], small[:, 0:HEADS], ident[:, :]).then_inc(emxt, 1)
            pe.wait_ge(emxd, 1)
            pe.matmul(ps[:, 3, 0:HEADS], ones[0:HEADS, :], small[0:HEADS, 8:8 + HEADS], start=True, stop=True).then_inc(emxb, 1)
            pe.wait_ge(vals_ready, 2)
            pe.wait_ge(gb_in, 16)
            trips = pe.value_load(gcount[0:1, 0:1], min_val=1, max_val=(NG + 1) // 2)

            def dst_side(r, g, need):
                pe.wait_ge(oh_ready, need)
                for q in range(GRP):
                    ins = pe.transpose(ps[:, 2 + r, q * P:(q + 1) * P], oh[:, r, q, :], ident[:, :])
                ins.then_inc(ohp_ready, 1)
                bk = pe.value_load(gb[0:1, bass.ds(g, 1)], min_val=0, max_val=T - 1)
                pe.wait_ge(oht_ready, need)
                for q in range(GRP):
                    ins = pe.matmul(ps[:, 4 + r, q * 8:(q + 1) * 8], oht[:, r, q, :], dtab[:, bass.ds(bk, 1), :],
                                    start=True, stop=True)
                ins.then_inc(dst_ready, 1)

            pe.sem_inc(sum_ready, 2)
            dst_side(0, 0, 1)
            with pe.Fori(0, trips) as i:
                for r in range(2):
                    dst_side(1 - r, i * 2 + (r + 1), i * 2 + (r + 2))
                    pe.wait_ge(vals_ready, i * 2 + (r + 3))
                    for q in range(GRP):
                        ins = pe.matmul(ps[:, 6 + r, 0:TW], oh[:, r, q, :], vals[:, r, q, :], start=(q == 0), stop=(q == GRP - 1))
                    ins.then_inc(sum_ready, 1)

            pe.wait_ge(w1b_in, 32)
            pe.wait_ge(gates_ready, 2)
            experts(E1, C1, w1bv, w2bv, b2b, NBLK * E0, NBLK, NBLK * E0 * C0)

        @block.scalar
        def _(act):
            def root(ap, n, trip=None):
                act.wait_ge(var_ready, n if trip is None else trip + n)
                act.activation(ap, ap, ACT.Sqrt).then_inc(std_ready, 1)

            nv = 0
            with act.Fori(0, 2 * T // 6) as i:
                for k in range(6):
                    r = k % NS1
                    act.wait_ge(arow_in[r], i * 32 + (k // NS1 * 16 + 16))
                    act.activation(arow[r], arow[r], ACT.Copy,
                                   accum_out=deg2[:, bass.ds(i * 3 + k // 2, 1), k % 2]).then_inc(row_summed, 1)
            for n in range(6 * (2 * T // 6), 2 * T):
                r = n % NS1
                act.wait_ge(arow_in[r], 16 * (n // NS1 + 1))
                act.activation(arow[r], arow[r], ACT.Copy, accum_out=deg2[:, n // 2, n % 2:n % 2 + 1]).then_inc(row_summed, 1)
            for q in range(NB):
                nv += 1
                root(stats[:, 1, 0:TB], nv)
            nv += 1
            root(dinv[:, :], nv)

            act.wait_ge(feats0, 1)
            for k in range(NB):
                with act.Fori(0, T // NS2) as i:
                    for r in range(NS2):
                        act.wait_ge(tile_used, i * NS2 + (k * T + r + 1))
                        act.sem_inc(slot_taken, 1)
                        act.activation(xs[:, r, :].unsqueeze(1), featp[:, bass.ds(i * NS2 + r, 1), :], ACT.Copy).then_inc(staged_x, 1)
                act.wait_ge(agg_ready, k + 1)
                kb = (k % 2) * 4
                for b in range(4):
                    act.activation(agg[:, b * BANK:(b + 1) * BANK], ps[:, kb + b, :], ACT.Copy).then_inc(agg_copied, 1)

            with act.Fori(0, NBLK) as i:
                for s in range(2):
                    root(stats[:, 1, 0:SB4], nv + s + 1, i * 2)
                act.wait_ge(tr_ready, i + 1)
                act.activation(uT, ps[:, 0, :], ACT.Copy).then_inc(act_c, 1)
                act.activation(featT[:, bass.ds(i * BANK, BANK)], ps[:, 1, :], ACT.Copy).then_inc(act_c, 1)
                act.wait_ge(act_c, i * 2 + 2)
                act.sem_inc(tr_copied, 1)
            nv += 2 * NBLK
            act.wait_ge(tops_done, 1)
            act.activation(wts[:, 0, :], wts[:, 0, :], ACT.Exp).then_inc(exp_ready, 1)

            def gelus(E, C, b1, base_y, base_b, base_h):
                with act.Fori(0, NBLK) as i:
                    for e in range(E):
                        for h in range(C):
                            act.wait_ge(h_ready, i * (E * C) + (base_h + e * C + h + 1))
                            if h == 0:
                                act.wait_ge(y_ready, i * E + (base_y + e + 1))
                            bank = h if C == 4 else h + 2 * (e % 2)
                            act.activation(hid[e % 2][:, h, :], ps[:, bank, :], ACT.Gelu,
                                           bias=b1[:, e * C + h:e * C + h + 1]).then_inc(hid_ready, 1)
                        if e == 0:
                            act.wait_ge(gt_ready, i + (base_b + 1))
                            act.activation(gts[:, :], ps[0:8, 6, :], ACT.Copy).then_inc(gts_ready, 1)

            act.sem_inc(hid_ready, 4)
            act.wait_ge(wa_ready, 1)
            gelus(E0, C0, b1a, 0, 0, 0)

            with act.Fori(0, NBLK) as i:
                root(stats[:, 1, 0:SB4], nv + 1, i)
                act.wait_ge(tr_ready, i + (NBLK + 1))
                act.activation(uT, ps[:, 0, :], ACT.Copy).then_inc(tr_copied, 1)
            nv += NBLK
            act.wait_ge(fac_in, 1)
            act.activation(fac[:, :, :], fac[:, :, :], ACT.Exp).then_inc(fac_ready, 1)
            act.wait_ge(q_out, 16)
            qrows = q_d.rearrange("(k t) p -> k (t p)", k=2)
            for k in range(NB):
                if k:
                    act.wait_ge(block_done, k)
                act.dma_start(qb[:, :, :], qrows[:, k * IB:(k + 1) * IB].unsqueeze(0).to_broadcast([P, 2, IB])).then_inc(q_in, 16)
                act.wait_ge(q_in, 16 * (k + 1))
                with act.Fori(0, T // 2) as i:
                    for s in range(2):
                        act.wait_ge(e_ready, i * 2 + (k * T + s + 1))
                        act.sem_inc(slot_taken, 1)
                        act.activation(prod[s], qb[:, 0, :], ACT.Copy,
                                       scale=fac[:, 0, bass.ds(i * 2 + s, 1)]).then_inc(p_ready, 1)
                act.wait_ge(eneg, k + 1)
                act.activation(prod[1], prod[1], ACT.Exp).then_inc(x3_ready, 1)
            with act.Fori(0, NBLK) as i:
                root(stats[:, 1, 0:SB4], nv + 1, i)
                act.wait_ge(tr3_ready, i + 1)
                act.activation(uT, ps[:, 0, :], ACT.Copy).then_inc(act_c, 1)
                act.activation(featT[:, bass.ds(i * BANK, BANK)], ps[:, 0, :], ACT.Copy).then_inc(act_c, 1)
                act.wait_ge(act_c, i * 2 + (2 * NBLK + 2))
                act.sem_inc(tr3_copied, 1)
            nv += NBLK
            act.wait_ge(self_in, 1)
            act.activation(ee, ee, ACT.Exp).then_inc(self_exp, 1)
            act.wait_ge(gb_in, 16)
            trips = act.value_load(gcount[0:1, 0:1], min_val=1, max_val=(NG + 1) // 2)

            def turn(r, need):
                act.wait_ge(ohp_ready, need)
                act.activation(oht[:, r, :, :].rearrange("p c n -> p (c n)"), ps[:, 2 + r, :], ACT.Copy).then_inc(oht_ready, 1)

            turn(0, 1)
            with act.Fori(0, trips) as i:
                for r in range(2):
                    turn(1 - r, i * 2 + (r + 2))
                    act.wait_ge(z_ready, i * 2 + (r + 1))
                    act.wait_ge(sum_ready, i * 2 + (r + 1))
                    act.activation(vals[:, r, :, HF:TW], zt, ACT.Exp).then_inc(ez_ready, 1)
            nv += 1
            root(lst[:, 1, :], nv)
            act.wait_ge(tops_done, 2)
            act.activation(wts[:, 0, :], wts[:, 0, :], ACT.Exp).then_inc(exp_ready, 1)
            gelus(E1, C1, b1b, NBLK * E0, NBLK, NBLK * E0 * C0)


_ORDER = ["x", "adj", "adjT", "pairs", "W0T", "b0", "Wr", "br", "lngb", "W1a", "b1a", "W2a", "b2a",
          "Wg", "WgT", "attn", "W_gat", "att_src", "att_dst", "b_gat", "ln_gamma", "ln_beta",
          "W1b", "b1b", "W2b", "b2b"]


def kernel(x, adj, L0_gnn_W, L0_gnn_b, L0_ffn_Wr, L0_ffn_br, L0_ffn_ln_g, L0_ffn_ln_b, L0_ffn_W1, L0_ffn_b1,
           L0_ffn_W2, L0_ffn_b2, L1_gnn_W, L1_gnn_attn_src, L1_gnn_attn_dst, L1_ffn_W_gat, L1_ffn_att_src,
           L1_ffn_att_dst, L1_ffn_b_gat, L1_ffn_ln_gamma, L1_ffn_ln_beta, L1_ffn_W1, L1_ffn_b1, L1_ffn_W2,
           L1_ffn_b2, L1_ffn_edge_index):
    import numpy as np
    import concourse.bacc as bacc
    from concourse.bass_utils import run_bass_kernel_spmd

    A = np.ascontiguousarray
    n = x.shape[0]

    def cols(b):
        b = np.asarray(b)
        return A(b.reshape(b.shape[0], -1, 128).transpose(2, 0, 1).reshape(128, -1))

    def down(w):
        w = np.asarray(w)
        return A(w.reshape(w.shape[0], -1, 128, w.shape[2]).transpose(2, 0, 1, 3))

    adj = np.asarray(adj)
    arrays = {
        "x": A(x), "adj": A(adj), "adjT": A(adj.reshape(4, n // 4, n).transpose(0, 2, 1)),
        "pairs": A(np.asarray(L1_ffn_edge_index).T),
        "W0T": A(np.asarray(L0_gnn_W).T), "b0": A(L0_gnn_b), "Wr": A(L0_ffn_Wr), "br": A(L0_ffn_br),
        "lngb": A(np.stack([np.asarray(L0_ffn_ln_g).T, np.asarray(L0_ffn_ln_b).T], axis=1)),
        "W1a": A(np.asarray(L0_ffn_W1).transpose(1, 0, 2)), "b1a": cols(L0_ffn_b1), "W2a": down(L0_ffn_W2), "b2a": A(L0_ffn_b2),
        "Wg": A(L1_gnn_W), "WgT": A(np.asarray(L1_gnn_W).T),
        "attn": A(np.concatenate([np.asarray(L1_gnn_attn_src), np.asarray(L1_gnn_attn_dst)]).T),
        "W_gat": A(L1_ffn_W_gat), "att_src": A(np.asarray(L1_ffn_att_src).reshape(-1)),
        "att_dst": A(np.asarray(L1_ffn_att_dst).reshape(-1)), "b_gat": A(L1_ffn_b_gat),
        "ln_gamma": A(L1_ffn_ln_gamma), "ln_beta": A(L1_ffn_ln_beta),
        "W1b": A(np.asarray(L1_ffn_W1).transpose(1, 0, 2)), "b1b": cols(L1_ffn_b1), "W2b": down(L1_ffn_W2), "b2b": A(L1_ffn_b2),
    }
    nc = bacc.Bacc("TRN2", target_bir_lowering=False, num_devices=1)
    d = {k: nc.dram_tensor(f"in_{k}", arrays[k].shape, mybir.dt.from_np(arrays[k].dtype), kind="ExternalInput").ap()
         for k in _ORDER}
    out = nc.dram_tensor("out_0", (n, 128), F32, kind="ExternalOutput").ap()
    build(nc, d, out)
    r = run_bass_kernel_spmd(nc, [{f"in_{k}": arrays[k] for k in _ORDER}], core_ids=[0])
    return r.results[0]["out_0"]
```

```python
from contextlib import ExitStack

import concourse.bass as bass
from concourse import mybir

F32 = mybir.dt.float32
I32 = mybir.dt.int32
BF16 = mybir.dt.bfloat16
U16 = mybir.dt.uint16
ALU = mybir.AluOpType
ACT = mybir.ActivationFunctionType
AX = mybir.AxisListType

P = 128
BANK = 512
EPS = 1e-5


class Chain:

    def __init__(self, eng, sem):
        self.eng, self.sem, self.n, self.trip = eng, sem, 0, None

    def __call__(self, ins):
        self.n += 1
        ins.then_inc(self.sem, 1)
        self.eng.wait_ge(self.sem, self.n if self.trip is None else self.trip + self.n)

    def enter(self, i, per, first=0):
        self.trip, self.start, self.per = i * per, self.n, per
        self.n -= first * per

    def leave(self, trips, first=0):
        assert self.n + first * self.per - self.start == self.per, (self.n + first * self.per - self.start, self.per)
        self.trip, self.n = None, self.start + trips * self.per


def build(nc, d, out):
    N = d["x"].shape[0]
    T = N // P
    IB = 2048
    NB = N // IB
    TB = IB // P
    E0, H0 = d["W1a"].shape[1], d["W1a"].shape[2]
    E1, H1 = d["W1b"].shape[1], d["W1b"].shape[2]
    C0, C1 = H0 // P, H1 // P
    SB4 = 4
    NBLK = T // SB4
    HEADS = 4
    EX = E1
    HF = HEADS * EX
    TW = HF + HEADS

    NE = d["edge_index"].shape[1]
    EC = NE // P
    B, G = 8, 2
    WB = B + 1
    STEPS = EC // (B * G)
    W = 1056
    BLOCKS = -(-(EC + WB) // W)
    CW = W * BLOCKS
    CSTEPS = W // (B * G)
    CH = BANK
    GRP = 5
    GE = GRP * P
    GR = 4
    NG = NE // GE + T
    NGP = -(-(NG + 2) // P) * P
    GTRIPS = -(-NG // GR)
    assert GR * (GTRIPS + 1) <= NGP
    SC = 16

    sorted_d = nc.dram_tensor("sorted_edges", (NGP * GE, 1), I32, kind="Internal").ap()
    table_d = nc.dram_tensor("node_table", (N, TW), F32, kind="Internal").ap()
    gb_d = nc.dram_tensor("group_bucket", (NGP,), I32, kind="Internal").ap()
    q_d = nc.dram_tensor("score_factors", (P, P), F32, kind="Internal").ap()

    with ExitStack() as c:
        def sb(n, s, dt=F32):
            return c.enter_context(nc.sbuf_tensor(n, s, dt))

        def sem(n):
            return c.enter_context(nc.semaphore(n))

        ps = c.enter_context(nc.psum_tensor("ps", [P, 8, BANK], F32))

        resid = sb("resid", [P, T, P])
        feat = sb("feat", [P, T * 130])
        work = sb("work", [P, 18432])
        edge = sb("edge", [P, 3 * EC])
        ident = sb("ident", [P, P])
        lower = sb("lower", [P, P])
        ones = sb("ones", [P, P])
        iota_i = sb("iota_i", [P, P], I32)
        iota = sb("iota", [P, P])
        zeros_b = sb("zeros_b", [P, BANK], BF16)
        w0t = sb("w0t", [P, P])
        wr = sb("wr", [P, E0])
        rows = sb("rows", [P, P + E0 + 5 * HF])
        b2a = sb("b2a", [E0, P])
        b2b = sb("b2b", [E1, P])
        lngb = sb("lngb", [P, 2, E0])
        b1a = sb("b1a", [P, E0 * C0])
        b1b = sb("b1b", [P, E1 * C1])
        wg = sb("wg", [P, P])
        wext = sb("wext", [P, P + 2])
        att = sb("att", [P, 2])
        wgat = sb("wgat", [P, HF + 2 * HEADS])
        stats = sb("stats", [P, 2, T])
        deg2 = sb("deg2", [P, T, 2])
        dinv = sb("dinv", [P, T])
        dmask = sb("dmask", [P, T])
        gates = sb("gates", [P, T, 8])
        gst = sb("gst", [P, SB4, 8])
        tops = sb("tops", [P, 2, T])
        wts = sb("wts", [P, 2, T])
        gts = sb("gts", [8, BANK])
        small = sb("small", [P, 16])
        low_i = sb("low_i", [P, 1], I32)
        asd = sb("asd", [P, 2, T])
        fac = sb("fac", [P, 5, T])
        cnt = sb("cnt", [P, T])
        cnt1 = sb("cnt1", [P, T])
        nclamp = sb("nclamp", [P, T])
        ngi = sb("ngi", [P, T], I32)
        ngf = sb("ngf", [P, T])
        gend = sb("gend", [P, T])
        cur = sb("cur", [P, T])
        gid_i = sb("gid_i", [P, NGP // P], I32)
        gid = sb("gid", [P, NGP // P])
        gbf = sb("gbf", [P, NGP // P])
        gbi = sb("gbi", [P, NGP // P], I32)
        gcount = sb("gcount", [P, 1], I32)
        bcount = sb("bcount", [P, 1], I32)
        vcount = sb("vcount", [P, 1])
        stg_i = sb("stg_i", [P, 2, SC], I32)
        stg_p = sb("stg_p", [P, 2, SC], I32)
        woh = sb("woh", [P, 2, G, WB, B], BF16)
        rhs = sb("rhs", [P, 2, G, 4, WB, B], BF16)
        wins = sb("wins", [P, 2, G * 4 * WB], BF16)

        bias0 = rows[:, 0:P]
        brr = rows[:, P:P + E0]
        attr = rows[:, P + E0:P + E0 + 2 * HF].rearrange("p (s h e) -> p s h e", s=2, h=HEADS)
        bgat = rows[:, P + E0 + 2 * HF:P + E0 + 3 * HF]
        gam = rows[:, P + E0 + 3 * HF:P + E0 + 4 * HF]
        bet = rows[:, P + E0 + 4 * HF:P + E0 + 5 * HF]

        NS1 = 3
        HALF = N // 2
        arow = [work[:, r * HALF:(r + 1) * HALF] for r in range(NS1)]
        ew = NS1 * HALF
        es = resid[:, :, :].rearrange("p t f -> p (t f)")[:, 0:2 * EC].bitcast(I32).rearrange("p (two e) -> p two e", two=2)
        ci = resid[:, 0:CH // P, :].rearrange("p t f -> p (t f)").bitcast(I32)
        ci2 = resid[:, CH // P:2 * CH // P, :].rearrange("p t f -> p (t f)").bitcast(I32)
        pcs = feat[:, 0:2 * EC].bitcast(BF16).rearrange("p (k e) -> p k e", k=4)
        ca = edge[:, 0:2 * CW].bitcast(BF16).rearrange("p (k w) -> p k w", k=4)
        wbi = gates[:, :, :].rearrange("p t e -> p (t e)")[:, 0:EC // B].bitcast(I32)
        fillt = edge[:, 0:NGP * GE // P // 8].bitcast(I32)
        o = 2 * CW
        pos = edge[:, o:o + W].bitcast(I32)
        pay = edge[:, o + W:o + 2 * W].bitcast(I32)
        lnsq = work[:, 18432 - P:18432].unsqueeze(1)
        ohq = edge[:, o:o + G * P * B].bitcast(BF16).rearrange("p (s g q b) -> p s g q b", s=2, g=G, q=P)
        o += G * P * B
        rep = edge[:, o:o + P * B // 2].bitcast(BF16).rearrange("p (q b) -> p q b", q=P)
        o += P * B // 2
        incl = edge[:, o:o + CH]
        gcv = edge[:, o:o + NGP // P * T].rearrange("p (k b) -> p k b", b=T)
        o += CH
        base = edge[:, o:o + CH]
        o += CH
        lt_b = edge[:, o:o + P // 2].bitcast(BF16)
        o += P // 2
        on_b = edge[:, o:o + P // 2].bitcast(BF16)
        o += P // 2
        assert o <= 3 * EC
        valid = work[:, ew:ew + EC // 2].bitcast(BF16)
        tmp = work[:, ew + EC // 2:ew + EC // 2 + EC].bitcast(I32)
        qq = work[:, ew + EC // 2:ew + EC].bitcast(BF16)
        wl = work[:, ew + EC:ew + EC + EC // 2].bitcast(BF16)
        o = ew
        lin = work[:, o:o + W]
        sc = lin.bitcast(I32)
        o += W
        keyr, keyc, mk, ones_b = [work[:, o + n * W // 2:o + (n + 1) * W // 2].bitcast(BF16) for n in range(4)]
        o += 2 * W
        coh = work[:, o:o + G * T * B].bitcast(BF16).rearrange("p (s g q b) -> p s g q b", s=2, g=G, q=T)
        assert o + G * T * B <= 18432 - P
        NS2 = 4
        at2 = [work[:, r * IB:(r + 1) * IB] for r in range(NS2)]
        agg = work[:, NS2 * IB:(NS2 + 1) * IB]
        xs = work[:, (NS2 + 1) * IB:(NS2 + 1) * IB + NS2 * P].rearrange("p (r f) -> p r f", r=NS2)
        assert (NS2 + 1) * IB + NS2 * P <= ew
        featp = feat[:, 0:T * P].rearrange("p (t f) -> p t f", t=T)
        feath = feat[:, :].rearrange("p (t f) -> p t f", t=T)
        featT = feat[:, 0:N]
        w1 = work[:, 0:4096]
        w2 = work[:, 4096:8192]
        w1av = w1.rearrange("p (e h) -> p e h", e=E0)
        w2av = w2.rearrange("p (e c f) -> p e c f", e=E0, c=C0)
        w1bv = work[:, 12288:12288 + E1 * H1].rearrange("p (e h) -> p e h", e=E1)
        w2bv = work[:, 12288 + E1 * H1:12288 + 2 * E1 * H1].rearrange("p (e c f) -> p e c f", e=E1, c=C1)
        hid = [work[:, 8192 + r * 2048:8192 + (r + 1) * 2048].rearrange("p (c n) -> p c n", n=BANK) for r in range(2)]
        un = work[:, 8192:16384].rearrange("p (t f) -> p t f", t=T)
        sqn = work[:, 16384:16384 + TB * P].rearrange("p (t f) -> p t f", t=TB)
        uT = [work[:, r * BANK:(r + 1) * BANK] for r in range(2)]
        lgT = [edge[:, 3 * EC - (r + 1) * BANK:3 * EC - r * BANK] for r in range(2)]
        assert 2 * CW + 2 * W <= 3 * EC - 2 * BANK
        qst = work[:, 18432 - P:18432]
        lgt = work[:, 16384:16384 + 8 * T].rearrange("p (t e) -> p t e", t=T)
        topv = work[:, 16896:16896 + 8 * T].rearrange("p (t e) -> p t e", t=T)
        topx = work[:, 17408:17408 + 8 * T].bitcast(mybir.dt.uint32).rearrange("p (t e) -> p t e", t=T)
        NS6 = 5
        at6 = [work[:, r * IB:(r + 1) * IB] for r in range(NS6)]
        prod = [work[:, (NS6 + r) * IB:(NS6 + r + 1) * IB] for r in range(2)]
        qb = work[:, (NS6 + 2) * IB:(NS6 + 4) * IB].rearrange("p (k n) -> p k n", k=2)
        rden = stats[:, 0, :]
        quot = edge[:, 0:TB * P].rearrange("p (t f) -> p t f", t=TB)
        qneg = edge[:, TB * P:2 * TB * P].rearrange("p (t f) -> p t f", t=TB)
        oh = work[:, 0:2 * GRP * P].rearrange("p (r c n) -> p r c n", r=2, c=GRP)
        oht = work[:, 2 * GRP * P:4 * GRP * P].rearrange("p (r c n) -> p r c n", r=2, c=GRP)
        o = 4 * GRP * P
        gt = work[:, o:o + GR * GRP * TW].rearrange("p (r c k) -> p r c k", r=GR, c=GRP)
        o += GR * GRP * TW
        vals = work[:, o:o + 2 * GRP * TW].rearrange("p (r c k) -> p r c k", r=2, c=GRP)
        o += 2 * GRP * TW
        pt = work[:, o:o + GR * GRP].bitcast(I32).rearrange("p (r c) -> p r c", r=GR)
        o += GR * GRP
        srci = work[:, o:o + GR * GRP].bitcast(I32).rearrange("p (r c) -> p r c", r=GR)
        o += GR * GRP
        dli = work[:, o:o + GR * GRP].bitcast(I32).rearrange("p (r c) -> p r c", r=GR)
        o += GR * GRP
        dlf = work[:, o:o + GR * GRP].rearrange("p (r c) -> p r c", r=GR)
        o += GR * GRP
        zt = work[:, o:o + GRP * HEADS].rearrange("p (c k) -> p c k", c=GRP)
        o += GRP * HEADS
        last = work[:, o:o + TW]
        o += TW
        assert o <= 8192
        gb = work[0:1, 14336:14336 + NGP + 1].bitcast(I32)
        o = 0
        ntab = edge[:, o:o + T * 24].rearrange("p (t k) -> p t k", t=T)
        o += T * 24
        dtab = edge[:, o:o + T * 8].rearrange("p (t k) -> p t k", t=T)
        o += T * 8
        acc = edge[:, o:o + T * TW].rearrange("p (t k) -> p t k", t=T)
        o += T * TW
        ee = edge[:, o:o + 2 * T * HEADS].rearrange("p (s t k) -> p s t k", s=2, t=T)
        o += 2 * T * HEADS
        ag = edge[:, o:o + T * HF].rearrange("p (t k) -> p t k", t=T)
        o += T * HF
        ag2 = edge[:, o:o + T * HF].rearrange("p (t k) -> p t k", t=T)
        o += T * HF
        lg8 = edge[:, o:o + T * 8].rearrange("p (t k) -> p t k", t=T)
        o += T * 8
        lst = edge[:, o:o + 2 * T].rearrange("p (s t) -> p s t", s=2)
        o += 2 * T

        const = sem("const"); fill_made = sem("fill_made"); tables_ready = sem("tables_ready")
        edges_in = sem("edges_in"); valid_ready = sem("valid_ready"); off_ready = sem("off_ready"); off_used = sem("off_used")
        windows_ready = sem("windows_ready"); win_oh = sem("win_oh"); oh_made = sem("oh_made"); moved = sem("moved"); taken = sem("taken")
        compacted = sem("compacted"); coh_made = sem("coh_made"); clamped = sem("clamped"); nclamp_ready = sem("nclamp_ready")
        blk_c = sem("blk_c"); counted = sem("counted"); rank_c = sem("rank_c"); cnt_c = sem("cnt_c"); blk_scattered = sem("blk_scattered")
        last_in = sem("last_in"); unpacked = sem("unpacked")
        x_in = sem("x_in"); small_in = sem("small_in")
        arow_in = [sem(f"arow_in{r}") for r in range(NS1)]
        row_summed = sem("row_summed")
        dve_c = sem("dve_c"); act_c = sem("act_c")
        var_ready = sem("var_ready"); std_ready = sem("std_ready")
        counts = sem("counts"); offs = sem("offs"); cur_moved = sem("cur_moved"); pos_ready = sem("pos_ready")
        scat = [sem("scat0"), sem("scat1")]; staged = sem("staged"); slot_open = sem("slot_open"); slot_taken = sem("slot_taken"); sorting = sem("sorting")
        gbi_ready = sem("gbi_ready"); gb_out = sem("gb_out"); gb_in = sem("gb_in"); scattered = sem("scattered")
        feats0 = sem("feats0")
        at_in = [sem(f"at_in{r}") for r in range(NS2)]
        staged_x = sem("staged_x"); tile_used = sem("tile_used"); agg_ready = sem("agg_ready")
        agg_copied = sem("agg_copied"); lin_ready = sem("lin_ready"); x1_ready = sem("x1_ready")
        w1_in = sem("w1_in"); wa_ready = sem("wa_ready"); b1_ready = sem("b1_ready"); b1_done = sem("b1_done")
        ln_ready = sem("ln_ready"); sub_ready = sem("sub_ready"); sq_ready = sem("sq_ready"); sq_used = sem("sq_used"); lgt_used = sem("lgt_used")
        tr_ready = sem("tr_ready"); tr_copied = sem("tr_copied")
        lg_ready = sem("lg_ready"); tops_done = sem("tops_done"); exp_ready = sem("exp_ready"); gates_ready = sem("gates_ready")
        gst_ready = sem("gst_ready"); gt_ready = sem("gt_ready"); gts_ready = sem("gts_ready"); bt_ready = sem("bt_ready")
        h_ready = sem("h_ready"); hid_ready = sem("hid_ready"); y_ready = sem("y_ready"); y_added = sem("y_added")
        hx_ready = sem("hx_ready"); hx_copied = sem("hx_copied"); wext_ready = sem("wext_ready"); wext_done = sem("wext_done")
        mx_ready = sem("mx_ready"); mxt_ready = sem("mxt_ready"); mxd_ready = sem("mxd_ready"); mxb_ready = sem("mxb_ready")
        fac_in = sem("fac_in"); fac_ready = sem("fac_ready"); qt_ready = sem("qt_ready"); qs_ready = sem("qs_ready"); q_out = sem("q_out"); q_in = sem("q_in")
        a6_in = [sem(f"a6_in{r}") for r in range(NS6)]
        p_ready = sem("p_ready"); e_ready = sem("e_ready"); e_used = sem("e_used"); att_ready = sem("att_ready")
        vpos = sem("vpos"); eneg = sem("eneg"); neg_ready = sem("neg_ready"); elu_c = sem("elu_c"); mean_ready = sem("mean_ready"); x_centred = sem("x_centred"); squared = sem("squared"); offs_taken = sem("offs_taken"); x3_ready = sem("x3_ready")
        block_done = sem("block_done"); gat_ready = sem("gat_ready"); gat_copied = sem("gat_copied")
        wgat_done = sem("wgat_done"); ntab_ready = sem("ntab_ready"); tab_out = sem("tab_out")
        emx = sem("emx"); emxt = sem("emxt"); emxd = sem("emxd"); emxb = sem("emxb")
        self_in = sem("self_in"); self_exp = sem("self_exp")
        pt_in = [sem(f"pt_in{r}") for r in range(GR)]; gathered = [sem(f"gathered{r}") for r in range(GR)]
        oh_ready = sem("oh_ready"); ohp_ready = sem("ohp_ready"); oht_ready = sem("oht_ready"); dst_ready = sem("dst_ready")
        z_ready = sem("z_ready"); ez_ready = sem("ez_ready"); vals_ready = sem("vals_ready"); sum_ready = sem("sum_ready")
        grp_c = sem("grp_c")
        w1b_in = sem("w1b_in")
        out_ready = sem("out_ready"); out_done = sem("out_done")

        NW = 15
        ring = 4

        block = c.enter_context(nc.Block())

        @block.sync
        def _(sp):
            sp.dma_start(es, d["edge_index"].rearrange("two (p e) -> p two e", p=P)).then_inc(edges_in, 16)

            def row(ap):
                return ap.rearrange("(a n) -> a n", a=1).to_broadcast([P, ap.shape[0]])

            loads = [(w0t[:, :], d["W0T"]), (wr[:, :], d["Wr"]), (bias0, row(d["b0"])), (brr, row(d["br"])),
                     (attr[:, 0].rearrange("p h e -> p (h e)"), row(d["att_src"])),
                     (attr[:, 1].rearrange("p h e -> p (h e)"), row(d["att_dst"])),
                     (bgat, row(d["b_gat"])), (gam, row(d["ln_gamma"])), (bet, row(d["ln_beta"])),
                     (b2a[:, :], d["b2a"]), (b2b[:, :], d["b2b"]),
                     (lngb[:, :, :], d["lngb"]), (b1a[:, :], d["b1a"]), (b1b[:, :], d["b1b"]),
                     (wg[:, :], d["Wg"]), (wext[:, 0:P], d["WgT"]), (att[:, :], d["attn"]),
                     (wgat[:, 0:HF], d["W_gat"])]
            for dst, src in loads:
                sp.dma_start(dst, src).then_inc(small_in, 16)

            halves = d["adj"].rearrange("(t p) (h n) -> t h p n", p=P, h=2)

            def load_half(n, r):
                sp.dma_start(arow[r], halves[n // 2, n % 2]).then_inc(arow_in[r], 16)

            for n in range(NS1):
                load_half(n, n)
            def turns(first, end):
                with sp.Fori(first, end) as i:
                    for n in range(6):
                        sp.wait_ge(row_summed, 6 * i + (n + 1))
                        m = n + NS1
                        sp.dma_start(arow[n % NS1], halves[3 * i + m // 2, m % 2]).then_inc(arow_in[n % NS1], 16)

            full = (2 * T - NS1) // 6
            turns(0, 4)
            sp.wait_ge(windows_ready, 1)
            sp.dma_start(resid[:, :, :], d["x"].rearrange("(t p) f -> p t f", p=P)).then_inc(x_in, 16)
            turns(4, full)
            for n in range(6 * full + NS1, 2 * T):
                sp.wait_ge(row_summed, n - NS1 + 1)
                load_half(n, n % NS1)

            tiles = d["adjT"].rearrange("k (j p) n -> (k j) p n", p=P)
            sp.wait_ge(row_summed, 2 * T)
            for r in range(NS2):
                sp.dma_start(at2[r], tiles[r]).then_inc(at_in[r], 16)
            with sp.Fori(0, NB * T // NS2 - 1) as i:
                for r in range(NS2):
                    sp.wait_ge(tile_used, i * NS2 + (NS2 + r + 1))
                    sp.dma_start(at2[r], tiles[i * NS2 + (NS2 + r)]).then_inc(at_in[r], 16)

            sp.wait_ge(x1_ready, NB)
            sp.dma_start(w1av, d["W1a"]).then_inc(w1_in, 16)
            sp.dma_start(w2av, d["W2a"]).then_inc(w1_in, 16)

            sp.wait_ge(qs_ready, 1)
            sp.dma_start(q_d, qst).then_inc(q_out, 16)
            for r in range(NS6):
                sp.dma_start(at6[r], tiles[r]).then_inc(a6_in[r], 16)
            total = NB * T
            full = (total - NS6) // NS6
            with sp.Fori(0, full) as i:
                for r in range(NS6):
                    sp.wait_ge(e_used, i * NS6 + (r + 1))
                    sp.dma_start(at6[r], tiles[i * NS6 + (NS6 + r)]).then_inc(a6_in[r], 16)
            for n in range(full * NS6, total - NS6):
                sp.wait_ge(e_used, n + 1)
                sp.dma_start(at6[n % NS6], tiles[n + NS6]).then_inc(a6_in[n % NS6], 16)

            sp.wait_ge(ntab_ready, 1)
            sp.dma_start(table_d.rearrange("(t p) k -> p t k", p=P), ntab[:, :, 0:TW]).then_inc(tab_out, 16)
            sp.wait_ge(tab_out, 16)
            sp.dma_start(last, table_d[N - 1:N, :].to_broadcast([P, TW])).then_inc(last_in, 16)
            sp.wait_ge(gb_out, 16)
            sp.dma_start(gb[0:1, 1:NGP + 1], gb_d.rearrange("(a g) -> a g", a=1)).then_inc(gb_in, 16)
            sp.dma_start(w1bv, d["W1b"]).then_inc(w1b_in, 16)
            sp.dma_start(w2bv, d["W2b"]).then_inc(w1b_in, 16)
            sp.wait_ge(scattered, 1)
            trips = sp.value_load(gcount[0:1, 0:1], min_val=1, max_val=GTRIPS)
            groups = sorted_d.rearrange("(g p r) o -> g p (r o)", p=P, r=GRP)
            for r in range(GR):
                sp.dma_start(pt[:, r, :], groups[r]).then_inc(pt_in[r], 16)
            with sp.Fori(0, trips) as i:
                for r in range(GR):
                    sp.wait_ge(unpacked, i * GR + (r + 1))
                    sp.dma_start(pt[:, r, :], groups[i * GR + (GR + r)]).then_inc(pt_in[r], 16)

            sp.wait_ge(out_ready, 1)
            sp.dma_start(out.rearrange("(t p) f -> p t f", p=P), resid[:, :, :]).then_inc(out_done, 16)
            sp.wait_ge(out_done, 16)

        @block.gpsimd
        def _(pool):
            pool.iota(iota_i[:, :], pattern=[[1, P]], base=0, channel_multiplier=0).then_inc(const, 1)
            pool.iota(gid_i[:, :], pattern=[[P, NGP // P]], base=0, channel_multiplier=1).then_inc(const, 1)
            pool.memset(ones[:, :], 1.0).then_inc(const, 1)
            pool.memset(ident[:, :], 0.0).then_inc(const, 1)
            pool.memset(zeros_b[:, :], 0.0).then_inc(const, 1)
            pool.memset(fillt, 255).then_inc(fill_made, 1)
            pool.wait_ge(const, 5)
            pool.affine_select(out=ident[:, :], in_=ident[:, :], compare_op=ALU.not_equal, fill=1.0, base=0,
                               pattern=[[-1, P]], channel_multiplier=1).then_inc(const, 1)
            pool.affine_select(out=lower[:, :], in_=ones[:, :], compare_op=ALU.is_gt, fill=0.0, base=0,
                               pattern=[[1, P]], channel_multiplier=-1).then_inc(const, 1)
            pool.wait_ge(fill_made, 1)
            fill_v = sorted_d.rearrange("(k p r) o -> k p (r o)", k=8, p=P)
            for k in range(8):
                pool.dma_start(fill_v[k], fillt).then_inc(scat[k % 2], 16)
            FILL = 16 * 4
            slot_bound = pool.to_reg(NG * GE - 1)
            node_bound = pool.to_reg(N - 1)
            for r in range(2):
                pool.wait_ge(scat[r], FILL)
            pool.memset(ca, 0.0).then_inc(compacted, 4)
            pool.wait_ge(compacted, 4)
            pool.wait_ge(windows_ready, 1)
            with pool.Fori(0, STEPS // 2) as i:
                for r in range(2):
                    ws = [pool.value_load(wbi[0:1, bass.ds(i * (2 * G) + (r * G + g), 1)], min_val=0, max_val=CW - WB) for g in range(G)]
                    pool.wait_ge(taken, i * 2 + (r + 3))
                    pool.sem_inc(slot_open, 1)
                    for g in range(G):
                        dst = ca[:, :, bass.ds(ws[g], WB)]
                        pool.tensor_tensor(dst, dst, wins[:, r, g * 4 * WB:(g + 1) * 4 * WB].rearrange("p (k w) -> p k w", k=4),
                                           ALU.add).then_inc(compacted, 1)
                        pool.wait_ge(compacted, i * 4 + (2 * r + g + 5))

            pool.wait_ge(mean_ready, 1)
            pool.tensor_tensor(featp, resid[:, :, :], stats[:, 0, :].unsqueeze(2).to_broadcast([P, T, P]), ALU.subtract).then_inc(x_centred, 1)

            pool.wait_ge(gbi_ready, 1)
            with nc.allow_non_contiguous_dma(reason="one word per group of edges"):
                pool.dma_start(gb_d.rearrange("(k p) -> p k", p=P), gbi[:, :]).then_inc(gb_out, 16)
            pool.wait_ge(gb_out, 16)

            per = W // (2 * SC)
            pool.wait_ge(pos_ready, 1)
            nb = pool.value_load(bcount[0:1, 0:1], min_val=1, max_val=BLOCKS)
            with pool.Fori(0, nb) as i:
                pool.wait_ge(pos_ready, i + 1)
                pool.sem_inc(slot_open, 1)
                with pool.Fori(0, per) as n:
                    for r in range(2):
                        pool.wait_ge(scat[r], (i * per + n) * (16 * SC) + FILL)
                        pool.tensor_copy(stg_i[:, r, :], pos[:, bass.ds(n * (2 * SC) + r * SC, SC)]).then_inc(staged, 1)
                        pool.tensor_copy(stg_p[:, r, :], pay[:, bass.ds(n * (2 * SC) + r * SC, SC)]).then_inc(staged, 1)
                        pool.wait_ge(staged, (i * per + n) * 4 + (2 * r + 2))
                        pool.sem_inc(slot_open, 1)
                        for k in range(SC):
                            pool.indirect_dma_start(sorted_d, bass.IndirectOffsetOnAxis(ap=stg_i[:, r, k:k + 1], axis=0),
                                                    stg_p[:, r, k:k + 1], None, bounds_check=slot_bound,
                                                    oob_is_err=False).then_inc(scat[r], 16)
                for r in range(2):
                    pool.wait_ge(scat[r], (i + 1) * (per * 16 * SC) + FILL)
                pool.sem_inc(blk_scattered, 1)
            pool.sem_inc(scattered, 1)
            for k in range(NB - 1):
                pool.wait_ge(eneg, k + 1)
                pool.tensor_scalar(qneg, quot, 0.0, None, ALU.min).then_inc(neg_ready, 1)
                pool.wait_ge(neg_ready, k + 1)
                pool.tensor_scalar(quot, quot, 0.0, -1.0, ALU.max, ALU.add).then_inc(elu_c, 1)
                pool.wait_ge(elu_c, 2 * k + 1)
                rs = resid[:, k * TB:(k + 1) * TB, :]
                pool.tensor_tensor(rs, rs, quot, ALU.add).then_inc(elu_c, 1)
                pool.wait_ge(elu_c, 2 * k + 2)
                pool.wait_ge(x3_ready, k + 1)
                pool.tensor_tensor(rs, rs, qneg, ALU.add).then_inc(block_done, 1)

            pool.wait_ge(tab_out, 16)
            trips = pool.value_load(gcount[0:1, 0:1], min_val=1, max_val=GTRIPS)
            with pool.Fori(0, trips) as i:
                for r in range(GR):
                    pool.wait_ge(unpacked, i * GR + (r + 1))
                    pool.wait_ge(vals_ready, i * GR + (r + 1))
                    pool.sem_inc(slot_open, 1)
                    for k in range(GRP):
                        pool.indirect_dma_start(gt[:, r, k, :], None, table_d,
                                                bass.IndirectOffsetOnAxis(ap=srci[:, r, k:k + 1], axis=0),
                                                bounds_check=node_bound, oob_is_err=False).then_inc(gathered[r], 16)

        @block.vector
        def _(dve):
            link = Chain(dve, dve_c)
            nvar = [0]

            def bc(ap, shape, axis=2):
                return ap.unsqueeze(axis).to_broadcast(shape)

            def layer_norms(g, twice=False):
                def first(c):
                    ts = slice(c * TB, (c + 1) * TB)
                    link(dve.tensor_reduce(stats[:, 0, ts], resid[:, ts, :], AX.X, ALU.add))
                    link(dve.tensor_scalar(stats[:, 0, ts], stats[:, 0, ts], 1.0 / P, None, ALU.mult))
                    dve.tensor_tensor(un[:, ts, :], resid[:, ts, :], bc(stats[:, 0, ts], [P, TB, P]), ALU.subtract).then_inc(sub_ready, 1)

                def second(c):
                    ts = slice(c * TB, (c + 1) * TB)
                    var = stats[:, 1, ts]
                    dve.wait_ge(sq_ready, g * NB + c + 1)
                    link(dve.tensor_reduce(var, sqn, AX.X, ALU.add))
                    dve.sem_inc(sq_used, 1)
                    link(dve.tensor_scalar(var, var, 1.0 / P, None, ALU.mult))
                    if twice:
                        link(dve.tensor_copy(stats[:, 0, ts], var))
                    nvar[0] += 1
                    dve.tensor_scalar(var, var, EPS, None, ALU.add).then_inc(var_ready, 1)
                    dve.wait_ge(std_ready, nvar[0])
                    link(dve.reciprocal(var, var))
                    if twice:
                        link(dve.tensor_tensor(stats[:, 0, ts], stats[:, 0, ts], var, ALU.mult))
                        link(dve.tensor_tensor(stats[:, 0, ts], stats[:, 0, ts], var, ALU.mult))
                        nvar[0] += 1
                        dve.tensor_scalar(stats[:, 0, ts], stats[:, 0, ts], EPS, None, ALU.add).then_inc(var_ready, 1)
                        dve.wait_ge(std_ready, nvar[0])
                        link(dve.reciprocal(small[:, 0:TB], stats[:, 0, ts]))
                        link(dve.tensor_tensor(var, var, small[:, 0:TB], ALU.mult))
                    dve.tensor_tensor(un[:, ts, :], un[:, ts, :], bc(var, [P, TB, P]), ALU.mult).then_inc(ln_ready, SB4)

                first(0)
                for c in range(NB):
                    if c + 1 < NB:
                        first(c + 1)
                    second(c)

            def best(logits, first):
                for t in range(T):
                    ins = dve.max(topv[:, t, :], logits[:, t, :])
                link(ins)
                for t in range(T):
                    ins = dve.max_index(topx[:, t, :], topv[:, t, :], logits[:, t, :])
                link(ins)
                for s in range(2):
                    link(dve.tensor_copy(tops[:, s, :], topx[:, :, s]))
                dve.tensor_tensor(wts[:, 0, :], topv[:, :, 1], topv[:, :, 0], ALU.subtract).then_inc(tops_done, 1)
                dve.wait_ge(exp_ready, first)
                link(dve.tensor_scalar(wts[:, 1, :], wts[:, 0, :], 1.0, None, ALU.add))
                link(dve.reciprocal(wts[:, 1, :], wts[:, 1, :]))
                link(dve.tensor_tensor(wts[:, 0, :], wts[:, 0, :], wts[:, 1, :], ALU.mult))
                i8 = bc(iota[:, 0:8], [P, T, 8], 1)
                link(dve.tensor_tensor(gates[:, :, :], i8, bc(tops[:, 0, :], [P, T, 8]), ALU.is_equal))
                link(dve.tensor_tensor(gates[:, :, :], gates[:, :, :], bc(wts[:, 1, :], [P, T, 8]), ALU.mult))
                link(dve.tensor_tensor(logits, i8, bc(tops[:, 1, :], [P, T, 8]), ALU.is_equal))
                link(dve.tensor_tensor(logits, logits, bc(wts[:, 0, :], [P, T, 8]), ALU.mult))
                dve.tensor_tensor(gates[:, :, :], gates[:, :, :], logits, ALU.add).then_inc(gates_ready, 1)
                dve.wait_ge(gates_ready, first)

            dve.wait_ge(const, 7)
            link(dve.tensor_copy(iota[:, :], iota_i[:, :]))
            link(dve.tensor_copy(gid[:, :], gid_i[:, :]))
            link(dve.tensor_copy(rep, bc(iota_i[:, :], [P, P, B])))
            link(dve.tensor_copy(lt_b, lower[:, :]))
            link(dve.tensor_copy(on_b, ones[:, :]))
            link(dve.memset(cnt[:, :], 0.0))
            dve.sem_inc(tables_ready, 1)
            dve.wait_ge(edges_in, 16)
            link(dve.tensor_scalar(tmp, es[:, 1, :], 7, None, ALU.logical_shift_right))
            link(dve.tensor_scalar(valid, tmp, float(T), None, ALU.is_lt))
            dve.sem_inc(valid_ready, 1)
            link(dve.scalar_tensor_tensor(pcs[:, 0, :], tmp, 1.0, valid, ALU.add, ALU.mult))
            link(dve.tensor_scalar(tmp, es[:, 1, :], P - 1, None, ALU.bitwise_and))
            link(dve.tensor_tensor(pcs[:, 1, :], tmp, valid, ALU.mult))
            link(dve.tensor_scalar(es[:, 0, :], es[:, 0, :], float(N - 1), 0.0, ALU.min, ALU.max))
            link(dve.tensor_scalar(tmp, es[:, 0, :], 7, None, ALU.logical_shift_right))
            link(dve.tensor_tensor(pcs[:, 2, :], tmp, valid, ALU.mult))
            link(dve.tensor_scalar(tmp, es[:, 0, :], P - 1, None, ALU.bitwise_and))
            link(dve.tensor_tensor(pcs[:, 3, :], tmp, valid, ALU.mult))
            for k in range(EC // CH):
                ks = slice(k * CH, (k + 1) * CH)
                kw = slice(k * CH // B, (k + 1) * CH // B)
                before, total = ps[:, k % 2, :], ps[:, 2 + k % 2, :]
                dve.wait_ge(off_ready, k + 1)
                link(dve.tensor_tensor_scan(incl, zeros_b[:, 0:CH], total, 0.0 if k == 0 else vcount[:, 0:1], ALU.add, ALU.add))
                link(dve.tensor_copy(vcount[:, :], incl[:, CH - 1:CH]))
                link(dve.tensor_tensor(base, incl, total, ALU.subtract))
                link(dve.tensor_tensor(ci[:, :], base, before, ALU.add))
                dve.sem_inc(off_used, 1)
                link(dve.tensor_copy(wbi[:, kw], base.rearrange("p (n b) -> p n b", b=B)[:, :, 0]))
                link(dve.tensor_scalar(wbi[:, kw], wbi[:, kw], 7, None, ALU.logical_shift_right))
                link(dve.tensor_scalar(ci2[:, :], ci[:, :], 7, None, ALU.logical_shift_right))
                link(dve.tensor_tensor(wl[:, ks].rearrange("p (n b) -> p n b", b=B), ci2[:, :].rearrange("p (n b) -> p n b", b=B),
                                       bc(wbi[:, kw], [P, CH // B, B]), ALU.subtract))
                link(dve.tensor_scalar(ci[:, :], ci[:, :], P - 1, None, ALU.bitwise_and))
                link(dve.tensor_copy(qq[:, ks], ci[:, :]))
            link(dve.tensor_scalar(small[:, 0:1], vcount[:, :], float(W * P), 1.0, ALU.is_gt, ALU.add))
            for k in range(2, BLOCKS):
                link(dve.scalar_tensor_tensor(small[:, k - 1:k], vcount[:, :], float(k * W * P), small[:, k - 2:k - 1], ALU.is_gt, ALU.add))
            link(dve.tensor_copy(bcount[:, :], small[:, BLOCKS - 2:BLOCKS - 1]))
            dve.sem_inc(windows_ready, 1)

            def onehots(n, slot):
                cols = bass.ds(n * (G * B), G * B) if not isinstance(n, int) else slice(n * G * B, (n + 1) * G * B)
                qv = qq[:, cols].rearrange("p (g b) -> p g b", g=G).unsqueeze(2).to_broadcast([P, G, P, B])
                wv = wl[:, cols].rearrange("p (g b) -> p g b", g=G).unsqueeze(2).to_broadcast([P, G, WB, B])
                dve.tensor_tensor(ohq[:, slot], rep.unsqueeze(1).to_broadcast([P, G, P, B]), qv, ALU.is_equal)
                dve.tensor_tensor(woh[:, slot], rep[:, 0:WB, :].unsqueeze(1).to_broadcast([P, G, WB, B]), wv, ALU.is_equal).then_inc(win_oh, 1)
                dve.wait_ge(win_oh, n + 1)
                for g in range(G):
                    cg = bass.ds(n * (G * B) + g * B, B) if not isinstance(n, int) else slice(n * G * B + g * B, n * G * B + g * B + B)
                    ins = dve.tensor_tensor(rhs[:, slot, g], woh[:, slot, g].unsqueeze(1).to_broadcast([P, 4, WB, B]),
                                            pcs[:, :, cg].unsqueeze(2).to_broadcast([P, 4, WB, B]), ALU.mult)
                ins.then_inc(oh_made, 1)

            def take(n, slot):
                dve.wait_ge(moved, n + 2)
                dve.wait_ge(compacted, n * 2 + 2)
                dve.sem_inc(sorting, 1)
                dve.tensor_copy(wins[:, slot, :], ps[:, 4 + slot, 0:G * 4 * WB]).then_inc(taken, 1)

            onehots(0, 0)
            with dve.Fori(0, STEPS // 2 - 1) as i:
                for r in range(2):
                    dve.wait_ge(moved, i * 2 + (r + 1))
                    onehots(i * 2 + (r + 1), 1 - r)
                    take(i * 2 + r, r)
            dve.wait_ge(moved, STEPS - 1)
            onehots(STEPS - 1, 1)
            take(STEPS - 2, 0)
            take(STEPS - 1, 1)
            dve.wait_ge(compacted, 2 * STEPS + 4)

            dve.wait_ge(x_in, 16)
            link(dve.tensor_reduce(stats[:, 0, :], resid[:, :, :], AX.X, ALU.add))
            link(dve.tensor_scalar(stats[:, 0, :], stats[:, 0, :], 1.0 / P, None, ALU.mult))
            dve.sem_inc(mean_ready, 1)

            link(dve.memset(ones_b, 1.0))
            nb = dve.value_load(bcount[0:1, 0:1], min_val=1, max_val=BLOCKS)

            def keys(i):
                cb = bass.ds(i * W, W)
                return [lambda: dve.scalar_tensor_tensor(lin.unsqueeze(1), ca[:, 2:3, cb], 128.0, ca[:, 3:4, cb], ALU.mult, ALU.add),
                        lambda: dve.scalar_tensor_tensor(keyr.unsqueeze(1), lin.unsqueeze(1), float(N - 1), ca[:, 0:1, cb], ALU.is_lt, ALU.mult)]

            with dve.Fori(0, nb) as i:
                kk = keys(i)
                kk[0]().then_inc(blk_c, 1)
                dve.wait_ge(blk_c, i * 3 + 1)
                kk[1]().then_inc(blk_c, 1)
                dve.wait_ge(blk_c, i * 3 + 2)
                dve.tensor_tensor(keyc.unsqueeze(1), ca[:, 0:1, bass.ds(i * W, W)], keyr.unsqueeze(1), ALU.subtract).then_inc(blk_c, 1)
                dve.wait_ge(blk_c, i * 3 + 3)
                dve.sem_inc(sorting, 1)
                with dve.Fori(0, CSTEPS // 2) as j:
                    for r in range(2):
                        n = j * (2 * G * B) + r * G * B
                        dve.wait_ge(clamped, i * CSTEPS + (j * 2 + (r + 1)))
                        dv = ca[:, 1, bass.ds(i * W + n, G * B)].rearrange("p (g b) -> p g b", g=G).unsqueeze(2).to_broadcast([P, G, P, B])
                        kv = keyc[:, bass.ds(n, G * B)].rearrange("p (g b) -> p g b", g=G).unsqueeze(2).to_broadcast([P, G, T, B])
                        dve.tensor_tensor(ohq[:, r], rep.unsqueeze(1).to_broadcast([P, G, P, B]), dv, ALU.is_equal)
                        dve.tensor_tensor(coh[:, r], rep[:, 1:T + 1, :].unsqueeze(1).to_broadcast([P, G, T, B]), kv, ALU.is_equal).then_inc(coh_made, 1)
            dve.wait_ge(nclamp_ready, 1)
            link(dve.tensor_copy(nclamp[:, :], ps[:, 6, 0:T]))
            dve.sem_inc(nclamp_ready, 1)

            dve.wait_ge(x_in, 16)
            dve.wait_ge(small_in, 16 * 18)
            dve.wait_ge(squared, T)
            nvar[0] += 1
            dve.tensor_scalar(stats[:, 1, :], stats[:, 1, :], 1.0 / P, EPS, ALU.mult, ALU.add).then_inc(var_ready, 1)
            dve.wait_ge(row_summed, 2 * T)
            link(dve.tensor_tensor(dinv[:, :], deg2[:, :, 0], deg2[:, :, 1], ALU.add))
            link(dve.tensor_scalar(dinv[:, :], dinv[:, :], 1.0, None, ALU.add))
            link(dve.tensor_scalar(dmask[:, :], dinv[:, :], 0.0, None, ALU.is_gt))
            nvar[0] += 1
            dve.tensor_scalar(dinv[:, :], dinv[:, :], 1e-30, None, ALU.max).then_inc(var_ready, 1)
            dve.wait_ge(std_ready, nvar[0])
            link(dve.reciprocal(stats[:, 1, :], stats[:, 1, :]))
            link(dve.reciprocal(dinv[:, :], dinv[:, :]))
            link(dve.tensor_tensor(dinv[:, :], dinv[:, :], dmask[:, :], ALU.mult))
            link(dve.tensor_tensor(stats[:, 1, :], stats[:, 1, :], dinv[:, :], ALU.mult))
            dve.tensor_tensor(featp, featp, bc(stats[:, 1, :], [P, T, P]), ALU.mult).then_inc(feats0, 1)
            link(dve.tensor_tensor(resid[:, :, :], resid[:, :, :], bc(bias0, [P, T, P], 1), ALU.add))


            with dve.Fori(0, nb) as i:
                kk = keys(i)
                kk[0]().then_inc(cnt_c, 1)
                dve.wait_ge(cnt_c, i * 3 + 1)
                kk[1]().then_inc(cnt_c, 1)
                dve.wait_ge(cnt_c, i * 3 + 2)
                dve.sem_inc(sorting, 1)
                with dve.Fori(0, T) as b:
                    dve.tensor_scalar(mk, keyr, iota[:, bass.ds(b + 1, 1)], 0.0, ALU.is_equal, ALU.add,
                                      accum_out=cnt1[:, bass.ds(b, 1)]).then_inc(counts, 1)
                    dve.wait_ge(counts, i * T + (b + 1))
                dve.tensor_tensor(cnt[:, :], cnt[:, :], cnt1[:, :], ALU.add).then_inc(cnt_c, 1)
                dve.wait_ge(cnt_c, i * 3 + 3)
            dve.sem_inc(counted, 1)
            dve.wait_ge(offs, 1)
            link(dve.tensor_copy(cnt[:, :], ps[:, 4, 0:T]))
            link(dve.tensor_copy(cnt1[:, :], ps[:, 5, 0:T]))
            dve.sem_inc(offs_taken, 1)
            link(dve.tensor_scalar(ngi[:, :], cnt1[:, :], 1.0 / GE, None, ALU.mult))
            link(dve.tensor_copy(gend[:, :], ngi[:, :]))
            link(dve.scalar_tensor_tensor(ngf[:, :], gend[:, :], float(GE), cnt1[:, :], ALU.mult, ALU.is_lt))
            link(dve.tensor_tensor(ngf[:, :], ngf[:, :], gend[:, :], ALU.add))
            link(dve.tensor_scalar(ngf[:, :], ngf[:, :], 1.0, None, ALU.max))
            link(dve.tensor_tensor_scan(gend[:, :], ones_b[:, 0:T], ngf[:, :], 0.0, ALU.mult, ALU.add))
            link(dve.tensor_tensor(cur[:, :], gend[:, :], ngf[:, :], ALU.subtract))
            link(dve.tensor_scalar(cur[:, :], cur[:, :], float(GE), -1.0, ALU.mult, ALU.add))
            link(dve.tensor_tensor(cur[:, :], cur[:, :], cnt[:, :], ALU.add))
            link(dve.tensor_scalar(gcount[:, :], gend[:, T - 1:T], float(GR - 1), None, ALU.add))
            link(dve.tensor_scalar(gcount[:, :], gcount[:, :], GR.bit_length() - 1, None, ALU.logical_shift_right))
            K = NGP // P
            link(dve.tensor_tensor(gcv, bc(gid[:, :], [P, K, T]), bc(gend[:, :], [P, K, T], 1), ALU.is_ge))
            link(dve.tensor_reduce(gbf[:, :], gcv, AX.X, ALU.add))
            dve.tensor_scalar(gbi[:, :], gbf[:, :], float(T - 1), None, ALU.min).then_inc(gbi_ready, 1)

            for k in range(NB):
                dve.wait_ge(lin_ready, k + 1)
                kb = (k % 2) * 4
                for t in range(TB):
                    g = k * TB + t
                    ins = dve.scalar_tensor_tensor(resid[:, g, :], ps[:, kb + t // 4, (t % 4) * P:(t % 4 + 1) * P],
                                                   dinv[:, g:g + 1], resid[:, g, :], ALU.mult, ALU.add)
                ins.then_inc(x1_ready, 1)
                if k:
                    continue
                dve.sem_inc(blk_scattered, 1)
                with dve.Fori(0, nb) as i:
                    kk = keys(i)
                    dve.wait_ge(blk_scattered, i + 1)
                    kk[0]().then_inc(rank_c, 1)
                    dve.wait_ge(rank_c, i * (2 * T + 4) + 1)
                    kk[1]().then_inc(rank_c, 1)
                    dve.wait_ge(rank_c, i * (2 * T + 4) + 2)
                    dve.scalar_tensor_tensor(pay.unsqueeze(1), lin.unsqueeze(1), 256.0, ca[:, 1:2, bass.ds(i * W, W)], ALU.mult, ALU.add).then_inc(rank_c, 1)
                    dve.wait_ge(rank_c, i * (2 * T + 4) + 3)
                    dve.memset(pos, 1 << 30).then_inc(rank_c, 1)
                    dve.wait_ge(rank_c, i * (2 * T + 4) + 4)
                    dve.sem_inc(sorting, 1)
                    with dve.Fori(0, T) as b:
                        dve.tensor_scalar(mk, keyr, iota[:, bass.ds(b + 1, 1)], None, ALU.is_equal).then_inc(rank_c, 1)
                        dve.wait_ge(rank_c, i * (2 * T + 4) + (b * 2 + 5))
                        dve.tensor_tensor_scan(sc, ones_b, mk, cur[:, bass.ds(b, 1)], ALU.mult, ALU.add).then_inc(rank_c, 1)
                        dve.wait_ge(rank_c, i * (2 * T + 4) + (b * 2 + 6))
                        dve.tensor_scalar(cur[:, bass.ds(b, 1)], sc[:, W - 1:W], 0.0, None, ALU.add)
                        dve.copy_predicated(pos, mk.bitcast(U16), sc).then_inc(cur_moved, 1)
                        dve.wait_ge(cur_moved, i * T + (b + 1))
                    dve.sem_inc(pos_ready, 1)

            dve.wait_ge(x1_ready, NB)
            dve.wait_ge(w1_in, 32)
            dve.wait_ge(b1_done, 1)
            link(dve.tensor_tensor(b1a[:, :], b1a[:, :], ps[:, 7, 0:E0 * C0], ALU.add))
            dve.tensor_tensor(w1av, w1av, bc(lngb[:, 0, :], [P, E0, H0]), ALU.mult).then_inc(wa_ready, 1)
            layer_norms(0, twice=True)
            dve.wait_ge(lg_ready, 1)
            link(dve.tensor_tensor(lgt, ps[:, 2, 0:T * E0].rearrange("p (t e) -> p t e", t=T), bc(stats[:, 0, :], [P, T, E0]), ALU.mult))
            link(dve.tensor_tensor(lgt, lgt, bc(brr, [P, T, E0], 1), ALU.add))
            best(lgt, 1)

            def combine(E, base_y, base_b):
                with dve.Fori(0, NBLK) as i:
                    link.enter(i, 1)
                    bt = bass.ds(i * SB4, SB4)
                    dve.tensor_scalar(gst[:, :, :], gates[:, bt, :], 0.0, None, ALU.add).then_inc(gst_ready, 1)
                    for e in range(E):
                        dve.wait_ge(y_ready, i * E + (base_y + e + 3))
                        for t in range(SB4):
                            g = bass.ds(i * SB4 + t, 1)
                            ins = dve.scalar_tensor_tensor(resid[:, g, :], ps[:, 4 + e % 2, t * P:(t + 1) * P].unsqueeze(1),
                                                           gates[:, g, e], resid[:, g, :], ALU.mult, ALU.add)
                        ins.then_inc(y_added, 1)
                        dve.wait_ge(y_added, i * E + (base_y + e + 3))
                    dve.wait_ge(bt_ready, i + (base_b + 1))
                    link(dve.tensor_tensor(resid[:, bt, :], resid[:, bt, :],
                                           ps[:, 7, :].rearrange("p (t f) -> p t f", t=SB4), ALU.add))
                    link.leave(NBLK)

            dve.sem_inc(y_added, 2)
            combine(E0, 0, 0)

            dve.wait_ge(wext_done, 1)
            link(dve.tensor_copy(wext[:, P:P + 2], ps[:, 6, 0:2]))
            dve.sem_inc(wext_ready, 1)
            link(dve.memset(feath[:, :, P:P + 1], 1.0))
            layer_norms(1)
            dve.wait_ge(hx_copied, NBLK + 2)
            dve.tensor_reduce(small[:, 0:2], asd[:, :, :], AX.X, ALU.max).then_inc(mx_ready, 1)
            dve.wait_ge(mxt_ready, 1)
            link(dve.tensor_reduce(small[0:2, 4:5], ps[0:2, 2, 0:P], AX.X, ALU.max))
            dve.tensor_scalar(small[0:2, 8:10], ident[0:2, 0:2], small[0:2, 4:5], None, ALU.mult).then_inc(mxd_ready, 1)
            dve.wait_ge(mxb_ready, 1)
            link(dve.tensor_copy(small[:, 2:4], ps[:, 3, 0:2]))
            low, high, low8, low2, nhigh = [small[:, c:c + 1] for c in (5, 6, 7, 10, 11)]
            link(dve.tensor_tensor(low, small[:, 2:3], small[:, 3:4], ALU.add))
            link(dve.tensor_scalar(low, low, 64.0, None, ALU.is_le))
            link(dve.tensor_copy(low_i[:, :], low))
            link(dve.tensor_scalar(high, low, -1.0, 1.0, ALU.mult, ALU.add))
            link(dve.tensor_scalar(nhigh, high, -1.0, None, ALU.mult))
            link(dve.tensor_scalar(low8, low, 0.8, None, ALU.mult))
            link(dve.tensor_scalar(low2, low, -0.2, None, ALU.mult))
            link(dve.tensor_scalar(fac[:, 0, :], asd[:, 0, :], small[:, 2:3], None, ALU.subtract))
            link(dve.tensor_scalar(fac[:, 1, :], fac[:, 0, :], 0.2, None, ALU.mult))
            link(dve.tensor_scalar(asd[:, 1, :], asd[:, 1, :], small[:, 2:3], None, ALU.add))
            link(dve.tensor_scalar(asd[:, 0, :], asd[:, 1, :], 0.0, None, ALU.max))
            link(dve.tensor_scalar(fac[:, 2, :], asd[:, 1, :], 0.0, None, ALU.min))
            link(dve.tensor_scalar(fac[:, 2, :], fac[:, 2, :], high, None, ALU.mult))
            link(dve.scalar_tensor_tensor(fac[:, 2, :], asd[:, 1, :], low8, fac[:, 2, :], ALU.mult, ALU.add))
            link(dve.scalar_tensor_tensor(fac[:, 3, :], asd[:, 1, :], 0.2, asd[:, 0, :], ALU.mult, ALU.subtract))
            link(dve.tensor_scalar(fac[:, 4, :], asd[:, 0, :], nhigh, None, ALU.mult))
            link(dve.scalar_tensor_tensor(fac[:, 4, :], asd[:, 1, :], low2, fac[:, 4, :], ALU.mult, ALU.add))
            link(dve.tensor_scalar(fac[:, 4, :], fac[:, 4, :], 60.0, None, ALU.min))
            dve.sem_inc(fac_in, 1)
            dve.wait_ge(fac_ready, 1)
            link(dve.tensor_scalar(fac[:, 4, :], fac[:, 4, :], 1e-8, None, ALU.mult))
            dve.wait_ge(qt_ready, 1)
            dve.tensor_copy(qst, ps[:, 4, 0:P]).then_inc(qs_ready, 1)
            is_low = dve.to_reg(dve.value_load(low_i[0:1, 0:1], min_val=0, max_val=1))

            dve.sem_inc(e_ready, 2)
            TURN = 2 * NS6
            for k in range(NB):
                dve.wait_ge(q_in, 16 * (k + 1))

                def masked(n, loaded, r, s):
                    dve.wait_ge(a6_in[r], loaded)
                    dve.sem_inc(sorting, 1)
                    dve.scalar_tensor_tensor(at6[r], at6[r], 0.0, prod[s], ALU.is_gt, ALU.mult).then_inc(e_ready, 1)

                def fast(n, s, j):
                    dve.tensor_scalar(prod[s], qb[:, 0, :], fac[:, 0, j], fac[:, 1, j], ALU.mult, ALU.max).then_inc(p_ready, 1)

                def general(n, s, j):
                    dve.tensor_scalar(prod[s], qb[:, 0, :], fac[:, 0, j], None, ALU.mult).then_inc(vpos, 1)
                    dve.wait_ge(vpos, n + 1)
                    dve.scalar_tensor_tensor(prod[s], qb[:, 1, :], fac[:, 1, j], prod[s], ALU.mult, ALU.max).then_inc(p_ready, 1)

                def block(make):
                    def pair(n0, trip, j):
                        n = trip * TURN + n0
                        for s in range(2):
                            dve.wait_ge(e_ready, n + (s + 1))
                            make(n + s, s, j(s))
                        for s in range(2):
                            dve.wait_ge(p_ready, n + (s + 1))
                            masked(n + s, trip * 32 + 16 * ((n0 + s) // NS6 + 1), (n0 + s) % NS6, s)

                    with dve.Fori(0, T // TURN) as i:
                        for m in range(0, TURN, 2):
                            pair(k * T + m, i, lambda s: bass.ds(i * TURN + (m + s), 1))
                    for m in range(T // TURN * TURN, T, 2):
                        pair(k * T + m, 0, lambda s: slice(m + s, m + s + 1))

                with dve.If_ne(is_low, 0):
                    block(fast)
                with dve.If_eq(is_low, 0):
                    block(general)
                dve.wait_ge(att_ready, k + 1)
                for b, m in ((0, 5), (5, 1)):
                    w = 3 if m > 1 else 1
                    den = ps[:, b:b + m, 0:w * 129].rearrange("p b (t f) -> p b t f", f=129)[:, :, :, P]
                    ts = slice(3 * b, 3 * b + m * w)
                    link(dve.tensor_tensor(rden[:, ts].rearrange("p (b t) -> p b t", b=m), den,
                                           fac[:, 4, k * TB + 3 * b:k * TB + 3 * b + m * w].rearrange("p (b t) -> p b t", b=m), ALU.add))
                link(dve.reciprocal(rden[:, 0:TB], rden[:, 0:TB]))
                if k:
                    dve.wait_ge(block_done, k)
                for b in range(6):
                    w = min(3, TB - 3 * b)
                    accv = ps[:, b, 0:w * 129].rearrange("p (t f) -> p t f", t=w)
                    ts = slice(3 * b, 3 * b + w)
                    ins = dve.tensor_tensor(quot[:, ts, :], accv[:, :, 0:P], bc(rden[:, ts], [P, w, P]), ALU.mult)
                ins.then_inc(eneg, 1)

            dve.wait_ge(eneg, NB)
            dve.tensor_scalar(qneg, quot, 0.0, None, ALU.min).then_inc(neg_ready, 1)
            dve.wait_ge(neg_ready, NB)
            rs = resid[:, (NB - 1) * TB:NB * TB, :]
            link(dve.tensor_scalar(quot, quot, 0.0, -1.0, ALU.max, ALU.add))
            link(dve.tensor_tensor(rs, rs, quot, ALU.add))
            dve.wait_ge(x3_ready, NB)
            link(dve.tensor_tensor(rs, rs, qneg, ALU.add))

            dve.wait_ge(scattered, 1)
            tmpw = ntab[:, 0:2, 0:HF].rearrange("p s (h e) -> p s h e", h=HEADS)
            wv = wgat[:, 0:HF].rearrange("p (h e) -> p h e", h=HEADS)
            for s in range(2):
                link(dve.tensor_tensor(tmpw[:, s], wv, attr[:, s], ALU.mult))
                link(dve.tensor_reduce(wgat[:, HF + s * HEADS:HF + (s + 1) * HEADS], tmpw[:, s], AX.X, ALU.add))
            dve.sem_inc(wgat_done, 1)
            layer_norms(2)
            dve.wait_ge(gat_copied, NBLK + 2)
            dve.sem_inc(ntab_ready, 1)
            dve.tensor_reduce(small[:, 0:HEADS], ntab[:, :, HF:TW].rearrange("p t h -> p h t"), AX.X, ALU.max).then_inc(emx, 1)
            dve.wait_ge(emxt, 1)
            link(dve.tensor_reduce(small[0:HEADS, 4:5], ps[0:HEADS, 2, 0:P], AX.X, ALU.max))
            dve.tensor_scalar(small[0:HEADS, 8:8 + HEADS], ident[0:HEADS, 0:HEADS], small[0:HEADS, 4:5], None, ALU.mult).then_inc(emxd, 1)
            dve.wait_ge(emxb, 1)
            link(dve.tensor_copy(small[:, 12:16], ps[:, 3, 0:HEADS]))
            link(dve.tensor_copy(dtab[:, :, 0:HEADS], ntab[:, :, TW:TW + HEADS]))
            link(dve.tensor_tensor(ee[:, 0], ntab[:, :, TW:TW + HEADS], bc(small[:, 12:16], [P, T, HEADS], 1), ALU.add))
            link(dve.scalar_tensor_tensor(dtab[:, :, HEADS:2 * HEADS], ee[:, 0], 0.2, ee[:, 0], ALU.mult, ALU.max))
            link(dve.tensor_tensor(ee[:, 0], ntab[:, :, HF:TW], ntab[:, :, TW:TW + HEADS], ALU.add))
            dve.wait_ge(last_in, 16)
            link(dve.tensor_tensor(ee[:, 1], bc(last[:, HF:TW], [P, T, HEADS], 1), ntab[:, :, TW:TW + HEADS], ALU.add))
            for s in range(2):
                link(dve.scalar_tensor_tensor(ee[:, s], ee[:, s], 0.2, ee[:, s], ALU.mult, ALU.max))
                link(dve.tensor_tensor(ee[:, s], ee[:, s], dtab[:, :, HEADS:2 * HEADS], ALU.subtract))
            dve.sem_inc(self_in, 1)
            dve.wait_ge(self_exp, 1)
            link(dve.tensor_tensor(ee[:, 1], ee[:, 1], bc(nclamp[:, :], [P, T, HEADS]), ALU.mult))
            link(dve.tensor_tensor(acc[:, :, HF:TW], ee[:, 0], ee[:, 1], ALU.add))
            for h in range(HEADS):
                hs = slice(h * EX, (h + 1) * EX)
                link(dve.tensor_tensor(acc[:, :, hs], ntab[:, :, hs], ee[:, 0, :, h:h + 1].to_broadcast([P, T, EX]), ALU.mult))
                link(dve.tensor_tensor(ag[:, :, hs], bc(last[:, hs], [P, T, EX], 1), ee[:, 1, :, h:h + 1].to_broadcast([P, T, EX]), ALU.mult))
            link(dve.tensor_tensor(acc[:, :, 0:HF], acc[:, :, 0:HF], ag, ALU.add))
            link(dve.memset(gb[0:1, 0:1], 0))
            dve.sem_inc(vals_ready, GR)
            dve.wait_ge(gb_in, 16)
            trips = dve.value_load(gcount[0:1, 0:1], min_val=1, max_val=GTRIPS)

            def unpack(r, loaded, k):
                dve.wait_ge(pt_in[r], loaded)
                dve.tensor_scalar(srci[:, r, :], pt[:, r, :], 8, None, ALU.logical_shift_right)
                dve.tensor_scalar(dli[:, r, :], pt[:, r, :], 255, None, ALU.bitwise_and).then_inc(unpacked, 1)
                dve.wait_ge(unpacked, k + 1)
                dve.tensor_copy(dlf[:, r, :], dli[:, r, :]).then_inc(grp_c, 1)

            def onehot(r, s):
                dve.tensor_tensor(oh[:, r, :, :], bc(iota[:, :], [P, GRP, P], 1), bc(dlf[:, s, :], [P, GRP, P]),
                                  ALU.is_equal).then_inc(oh_ready, 1)

            def take_sum(g, slot, done):
                bk = dve.value_load(gb[0:1, bass.ds(g, 1)], min_val=0, max_val=T - 1)
                dve.wait_ge(sum_ready, g + 2)
                dve.tensor_tensor(acc[:, bass.ds(bk, 1), :], acc[:, bass.ds(bk, 1), :],
                                  ps[:, 6 + slot, 0:TW].unsqueeze(1), ALU.add).then_inc(grp_c, 1)
                dve.wait_ge(grp_c, done)

            for g in range(GR - 1):
                unpack(g, 16, g)
            dve.wait_ge(grp_c, GR - 1)
            dve.wait_ge(sum_ready, 2)
            onehot(0, 0)
            with dve.Fori(0, trips) as i:
                for m in range(GR):
                    r = m % 2
                    k = i * (5 * GR) + (5 * m + GR - 1)
                    unpack((m + GR - 1) % GR, i * 16 + 16 * ((m + GR - 1) // GR + 1), i * GR + (m + GR - 1))
                    dve.wait_ge(sum_ready, i * GR + (m + 2))
                    onehot(1 - r, (m + 1) % GR)
                    dve.wait_ge(gathered[m], (i + 1) * 16 * GRP)
                    dve.wait_ge(dst_ready, i * GR + (m + 1))
                    pd = ps[:, 4 + r, 0:GRP * 8].rearrange("p (c k) -> p c k", k=8)
                    dve.tensor_tensor(zt, gt[:, m, :, HF:TW], pd[:, :, 0:HEADS], ALU.add).then_inc(grp_c, 1)
                    dve.wait_ge(grp_c, k + 2)
                    dve.scalar_tensor_tensor(zt, zt, 0.2, zt, ALU.mult, ALU.max).then_inc(grp_c, 1)
                    dve.wait_ge(grp_c, k + 3)
                    dve.tensor_tensor(zt, zt, pd[:, :, HEADS:2 * HEADS], ALU.subtract).then_inc(grp_c, 1)
                    dve.wait_ge(grp_c, k + 4)
                    dve.tensor_scalar(zt, zt, 0.0, None, ALU.min).then_inc(z_ready, 1)
                    take_sum(i * GR + m, 1 - r, k + 5)
                    dve.wait_ge(ez_ready, i * GR + (m + 1))
                    dve.tensor_tensor(vals[:, r, :, 0:HF].rearrange("p c (h e) -> p c h e", h=HEADS),
                                      gt[:, m, :, 0:HF].rearrange("p c (h e) -> p c h e", h=HEADS),
                                      vals[:, r, :, HF:TW].unsqueeze(3).to_broadcast([P, GRP, HEADS, EX]),
                                      ALU.mult).then_inc(vals_ready, 1)
            take_sum(trips * GR, 1, trips * (5 * GR) + GR)

            link(dve.tensor_scalar(ee[:, 0], acc[:, :, HF:TW], 1e-16, None, ALU.add))
            link(dve.reciprocal(ee[:, 0], ee[:, 0]))
            for h in range(HEADS):
                link(dve.tensor_tensor(ag[:, :, h * EX:(h + 1) * EX], acc[:, :, h * EX:(h + 1) * EX],
                                       ee[:, 0, :, h:h + 1].to_broadcast([P, T, EX]), ALU.mult))
            link(dve.tensor_tensor(ag, ag, bc(bgat, [P, T, HF], 1), ALU.add))
            link(dve.tensor_reduce(lst[:, 0, :], ag, AX.X, ALU.add))
            link(dve.tensor_scalar(lst[:, 0, :], lst[:, 0, :], 1.0 / HF, None, ALU.mult))
            link(dve.tensor_tensor(ag, ag, bc(lst[:, 0, :], [P, T, HF]), ALU.subtract))
            link(dve.tensor_tensor(ag2, ag, ag, ALU.mult))
            link(dve.tensor_reduce(lst[:, 1, :], ag2, AX.X, ALU.add))
            nvar[0] += 1
            dve.tensor_scalar(lst[:, 1, :], lst[:, 1, :], 1.0 / HF, EPS, ALU.mult, ALU.add).then_inc(var_ready, 1)
            dve.wait_ge(std_ready, nvar[0])
            link(dve.reciprocal(lst[:, 1, :], lst[:, 1, :]))
            link(dve.tensor_tensor(ag, ag, bc(lst[:, 1, :], [P, T, HF]), ALU.mult))
            link(dve.tensor_tensor(ag, ag, bc(gam, [P, T, HF], 1), ALU.mult))
            link(dve.tensor_tensor(ag, ag, bc(bet, [P, T, HF], 1), ALU.add))
            link(dve.memset(lg8, -3e38))
            link(dve.tensor_reduce(lg8[:, :, 0:EX], ag.rearrange("p t (h e) -> p t e h", h=HEADS), AX.X, ALU.add))
            link(dve.tensor_scalar(lg8[:, :, 0:EX], lg8[:, :, 0:EX], 1.0 / HEADS, None, ALU.mult))
            best(lg8, 2)
            combine(E1, NBLK * E0, NBLK)
            dve.sem_inc(out_ready, 1)

        @block.tensor
        def _(pe):
            def clear(bank, n=BANK):
                return pe.matmul(ps[:, bank, 0:n], zeros_b[:, 0:P], zeros_b[:, 0:n], start=True, stop=False,
                                 skip_group_check=True)

            def close(bank, n=BANK):
                return pe.matmul(ps[:, bank, 0:n], zeros_b[:, 0:P], zeros_b[:, 0:n], start=False, stop=True,
                                 skip_group_check=True)

            pe.wait_ge(const, 7)
            pe.wait_ge(tables_ready, 1)
            pe.wait_ge(valid_ready, 1)
            for k in range(EC // CH):
                ks = slice(k * CH, (k + 1) * CH)
                if k >= 2:
                    pe.wait_ge(off_used, k - 1)
                pe.matmul(ps[:, k % 2, :], lt_b, valid[:, ks], start=True, stop=True)
                pe.matmul(ps[:, 2 + k % 2, :], on_b, valid[:, ks], start=True, stop=True).then_inc(off_ready, 1)
            pe.sem_inc(taken, 2)
            pe.sem_inc(moved, 1)
            with pe.Fori(0, STEPS // 2) as i:
                for r in range(2):
                    pe.wait_ge(oh_made, i * 2 + (r + 1))
                    pe.wait_ge(taken, i * 2 + (r + 1))
                    for g in range(G):
                        for b in range(B):
                            ins = pe.matmul(ps[:, 4 + r, g * 4 * WB:(g + 1) * 4 * WB], ohq[:, r, g, :, b],
                                            rhs[:, r, g, :, :, b].rearrange("p k w -> p (k w)"), start=(b == 0), stop=(b == B - 1))
                    ins.then_inc(moved, 1)
            clear(6, T)
            pe.sem_inc(clamped, 2)
            pe.wait_ge(coh_made, 1)
            nb = pe.value_load(bcount[0:1, 0:1], min_val=1, max_val=BLOCKS)
            with pe.Fori(0, nb) as i:
                with pe.Fori(0, CSTEPS // 2) as j:
                    for r in range(2):
                        pe.wait_ge(coh_made, i * CSTEPS + (j * 2 + (r + 1)))
                        for g in range(G):
                            for b in range(B):
                                ins = pe.matmul(ps[:, 6, 0:T], ohq[:, r, g, :, b], coh[:, r, g, :, b], start=False, stop=False,
                                                skip_group_check=True)
                        ins.then_inc(clamped, 1)
            close(6, T).then_inc(nclamp_ready, 1)
            pe.wait_ge(nclamp_ready, 2)

            pe.wait_ge(feats0, 1)
            pe.sem_inc(tile_used, NS2)
            pe.wait_ge(small_in, 16 * 18)
            for k in range(NB):
                kb = (k % 2) * 4
                if k >= 2:
                    pe.wait_ge(x1_ready, k - 1)
                if k == 1:
                    pe.wait_ge(counted, 1)
                    pe.matmul(ps[:, 4, 0:T], lower[:, :], cnt[:, :], start=True, stop=True)
                    pe.matmul(ps[:, 5, 0:T], ones[:, :], cnt[:, :], start=True, stop=True).then_inc(offs, 1)
                    pe.wait_ge(offs_taken, 1)
                for b in range(4):
                    clear(kb + b)
                with pe.Fori(0, T // NS2) as i:
                    for r in range(NS2):
                        pe.wait_ge(at_in[r], i * 16 + (k * (T // NS2) * 16 + 16))
                        pe.wait_ge(staged_x, i * NS2 + (k * T + r + 1))
                        for b in range(4):
                            ins = pe.matmul(ps[:, kb + b, :], xs[:, r, :], at2[r][:, b * BANK:(b + 1) * BANK],
                                            start=False, stop=False, skip_group_check=True)
                        ins.then_inc(tile_used, 1)
                for t in range(TB):
                    pe.matmul(ps[:, kb + t // 4, (t % 4) * P:(t % 4 + 1) * P], featp[:, k * TB + t, :], ident[:, :],
                              start=False, stop=False, skip_group_check=True)
                for b in range(4):
                    ins = close(kb + b)
                ins.then_inc(agg_ready, 1)
                pe.wait_ge(agg_copied, 4 * (k + 1))
                for t in range(TB):
                    ins = pe.matmul(ps[:, kb + t // 4, (t % 4) * P:(t % 4 + 1) * P], agg[:, t * P:(t + 1) * P],
                                    w0t[:, :], start=True, stop=True)
                ins.then_inc(lin_ready, 1)

            pe.wait_ge(w1_in, 32)
            pe.wait_ge(x1_ready, NB)
            for e in range(E0):
                for h in range(C0):
                    ins = pe.matmul(ps[:, 7, e * C0 + h:e * C0 + h + 1], w1av[:, e, h * P:(h + 1) * P],
                                    lngb[:, 1, e:e + 1], start=True, stop=True)
            ins.then_inc(b1_done, 1)
            def transposes(g, product):
                for i in range(NBLK // 2):
                    for r in range(2):
                        n = 2 * i + r
                        pe.wait_ge(ln_ready, g * NBLK + n + 1)
                        for t in range(SB4):
                            ins = pe.transpose(ps[:, r, t * P:(t + 1) * P], un[:, n * SB4 + t, :], ident[:, :])
                        ins.then_inc(tr_ready, 1)
                    for r in range(2):
                        pe.wait_ge(tr_copied, g * NBLK + 2 * i + r + 1)
                        product(2 * i + r, r)

            def logits(n, r):
                for t in range(SB4):
                    c = (n * SB4 + t) * E0
                    ins = pe.matmul(ps[:, 2, c:c + E0], lgT[r][:, t * P:(t + 1) * P], wr[:, :], start=True, stop=True)
                if n == NBLK - 1:
                    ins.then_inc(lg_ready, 1)

            transposes(0, logits)

            def experts(E, C, w1v, w2v, b2, base_y, base_b, base_h):
                def hidden(i, e):
                    at = i * BANK
                    for h in range(C):
                        pe.wait_ge(hid_ready, i * (E * C) + (base_h + C * e + h + 1))
                        bank = h if C == 4 else h + 2 * (e % 2)
                        pe.matmul(ps[:, bank, :], w1v[:, e, h * P:(h + 1) * P],
                                  featT[:, slice(at, at + BANK) if isinstance(i, int) else bass.ds(at, BANK)],
                                  start=True, stop=True).then_inc(h_ready, 1)

                def one_block(i, last):
                    for e in range(E):
                        if e + 1 < E:
                            hidden(i, e + 1)
                        elif not last:
                            hidden(i + 1, 0)
                        pe.wait_ge(hid_ready, i * (E * C) + (base_h + C * (e + 1) + 4))
                        pe.wait_ge(y_added, i * E + (base_y + e + 1))
                        for t in range(SB4):
                            for h in range(C):
                                ins = pe.matmul(ps[:, 4 + e % 2, t * P:(t + 1) * P], hid[e % 2][:, h, t * P:(t + 1) * P],
                                                w2v[:, e, h, :], start=(h == 0), stop=(h == C - 1))
                        ins.then_inc(y_ready, 1)
                        if e == 0:
                            pe.wait_ge(gst_ready, i + (base_b + 1))
                            for t in range(SB4):
                                ins = pe.transpose(ps[0:8, 6, t * P:(t + 1) * P], gst[:, t, :], ident[:, :])
                            ins.then_inc(gt_ready, 1)
                        if e == 2:
                            pe.wait_ge(gts_ready, i + (base_b + 1))
                            for t in range(SB4):
                                ins = pe.matmul(ps[:, 7, t * P:(t + 1) * P], gts[0:E, t * P:(t + 1) * P], b2[:, :], start=True, stop=True)
                            ins.then_inc(bt_ready, 1)

                hidden(0, 0)
                with pe.Fori(0, NBLK - 1) as i:
                    one_block(i, False)
                one_block(NBLK - 1, True)

            pe.sem_inc(y_ready, 2)
            pe.wait_ge(wa_ready, 1)
            experts(E0, C0, w1av, w2av, b2a, 0, 0, 0)

            pe.wait_ge(small_in, 16 * 18)
            pe.matmul(ps[:, 6, 0:2], wg[:, :], att[:, :], start=True, stop=True).then_inc(wext_done, 1)
            pe.wait_ge(wext_ready, 1)
            def hidden_scores(n, r):
                pe.wait_ge(hx_copied, n + 1)
                for t in range(SB4):
                    ins = pe.matmul(ps[:, 2 + 2 * r + t // 2, (t % 2) * 256:(t % 2) * 256 + P + 2], uT[r][:, t * P:(t + 1) * P],
                                    wext[:, :], start=True, stop=True)
                ins.then_inc(hx_ready, 1)

            pe.sem_inc(hx_copied, 2)
            transposes(1, hidden_scores)
            pe.wait_ge(hx_copied, NBLK + 2)
            pe.wait_ge(mx_ready, 1)
            pe.transpose(ps[0:2, 2, 0:P], small[:, 0:2], ident[:, :]).then_inc(mxt_ready, 1)
            pe.wait_ge(mxd_ready, 1)
            pe.matmul(ps[:, 3, 0:2], ones[0:2, :], small[0:2, 8:10], start=True, stop=True).then_inc(mxb_ready, 1)
            pe.wait_ge(fac_ready, 1)
            pe.transpose(ps[:, 4, 0:P], fac[:, 2:4, :].rearrange("p k t -> p (k t)"), ident[:, :]).then_inc(qt_ready, 1)
            pe.wait_ge(qs_ready, 1)

            for k in range(NB):
                if k:
                    pe.wait_ge(eneg, k)
                for b in range(6):
                    clear(b, 129 * min(3, TB - 3 * b))

                def tile6(n, r, j):
                    pe.wait_ge(e_ready, n + 3)
                    for t in range(TB):
                        ins = pe.matmul(ps[:, t // 3, (t % 3) * 129:(t % 3 + 1) * 129], at6[r][:, t * P:(t + 1) * P],
                                        feath[:, j, 0:129], start=False, stop=False, skip_group_check=True)
                    ins.then_inc(e_used, 1)

                full = T // NS6
                with pe.Fori(0, full) as i:
                    for m in range(NS6):
                        tile6(i * NS6 + (k * T + m), (k * T + m) % NS6, bass.ds(i * NS6 + m, 1))
                for m in range(full * NS6, T):
                    tile6(k * T + m, (k * T + m) % NS6, slice(m, m + 1))
                for b in range(6):
                    ins = close(b, 129 * min(3, TB - 3 * b))
                ins.then_inc(att_ready, 1)

            pe.wait_ge(wgat_done, 1)
            def features(n, r):
                pe.wait_ge(gat_copied, n + 1)
                for t in range(SB4):
                    ins = pe.matmul(ps[:, 2 + r, t * 24:(t + 1) * 24], lgT[r][:, t * P:(t + 1) * P], wgat[:, :], start=True, stop=True)
                ins.then_inc(gat_ready, 1)

            pe.sem_inc(gat_copied, 2)
            transposes(2, features)
            pe.wait_ge(gat_copied, NBLK + 2)
            pe.wait_ge(emx, 1)
            pe.transpose(ps[0:HEADS, 2, 0:P], small[:, 0:HEADS], ident[:, :]).then_inc(emxt, 1)
            pe.wait_ge(emxd, 1)
            pe.matmul(ps[:, 3, 0:HEADS], ones[0:HEADS, :], small[0:HEADS, 8:8 + HEADS], start=True, stop=True).then_inc(emxb, 1)
            pe.wait_ge(vals_ready, GR)
            pe.wait_ge(gb_in, 16)
            trips = pe.value_load(gcount[0:1, 0:1], min_val=1, max_val=GTRIPS)

            def dst_side(r, g, need):
                pe.wait_ge(oh_ready, need)
                for q in range(GRP):
                    ins = pe.transpose(ps[:, 2 * r + q // 4, (q % 4) * P:(q % 4 + 1) * P], oh[:, r, q, :], ident[:, :])
                ins.then_inc(ohp_ready, 1)
                bk = pe.value_load(gb[0:1, bass.ds(g + 1, 1)] if not isinstance(g, int) else gb[0:1, g + 1:g + 2], min_val=0, max_val=T - 1)
                pe.wait_ge(oht_ready, need)
                for q in range(GRP):
                    ins = pe.matmul(ps[:, 4 + r, q * 8:(q + 1) * 8], oht[:, r, q, :], dtab[:, bass.ds(bk, 1), :],
                                    start=True, stop=True)
                ins.then_inc(dst_ready, 1)

            pe.matmul(ps[:, 7, 0:TW], zeros_b[:, 0:P], zeros_b[:, 0:TW], start=True, stop=True).then_inc(sum_ready, 2)
            dst_side(0, 0, 1)
            with pe.Fori(0, trips) as i:
                for m in range(GR):
                    r = m % 2
                    dst_side(1 - r, i * GR + (m + 1), i * GR + (m + 2))
                    pe.wait_ge(vals_ready, i * GR + (m + 1 + GR))
                    for q in range(GRP):
                        ins = pe.matmul(ps[:, 6 + r, 0:TW], oh[:, r, q, :], vals[:, r, q, :], start=(q == 0), stop=(q == GRP - 1))
                    ins.then_inc(sum_ready, 1)

            pe.wait_ge(w1b_in, 32)
            experts(E1, C1, w1bv, w2bv, b2b, NBLK * E0, NBLK, NBLK * E0 * C0)

        @block.scalar
        def _(act):
            def root(ap, n, trip=None):
                act.wait_ge(var_ready, n if trip is None else trip + n)
                act.activation(ap, ap, ACT.Sqrt).then_inc(std_ready, 1)

            with act.Fori(0, 2 * T // 6) as i:
                for k in range(6):
                    r = k % NS1
                    act.wait_ge(arow_in[r], i * 32 + (k // NS1 * 16 + 16))
                    act.activation(arow[r], arow[r], ACT.Copy,
                                   accum_out=deg2[:, bass.ds(i * 3 + k // 2, 1), k % 2]).then_inc(row_summed, 1)
            for n in range(6 * (2 * T // 6), 2 * T):
                r = n % NS1
                act.wait_ge(arow_in[r], 16 * (n // NS1 + 1))
                act.activation(arow[r], arow[r], ACT.Copy, accum_out=deg2[:, n // 2, n % 2:n % 2 + 1]).then_inc(row_summed, 1)
            act.wait_ge(x_centred, 1)
            with act.Fori(0, T) as i:
                act.activation(lnsq, featp[:, bass.ds(i, 1), :], ACT.Square, accum_out=stats[:, 1, bass.ds(i, 1)]).then_inc(squared, 1)
                act.wait_ge(squared, i + 1)
            root(stats[:, 1, :], 1)
            root(dinv[:, :], 2)
            nv = 2

            act.wait_ge(feats0, 1)
            for k in range(NB):
                with act.Fori(0, T // NS2) as i:
                    for r in range(NS2):
                        act.wait_ge(tile_used, i * NS2 + (k * T + r + 1))
                        act.sem_inc(slot_taken, 1)
                        act.activation(xs[:, r, :].unsqueeze(1), featp[:, bass.ds(i * NS2 + r, 1), :], ACT.Copy).then_inc(staged_x, 1)
                act.wait_ge(agg_ready, k + 1)
                kb = (k % 2) * 4
                for b in range(4):
                    act.activation(agg[:, b * BANK:(b + 1) * BANK], ps[:, kb + b, :], ACT.Copy).then_inc(agg_copied, 1)

            def preparation(g, nv, per, copies):
                def square(c):
                    act.wait_ge(sub_ready, g * NB + c + 1)
                    if g * NB + c:
                        act.wait_ge(sq_used, g * NB + c)
                    act.activation(sqn, un[:, c * TB:(c + 1) * TB, :], ACT.Square).then_inc(sq_ready, 1)

                def blocks(c):
                    with act.Fori(c * (TB // SB4 // 2), (c + 1) * (TB // SB4 // 2)) as i:
                        copies(i)

                square(0)
                for c in range(NB):
                    ts = slice(c * TB, (c + 1) * TB)
                    root(stats[:, 1, ts], nv + c * per + 1)
                    if per == 2:
                        root(stats[:, 0, ts], nv + c * per + 2)
                    if c + 1 < NB:
                        square(c + 1)
                    if c:
                        blocks(c - 1)
                blocks(NB - 1)
                return nv + NB * per

            def to_experts(g):
                def copies(i):
                    for r in range(2):
                        act.wait_ge(tr_ready, i * 2 + (g * NBLK + r + 1))
                        act.activation(lgT[r], ps[:, r, :], ACT.Copy)
                        act.activation(featT[:, bass.ds(i * (2 * BANK) + r * BANK, BANK)], ps[:, r, :], ACT.Copy).then_inc(tr_copied, 1)
                    if g:
                        for r in range(2):
                            act.wait_ge(gat_ready, i * 2 + (r + 1))
                            act.sem_inc(slot_taken, 1)
                            act.activation(ntab[:, bass.ds(i * (2 * SB4) + r * SB4, SB4), :],
                                           ps[:, 2 + r, 0:SB4 * 24].rearrange("p (t k) -> p t k", t=SB4), ACT.Copy).then_inc(gat_copied, 1)
                return copies

            nv = preparation(0, nv, 2, to_experts(0))
            act.wait_ge(tops_done, 1)
            act.activation(wts[:, 0, :], wts[:, 0, :], ACT.Exp).then_inc(exp_ready, 1)

            def gelus(E, C, b1, base_y, base_b, base_h):
                with act.Fori(0, NBLK) as i:
                    for e in range(E):
                        for h in range(C):
                            act.wait_ge(h_ready, i * (E * C) + (base_h + e * C + h + 1))
                            if h == 0:
                                act.wait_ge(y_ready, i * E + (base_y + e + 1))
                            bank = h if C == 4 else h + 2 * (e % 2)
                            act.activation(hid[e % 2][:, h, :], ps[:, bank, :], ACT.Gelu,
                                           bias=b1[:, e * C + h:e * C + h + 1]).then_inc(hid_ready, 1)
                        if e == 2:
                            act.wait_ge(gt_ready, i + (base_b + 1))
                            act.activation(gts[:, :], ps[0:8, 6, :], ACT.Copy).then_inc(gts_ready, 1)

            act.sem_inc(hid_ready, 4)
            act.wait_ge(wa_ready, 1)
            gelus(E0, C0, b1a, 0, 0, 0)

            def to_attention(i):
                for r in range(2):
                    act.wait_ge(tr_ready, i * 2 + (NBLK + r + 1))
                    act.activation(uT[r], ps[:, r, :], ACT.Copy).then_inc(tr_copied, 1)
                for r in range(2):
                    bt = bass.ds(i * (2 * SB4) + r * SB4, SB4)
                    hv = ps[:, 2 + 2 * r:4 + 2 * r, :].rearrange("p b (t w) -> p (b t) w", t=2)
                    act.wait_ge(hx_ready, i * 2 + (r + 1))
                    act.sem_inc(slot_taken, 1)
                    act.activation(feath[:, bt, 0:P], hv[:, :, 0:P], ACT.Copy)
                    act.activation(asd[:, :, bt].rearrange("p s t -> p t s"), hv[:, :, P:P + 2], ACT.Copy).then_inc(hx_copied, 1)

            nv = preparation(1, nv, 1, to_attention)
            act.wait_ge(fac_in, 1)
            act.activation(fac[:, :, :], fac[:, :, :], ACT.Exp).then_inc(fac_ready, 1)
            act.wait_ge(q_out, 16)
            qrows = q_d.rearrange("(k t) p -> k (t p)", k=2)

            def elu(k):
                act.wait_ge(neg_ready, k + 1)
                act.activation(qneg, qneg, ACT.Exp).then_inc(x3_ready, 1)

            for k in range(NB):
                if k:
                    act.wait_ge(p_ready, k * T)
                act.dma_start(qb[:, :, :], qrows[:, k * IB:(k + 1) * IB].unsqueeze(0).to_broadcast([P, 2, IB])).then_inc(q_in, 16)
                act.wait_ge(q_in, 16 * (k + 1))
                if k:
                    elu(k - 1)
            elu(NB - 1)
            act.wait_ge(scattered, 1)
            nv = preparation(2, nv, 1, to_experts(2))
            act.wait_ge(self_in, 1)
            act.activation(ee, ee, ACT.Exp).then_inc(self_exp, 1)
            act.wait_ge(gb_in, 16)
            trips = act.value_load(gcount[0:1, 0:1], min_val=1, max_val=GTRIPS)

            def turn(r, need):
                act.wait_ge(ohp_ready, need)
                flat = ps[:, 2 * r:2 * r + 2, :].rearrange("p b n -> p (b n)")[:, 0:GRP * P]
                act.activation(oht[:, r, :, :].rearrange("p c n -> p (c n)"), flat, ACT.Copy).then_inc(oht_ready, 1)

            turn(0, 1)
            with act.Fori(0, trips) as i:
                for m in range(GR):
                    r = m % 2
                    turn(1 - r, i * GR + (m + 2))
                    act.wait_ge(z_ready, i * GR + (m + 1))
                    act.wait_ge(sum_ready, i * GR + (m + 1))
                    act.activation(vals[:, r, :, HF:TW], zt, ACT.Exp).then_inc(ez_ready, 1)
            nv += 1
            root(lst[:, 1, :], nv)
            act.wait_ge(tops_done, 2)
            act.activation(wts[:, 0, :], wts[:, 0, :], ACT.Exp).then_inc(exp_ready, 1)
            gelus(E1, C1, b1b, NBLK * E0, NBLK, NBLK * E0 * C0)


_ORDER = ["x", "adj", "adjT", "edge_index", "W0T", "b0", "Wr", "br", "lngb", "W1a", "b1a", "W2a", "b2a",
          "Wg", "WgT", "attn", "W_gat", "att_src", "att_dst", "b_gat", "ln_gamma", "ln_beta",
          "W1b", "b1b", "W2b", "b2b"]


def kernel(x, adj, L0_gnn_W, L0_gnn_b, L0_ffn_Wr, L0_ffn_br, L0_ffn_ln_g, L0_ffn_ln_b, L0_ffn_W1, L0_ffn_b1,
           L0_ffn_W2, L0_ffn_b2, L1_gnn_W, L1_gnn_attn_src, L1_gnn_attn_dst, L1_ffn_W_gat, L1_ffn_att_src,
           L1_ffn_att_dst, L1_ffn_b_gat, L1_ffn_ln_gamma, L1_ffn_ln_beta, L1_ffn_W1, L1_ffn_b1, L1_ffn_W2,
           L1_ffn_b2, L1_ffn_edge_index):
    import numpy as np
    import concourse.bacc as bacc
    from concourse.bass_utils import run_bass_kernel_spmd

    A = np.ascontiguousarray
    n = x.shape[0]

    def cols(b):
        b = np.asarray(b)
        return A(b.reshape(b.shape[0], -1, 128).transpose(2, 0, 1).reshape(128, -1))

    def down(w):
        w = np.asarray(w)
        return A(w.reshape(w.shape[0], -1, 128, w.shape[2]).transpose(2, 0, 1, 3))

    adj = np.asarray(adj)
    arrays = {
        "x": A(x), "adj": A(adj), "adjT": A(adj.reshape(4, n // 4, n).transpose(0, 2, 1)),
        "edge_index": A(L1_ffn_edge_index),
        "W0T": A(np.asarray(L0_gnn_W).T), "b0": A(L0_gnn_b), "Wr": A(L0_ffn_Wr), "br": A(L0_ffn_br),
        "lngb": A(np.stack([np.asarray(L0_ffn_ln_g).T, np.asarray(L0_ffn_ln_b).T], axis=1)),
        "W1a": A(np.asarray(L0_ffn_W1).transpose(1, 0, 2)), "b1a": cols(L0_ffn_b1), "W2a": down(L0_ffn_W2), "b2a": A(L0_ffn_b2),
        "Wg": A(L1_gnn_W), "WgT": A(np.asarray(L1_gnn_W).T),
        "attn": A(np.concatenate([np.asarray(L1_gnn_attn_src), np.asarray(L1_gnn_attn_dst)]).T),
        "W_gat": A(L1_ffn_W_gat), "att_src": A(np.asarray(L1_ffn_att_src).reshape(-1)),
        "att_dst": A(np.asarray(L1_ffn_att_dst).reshape(-1)), "b_gat": A(L1_ffn_b_gat),
        "ln_gamma": A(L1_ffn_ln_gamma), "ln_beta": A(L1_ffn_ln_beta),
        "W1b": A(np.asarray(L1_ffn_W1).transpose(1, 0, 2)), "b1b": cols(L1_ffn_b1), "W2b": down(L1_ffn_W2), "b2b": A(L1_ffn_b2),
    }
    nc = bacc.Bacc("TRN2", target_bir_lowering=False, num_devices=1)
    d = {k: nc.dram_tensor(f"in_{k}", arrays[k].shape, mybir.dt.from_np(arrays[k].dtype), kind="ExternalInput").ap()
         for k in _ORDER}
    out = nc.dram_tensor("out_0", (n, 128), F32, kind="ExternalOutput").ap()
    build(nc, d, out)
    r = run_bass_kernel_spmd(nc, [{f"in_{k}": arrays[k] for k in _ORDER}], core_ids=[0])
    return r.results[0]["out_0"]
```

```python
from contextlib import ExitStack

import concourse.bass as bass
from concourse import mybir

F32 = mybir.dt.float32
I32 = mybir.dt.int32
BF16 = mybir.dt.bfloat16
U16 = mybir.dt.uint16
ALU = mybir.AluOpType
ACT = mybir.ActivationFunctionType
AX = mybir.AxisListType

P = 128
BANK = 512
EPS = 1e-5


class Chain:

    def __init__(self, eng, sem):
        self.eng, self.sem, self.n, self.trip = eng, sem, 0, None

    def __call__(self, ins):
        self.n += 1
        ins.then_inc(self.sem, 1)
        self.eng.wait_ge(self.sem, self.n if self.trip is None else self.trip + self.n)

    def enter(self, i, per, first=0):
        self.trip, self.start, self.per = i * per, self.n, per
        self.n -= first * per

    def leave(self, trips, first=0):
        assert self.n + first * self.per - self.start == self.per, (self.n + first * self.per - self.start, self.per)
        self.trip, self.n = None, self.start + trips * self.per


def build(nc, d, out):
    N = d["x"].shape[0]
    T = N // P
    IB = 2048
    NB = N // IB
    TB = IB // P
    E0, H0 = d["W1a"].shape[1], d["W1a"].shape[2]
    E1, H1 = d["W1b"].shape[1], d["W1b"].shape[2]
    C0, C1 = H0 // P, H1 // P
    SB4 = 4
    NBLK = T // SB4
    HEADS = 4
    EX = E1
    HF = HEADS * EX
    TW = HF + HEADS

    NE = d["edge_index"].shape[1]
    EC = NE // P
    B, G = 8, 2
    WB = B + 1
    STEPS = EC // (B * G)
    W = 1056
    BLOCKS = -(-(EC + WB) // W)
    CW = W * BLOCKS
    CSTEPS = W // (B * G)
    CH = BANK
    GRP = 5
    GE = GRP * P
    GR = 4
    NG = NE // GE + T
    NGP = -(-(NG + 2) // P) * P
    GTRIPS = -(-NG // GR)
    assert GR * (GTRIPS + 1) <= NGP
    SC = 16

    sorted_d = nc.dram_tensor("sorted_edges", (NGP * GE, 1), I32, kind="Internal").ap()
    table_d = nc.dram_tensor("node_table", (N, TW), F32, kind="Internal").ap()
    gb_d = nc.dram_tensor("group_bucket", (NGP,), I32, kind="Internal").ap()
    q_d = nc.dram_tensor("score_factors", (P, P), F32, kind="Internal").ap()

    with ExitStack() as c:
        def sb(n, s, dt=F32):
            return c.enter_context(nc.sbuf_tensor(n, s, dt))

        def sem(n):
            return c.enter_context(nc.semaphore(n))

        ps = c.enter_context(nc.psum_tensor("ps", [P, 8, BANK], F32))

        resid = sb("resid", [P, T, P])
        feat = sb("feat", [P, T * 130])
        work = sb("work", [P, 18432])
        edge = sb("edge", [P, 3 * EC])
        ident = sb("ident", [P, P])
        lower = sb("lower", [P, P])
        ones = sb("ones", [P, P])
        iota_i = sb("iota_i", [P, P], I32)
        iota = sb("iota", [P, P])
        zeros_b = sb("zeros_b", [P, BANK], BF16)
        w0t = sb("w0t", [P, P])
        wr = sb("wr", [P, E0])
        rows = sb("rows", [P, P + E0 + 5 * HF])
        b2a = sb("b2a", [E0, P])
        b2b = sb("b2b", [E1, P])
        lngb = sb("lngb", [P, 2, E0])
        b1a = sb("b1a", [P, E0 * C0])
        b1b = sb("b1b", [P, E1 * C1])
        wg = sb("wg", [P, P])
        wext = sb("wext", [P, P + 2])
        att = sb("att", [P, 2])
        wgat = sb("wgat", [P, HF + 2 * HEADS])
        stats = sb("stats", [P, 2, T])
        deg2 = sb("deg2", [P, T, 2])
        dinv = sb("dinv", [P, T])
        dmask = sb("dmask", [P, T])
        gates = sb("gates", [P, T, 8])
        gst = sb("gst", [P, SB4, 8])
        tops = sb("tops", [P, 2, T])
        wts = sb("wts", [P, 2, T])
        gts = sb("gts", [8, BANK])
        small = sb("small", [P, 16])
        low_i = sb("low_i", [P, 1], I32)
        asd = sb("asd", [P, 2, T])
        fac = sb("fac", [P, 5, T])
        cnt = sb("cnt", [P, T])
        cnt1 = sb("cnt1", [P, T])
        nclamp = sb("nclamp", [P, T])
        ngi = sb("ngi", [P, T], I32)
        ngf = sb("ngf", [P, T])
        gend = sb("gend", [P, T])
        cur = sb("cur", [P, T])
        gid_i = sb("gid_i", [P, NGP // P], I32)
        gid = sb("gid", [P, NGP // P])
        gbf = sb("gbf", [P, NGP // P])
        gbi = sb("gbi", [P, NGP // P], I32)
        gcount = sb("gcount", [P, 1], I32)
        bcount = sb("bcount", [P, 1], I32)
        vcount = sb("vcount", [P, 1])
        stg_i = sb("stg_i", [P, 2, SC], I32)
        stg_p = sb("stg_p", [P, 2, SC], I32)
        woh = sb("woh", [P, 2, G, WB, B], BF16)
        rhs = sb("rhs", [P, 2, G, 4, WB, B], BF16)
        wins = sb("wins", [P, 2, G * 4 * WB], BF16)

        bias0 = rows[:, 0:P]
        brr = rows[:, P:P + E0]
        attr = rows[:, P + E0:P + E0 + 2 * HF].rearrange("p (s h e) -> p s h e", s=2, h=HEADS)
        bgat = rows[:, P + E0 + 2 * HF:P + E0 + 3 * HF]
        gam = rows[:, P + E0 + 3 * HF:P + E0 + 4 * HF]
        bet = rows[:, P + E0 + 4 * HF:P + E0 + 5 * HF]

        NS1 = 3
        HALF = N // 2
        arow = [work[:, r * HALF:(r + 1) * HALF] for r in range(NS1)]
        ew = NS1 * HALF
        es = resid[:, :, :].rearrange("p t f -> p (t f)")[:, 0:2 * EC].bitcast(I32).rearrange("p (two e) -> p two e", two=2)
        ci = resid[:, 0:CH // P, :].rearrange("p t f -> p (t f)").bitcast(I32)
        ci2 = resid[:, CH // P:2 * CH // P, :].rearrange("p t f -> p (t f)").bitcast(I32)
        pcs = feat[:, 0:2 * EC].bitcast(BF16).rearrange("p (k e) -> p k e", k=4)
        ca = edge[:, 0:2 * CW].bitcast(BF16).rearrange("p (k w) -> p k w", k=4)
        wbi = gates[:, :, :].rearrange("p t e -> p (t e)")[:, 0:EC // B].bitcast(I32)
        fillt = edge[:, 0:NGP * GE // P // 8].bitcast(I32)
        o = 2 * CW
        pos = edge[:, o:o + W].bitcast(I32)
        pay = edge[:, o + W:o + 2 * W].bitcast(I32)
        lnsq = work[:, 18432 - P:18432].unsqueeze(1)
        ohq = edge[:, o:o + G * P * B].bitcast(BF16).rearrange("p (s g q b) -> p s g q b", s=2, g=G, q=P)
        o += G * P * B
        rep = edge[:, o:o + P * B // 2].bitcast(BF16).rearrange("p (q b) -> p q b", q=P)
        o += P * B // 2
        incl = edge[:, o:o + CH]
        gcv = edge[:, o:o + NGP // P * T].rearrange("p (k b) -> p k b", b=T)
        o += CH
        base = edge[:, o:o + CH]
        o += CH
        lt_b = edge[:, o:o + P // 2].bitcast(BF16)
        o += P // 2
        on_b = edge[:, o:o + P // 2].bitcast(BF16)
        o += P // 2
        assert o <= 3 * EC
        valid = work[:, ew:ew + EC // 2].bitcast(BF16)
        tmp = work[:, ew + EC // 2:ew + EC // 2 + EC].bitcast(I32)
        qq = work[:, ew + EC // 2:ew + EC].bitcast(BF16)
        wl = work[:, ew + EC:ew + EC + EC // 2].bitcast(BF16)
        o = ew
        lin = work[:, o:o + W]
        sc = lin.bitcast(I32)
        o += W
        keyr, keyc, mk, ones_b = [work[:, o + n * W // 2:o + (n + 1) * W // 2].bitcast(BF16) for n in range(4)]
        o += 2 * W
        coh = work[:, o:o + G * T * B].bitcast(BF16).rearrange("p (s g q b) -> p s g q b", s=2, g=G, q=T)
        assert o + G * T * B <= 18432 - P
        NS2 = 4
        at2 = [work[:, r * IB:(r + 1) * IB] for r in range(NS2)]
        agg = work[:, NS2 * IB:(NS2 + 1) * IB]
        xs = work[:, (NS2 + 1) * IB:(NS2 + 1) * IB + NS2 * P].rearrange("p (r f) -> p r f", r=NS2)
        assert (NS2 + 1) * IB + NS2 * P <= ew
        featp = feat[:, 0:T * P].rearrange("p (t f) -> p t f", t=T)
        feath = feat[:, :].rearrange("p (t f) -> p t f", t=T)
        featT = feat[:, 0:N]
        w1av = work[:, 0:E0 * H0].rearrange("p (e h) -> p e h", e=E0)
        w2av = work[:, E0 * H0:2 * E0 * H0].rearrange("p (e c f) -> p e c f", e=E0, c=C0)
        w1bv = work[:, 12288:12288 + E1 * H1].rearrange("p (e h) -> p e h", e=E1)
        w2bv = work[:, 12288 + E1 * H1:12288 + 2 * E1 * H1].rearrange("p (e c f) -> p e c f", e=E1, c=C1)
        hid = [work[:, 8192 + r * 2048:8192 + (r + 1) * 2048].rearrange("p (c n) -> p c n", n=BANK) for r in range(2)]
        un = edge[:, 0:T * P].rearrange("p (t f) -> p t f", t=T)
        sqn = work[:, 16384:16384 + TB * P].rearrange("p (t f) -> p t f", t=TB)
        uT = [edge[:, 3 * EC - (r + 1) * BANK:3 * EC - r * BANK] for r in range(2)]
        assert 2 * CW + 2 * W <= 3 * EC - 2 * BANK
        qst = work[:, 18432 - P:18432]
        lgt = work[:, 16384:16384 + 8 * T].rearrange("p (t e) -> p t e", t=T)
        topv = work[:, 16896:16896 + 8 * T].rearrange("p (t e) -> p t e", t=T)
        topx = work[:, 17408:17408 + 8 * T].bitcast(mybir.dt.uint32).rearrange("p (t e) -> p t e", t=T)
        NS6 = 4
        at6 = [work[:, r * IB:(r + 1) * IB] for r in range(NS6)]
        prod = [work[:, (NS6 + r) * IB:(NS6 + r + 1) * IB] for r in range(2)]
        qb = work[:, (NS6 + 2) * IB:(NS6 + 4) * IB].rearrange("p (k n) -> p k n", k=2)
        rden = stats[:, 0, :]
        quots = [edge[:, 2 * 4096:2 * 4096 + TB * P]] * (NB - 1) + [prod[0]]
        qnegs = [edge[:, 2 * 4096 + TB * P:3 * 4096]] * (NB - 1) + [prod[1]]
        quots, qnegs = [[v.rearrange("p (t f) -> p t f", t=TB) for v in vs] for vs in (quots, qnegs)]
        oh = work[:, 0:GR * GRP * P].rearrange("p (r c n) -> p r c n", r=GR, c=GRP)
        oht = work[:, GR * GRP * P:(GR + 2) * GRP * P].rearrange("p (r c n) -> p r c n", r=2, c=GRP)
        o = (GR + 2) * GRP * P
        gt = work[:, o:o + GR * GRP * TW].rearrange("p (r c k) -> p r c k", r=GR, c=GRP)
        o += GR * GRP * TW
        vals = work[:, o:o + 2 * GRP * TW].rearrange("p (r c k) -> p r c k", r=2, c=GRP)
        o += 2 * GRP * TW
        pt = work[:, o:o + GR * GRP].bitcast(I32).rearrange("p (r c) -> p r c", r=GR)
        o += GR * GRP
        srci = work[:, o:o + GR * GRP].bitcast(I32).rearrange("p (r c) -> p r c", r=GR)
        o += GR * GRP
        dli = work[:, o:o + GR * GRP].bitcast(I32).rearrange("p (r c) -> p r c", r=GR)
        o += GR * GRP
        dlf = work[:, o:o + GR * GRP].rearrange("p (r c) -> p r c", r=GR)
        o += GR * GRP
        zt = work[:, o:o + GRP * HEADS].rearrange("p (c k) -> p c k", c=GRP)
        o += GRP * HEADS
        last = work[:, o:o + TW]
        o += TW
        assert o <= 5120
        ntab = work[:, 5120:5120 + T * 24].rearrange("p (t k) -> p t k", t=T)
        gb = work[0:1, 14336:14336 + NGP + 1].bitcast(I32)
        o = 0
        dtab = edge[:, o:o + T * 8].rearrange("p (t k) -> p t k", t=T)
        o += T * 8
        acc = edge[:, o:o + T * TW].rearrange("p (t k) -> p t k", t=T)
        o += T * TW
        ee = edge[:, o:o + 2 * T * HEADS].rearrange("p (s t k) -> p s t k", s=2, t=T)
        o += 2 * T * HEADS
        ag = edge[:, o:o + T * HF].rearrange("p (t k) -> p t k", t=T)
        o += T * HF
        ag2 = edge[:, o:o + T * HF].rearrange("p (t k) -> p t k", t=T)
        o += T * HF
        lg8 = edge[:, o:o + T * 8].rearrange("p (t k) -> p t k", t=T)
        o += T * 8
        lst = edge[:, o:o + 2 * T].rearrange("p (s t) -> p s t", s=2)
        o += 2 * T

        const = sem("const"); fill_made = sem("fill_made"); tables_ready = sem("tables_ready")
        edges_in = sem("edges_in"); valid_ready = sem("valid_ready"); off_ready = sem("off_ready"); off_used = sem("off_used")
        windows_ready = sem("windows_ready"); win_oh = sem("win_oh"); oh_made = sem("oh_made"); moved = sem("moved"); taken = sem("taken")
        compacted = sem("compacted"); coh_made = sem("coh_made"); clamped = sem("clamped"); nclamp_ready = sem("nclamp_ready")
        blk_c = sem("blk_c"); counted = sem("counted"); rank_c = sem("rank_c"); cnt_c = sem("cnt_c"); blk_scattered = sem("blk_scattered")
        last_in = sem("last_in"); unpacked = sem("unpacked")
        x_in = sem("x_in"); small_in = sem("small_in")
        arow_in = [sem(f"arow_in{r}") for r in range(NS1)]
        row_summed = sem("row_summed")
        dve_c = sem("dve_c")
        var_ready = sem("var_ready"); std_ready = sem("std_ready")
        counts = sem("counts"); offs = sem("offs"); cur_moved = sem("cur_moved"); pos_ready = sem("pos_ready")
        scat = [sem("scat0"), sem("scat1")]; staged = sem("staged"); slot_open = sem("slot_open"); slot_taken = sem("slot_taken"); sorting = sem("sorting")
        gbi_ready = sem("gbi_ready"); gb_out = sem("gb_out"); gb_in = sem("gb_in"); scattered = sem("scattered")
        feats0 = sem("feats0")
        at_in = [sem(f"at_in{r}") for r in range(NS2)]
        staged_x = sem("staged_x"); tile_used = sem("tile_used"); agg_ready = sem("agg_ready")
        agg_copied = sem("agg_copied"); lin_ready = sem("lin_ready"); x1_ready = sem("x1_ready")
        w1_in = sem("w1_in"); wa_ready = sem("wa_ready"); b1_done = sem("b1_done")
        ln_ready = sem("ln_ready"); sub_ready = sem("sub_ready"); sq_ready = sem("sq_ready"); sq_used = sem("sq_used");
        tr_ready = sem("tr_ready"); tr_copied = sem("tr_copied")
        lg_ready = sem("lg_ready"); tops_done = sem("tops_done"); exp_ready = sem("exp_ready"); gates_ready = sem("gates_ready")
        gst_ready = sem("gst_ready"); gt_ready = sem("gt_ready"); gts_ready = sem("gts_ready"); bt_ready = sem("bt_ready")
        h_ready = sem("h_ready"); hid_ready = sem("hid_ready"); y_ready = sem("y_ready"); y_added = sem("y_added")
        hx_ready = sem("hx_ready"); hx_copied = sem("hx_copied"); wext_ready = sem("wext_ready"); wext_done = sem("wext_done")
        mx_ready = sem("mx_ready"); mxt_ready = sem("mxt_ready"); mxd_ready = sem("mxd_ready"); mxb_ready = sem("mxb_ready")
        fac_in = sem("fac_in"); fac_ready = sem("fac_ready"); qt_ready = sem("qt_ready"); qs_ready = sem("qs_ready"); q_out = sem("q_out"); q_in = sem("q_in")
        a6_in = [sem(f"a6_in{r}") for r in range(NS6)]
        p_ready = sem("p_ready"); e_ready = sem("e_ready"); e_used = sem("e_used"); att_ready = sem("att_ready")
        vpos = sem("vpos"); eneg = sem("eneg"); neg_ready = sem("neg_ready"); elu_c = sem("elu_c"); mean_ready = sem("mean_ready"); x_centred = sem("x_centred"); squared = sem("squared"); offs_taken = sem("offs_taken"); x3_ready = sem("x3_ready")
        block_done = sem("block_done"); gat_ready = sem("gat_ready"); gat_copied = sem("gat_copied")
        wgat_done = sem("wgat_done"); ntab_ready = sem("ntab_ready"); tab_out = sem("tab_out")
        emx = sem("emx"); emxt = sem("emxt"); emxd = sem("emxd"); emxb = sem("emxb")
        self_in = sem("self_in"); self_exp = sem("self_exp")
        pt_in = [sem(f"pt_in{r}") for r in range(GR)]; gathered = [sem(f"gathered{r}") for r in range(GR)]
        oh_ready = sem("oh_ready"); ohp_ready = sem("ohp_ready"); oht_ready = sem("oht_ready"); dst_ready = sem("dst_ready")
        z_ready = sem("z_ready"); ez_ready = sem("ez_ready"); vals_ready = sem("vals_ready"); sum_ready = sem("sum_ready")
        grp_c = sem("grp_c")
        w1b_in = sem("w1b_in")
        out_ready = sem("out_ready"); out_done = sem("out_done")

        SMALL = 18

        block = c.enter_context(nc.Block())

        @block.sync
        def _(sp):
            sp.dma_start(es, d["edge_index"].rearrange("two (p e) -> p two e", p=P)).then_inc(edges_in, 16)

            def row(ap):
                return ap.rearrange("(a n) -> a n", a=1).to_broadcast([P, ap.shape[0]])

            loads = [(w0t[:, :], d["W0T"]), (wr[:, :], d["Wr"]), (bias0, row(d["b0"])), (brr, row(d["br"])),
                     (attr[:, 0].rearrange("p h e -> p (h e)"), row(d["att_src"])),
                     (attr[:, 1].rearrange("p h e -> p (h e)"), row(d["att_dst"])),
                     (bgat, row(d["b_gat"])), (gam, row(d["ln_gamma"])), (bet, row(d["ln_beta"])),
                     (b2a[:, :], d["b2a"]), (b2b[:, :], d["b2b"]),
                     (lngb[:, :, :], d["lngb"]), (b1a[:, :], d["b1a"]), (b1b[:, :], d["b1b"]),
                     (wg[:, :], d["Wg"]), (wext[:, 0:P], d["WgT"]), (att[:, :], d["attn"]),
                     (wgat[:, 0:HF], d["W_gat"])]
            for dst, src in loads:
                sp.dma_start(dst, src).then_inc(small_in, 16)

            halves = d["adj"].rearrange("(t p) (h n) -> t h p n", p=P, h=2)

            def load_half(n, r):
                sp.dma_start(arow[r], halves[n // 2, n % 2]).then_inc(arow_in[r], 16)

            for n in range(NS1):
                load_half(n, n)
            def turns(first, end):
                with sp.Fori(first, end) as i:
                    for n in range(6):
                        sp.wait_ge(row_summed, 6 * i + (n + 1))
                        m = n + NS1
                        sp.dma_start(arow[n % NS1], halves[3 * i + m // 2, m % 2]).then_inc(arow_in[n % NS1], 16)

            full = (2 * T - NS1) // 6
            turns(0, 4)
            sp.wait_ge(windows_ready, 1)
            sp.dma_start(resid[:, :, :], d["x"].rearrange("(t p) f -> p t f", p=P)).then_inc(x_in, 16)
            turns(4, full)
            for n in range(6 * full + NS1, 2 * T):
                sp.wait_ge(row_summed, n - NS1 + 1)
                load_half(n, n % NS1)

            tiles = d["adjT"].rearrange("k (j p) n -> (k j) p n", p=P)
            sp.wait_ge(row_summed, 2 * T)
            for r in range(NS2):
                sp.dma_start(at2[r], tiles[r]).then_inc(at_in[r], 16)
            with sp.Fori(0, NB * T // NS2 - 1) as i:
                for r in range(NS2):
                    sp.wait_ge(tile_used, i * NS2 + (NS2 + r + 1))
                    sp.dma_start(at2[r], tiles[i * NS2 + (NS2 + r)]).then_inc(at_in[r], 16)

            sp.wait_ge(x1_ready, NB)
            sp.dma_start(w1av, d["W1a"]).then_inc(w1_in, 16)
            sp.dma_start(w2av, d["W2a"]).then_inc(w1_in, 16)

            sp.wait_ge(qs_ready, 1)
            sp.dma_start(q_d, qst).then_inc(q_out, 16)
            for r in range(NS6):
                sp.dma_start(at6[r], tiles[r]).then_inc(a6_in[r], 16)
            total = NB * T
            full = (total - NS6) // NS6
            with sp.Fori(0, full) as i:
                for r in range(NS6):
                    sp.wait_ge(e_used, i * NS6 + (r + 1))
                    sp.dma_start(at6[r], tiles[i * NS6 + (NS6 + r)]).then_inc(a6_in[r], 16)
            for n in range(full * NS6, total - NS6):
                sp.wait_ge(e_used, n + 1)
                sp.dma_start(at6[n % NS6], tiles[n + NS6]).then_inc(a6_in[n % NS6], 16)

            sp.wait_ge(ntab_ready, 1)
            sp.dma_start(table_d.rearrange("(t p) k -> p t k", p=P), ntab[:, :, 0:TW]).then_inc(tab_out, 16)
            sp.wait_ge(tab_out, 16)
            sp.dma_start(last, table_d[N - 1:N, :].to_broadcast([P, TW])).then_inc(last_in, 16)
            sp.wait_ge(gb_out, 16)
            sp.dma_start(gb[0:1, 1:NGP + 1], gb_d.rearrange("(a g) -> a g", a=1)).then_inc(gb_in, 16)
            sp.dma_start(w1bv, d["W1b"]).then_inc(w1b_in, 16)
            sp.dma_start(w2bv, d["W2b"]).then_inc(w1b_in, 16)
            sp.wait_ge(scattered, 1)
            trips = sp.value_load(gcount[0:1, 0:1], min_val=1, max_val=GTRIPS)
            groups = sorted_d.rearrange("(g p r) o -> g p (r o)", p=P, r=GRP)
            for r in range(GR):
                sp.dma_start(pt[:, r, :], groups[r]).then_inc(pt_in[r], 16)
            with sp.Fori(0, trips) as i:
                for r in range(GR):
                    sp.wait_ge(unpacked, i * GR + (r + 1))
                    sp.dma_start(pt[:, r, :], groups[i * GR + (GR + r)]).then_inc(pt_in[r], 16)

            sp.wait_ge(out_ready, 1)
            sp.dma_start(out.rearrange("(t p) f -> p t f", p=P), resid[:, :, :]).then_inc(out_done, 16)
            sp.wait_ge(out_done, 16)

        @block.gpsimd
        def _(pool):
            pool.iota(iota_i[:, :], pattern=[[1, P]], base=0, channel_multiplier=0).then_inc(const, 1)
            pool.iota(gid_i[:, :], pattern=[[P, NGP // P]], base=0, channel_multiplier=1).then_inc(const, 1)
            pool.memset(ones[:, :], 1.0).then_inc(const, 1)
            pool.memset(ident[:, :], 0.0).then_inc(const, 1)
            pool.memset(zeros_b[:, :], 0.0).then_inc(const, 1)
            pool.memset(fillt, 255).then_inc(fill_made, 1)
            pool.wait_ge(const, 5)
            pool.affine_select(out=ident[:, :], in_=ident[:, :], compare_op=ALU.not_equal, fill=1.0, base=0,
                               pattern=[[-1, P]], channel_multiplier=1).then_inc(const, 1)
            pool.affine_select(out=lower[:, :], in_=ones[:, :], compare_op=ALU.is_gt, fill=0.0, base=0,
                               pattern=[[1, P]], channel_multiplier=-1).then_inc(const, 1)
            pool.wait_ge(fill_made, 1)
            fill_v = sorted_d.rearrange("(k p r) o -> k p (r o)", k=8, p=P)
            for k in range(8):
                pool.dma_start(fill_v[k], fillt).then_inc(scat[k % 2], 16)
            FILL = 16 * 4
            slot_bound = pool.to_reg(NG * GE - 1)
            node_bound = pool.to_reg(N - 1)
            for r in range(2):
                pool.wait_ge(scat[r], FILL)
            pool.memset(ca, 0.0).then_inc(compacted, 4)
            pool.wait_ge(compacted, 4)
            pool.wait_ge(windows_ready, 1)
            with pool.Fori(0, STEPS // 2) as i:
                for r in range(2):
                    ws = [pool.value_load(wbi[0:1, bass.ds(i * (2 * G) + (r * G + g), 1)], min_val=0, max_val=CW - WB) for g in range(G)]
                    pool.wait_ge(taken, i * 2 + (r + 3))
                    pool.sem_inc(slot_open, 1)
                    for g in range(G):
                        dst = ca[:, :, bass.ds(ws[g], WB)]
                        pool.tensor_tensor(dst, dst, wins[:, r, g * 4 * WB:(g + 1) * 4 * WB].rearrange("p (k w) -> p k w", k=4),
                                           ALU.add).then_inc(compacted, 1)
                        pool.wait_ge(compacted, i * 4 + (2 * r + g + 5))

            pool.wait_ge(mean_ready, 1)
            pool.tensor_tensor(featp, resid[:, :, :], stats[:, 0, :].unsqueeze(2).to_broadcast([P, T, P]), ALU.subtract).then_inc(x_centred, 1)

            pool.wait_ge(gbi_ready, 1)
            with nc.allow_non_contiguous_dma(reason="one word per group of edges"):
                pool.dma_start(gb_d.rearrange("(k p) -> p k", p=P), gbi[:, :]).then_inc(gb_out, 16)
            pool.wait_ge(gb_out, 16)

            per = W // (2 * SC)
            pool.wait_ge(pos_ready, 1)
            nb = pool.value_load(bcount[0:1, 0:1], min_val=1, max_val=BLOCKS)
            with pool.Fori(0, nb) as i:
                pool.wait_ge(pos_ready, i + 1)
                pool.sem_inc(slot_open, 1)
                with pool.Fori(0, per) as n:
                    for r in range(2):
                        pool.wait_ge(scat[r], (i * per + n) * (16 * SC) + FILL)
                        pool.tensor_copy(stg_i[:, r, :], pos[:, bass.ds(n * (2 * SC) + r * SC, SC)]).then_inc(staged, 1)
                        pool.tensor_copy(stg_p[:, r, :], pay[:, bass.ds(n * (2 * SC) + r * SC, SC)]).then_inc(staged, 1)
                        pool.wait_ge(staged, (i * per + n) * 4 + (2 * r + 2))
                        pool.sem_inc(slot_open, 1)
                        for k in range(SC):
                            pool.indirect_dma_start(sorted_d, bass.IndirectOffsetOnAxis(ap=stg_i[:, r, k:k + 1], axis=0),
                                                    stg_p[:, r, k:k + 1], None, bounds_check=slot_bound,
                                                    oob_is_err=False).then_inc(scat[r], 16)
                for r in range(2):
                    pool.wait_ge(scat[r], (i + 1) * (per * 16 * SC) + FILL)
                pool.sem_inc(blk_scattered, 1)
            pool.sem_inc(scattered, 1)
            for k in range(NB - 1):
                quot, qneg = quots[k], qnegs[k]
                pool.wait_ge(eneg, k + 1)
                pool.tensor_scalar(qneg, quot, 0.0, None, ALU.min).then_inc(neg_ready, 1)
                pool.wait_ge(neg_ready, k + 1)
                pool.tensor_scalar(quot, quot, 0.0, -1.0, ALU.max, ALU.add).then_inc(elu_c, 1)
                pool.wait_ge(elu_c, 2 * k + 1)
                rs = resid[:, k * TB:(k + 1) * TB, :]
                pool.tensor_tensor(rs, rs, quot, ALU.add).then_inc(elu_c, 1)
                pool.wait_ge(elu_c, 2 * k + 2)
                pool.wait_ge(x3_ready, k + 1)
                pool.tensor_tensor(rs, rs, qneg, ALU.add).then_inc(block_done, 1)

            pool.wait_ge(tab_out, 16)
            trips = pool.value_load(gcount[0:1, 0:1], min_val=1, max_val=GTRIPS)
            with pool.Fori(0, trips) as i:
                for r in range(GR):
                    pool.wait_ge(unpacked, i * GR + (r + 1))
                    pool.wait_ge(vals_ready, i * GR + (r + 1))
                    pool.sem_inc(slot_open, 1)
                    for k in range(GRP):
                        pool.indirect_dma_start(gt[:, r, k, :], None, table_d,
                                                bass.IndirectOffsetOnAxis(ap=srci[:, r, k:k + 1], axis=0),
                                                bounds_check=node_bound, oob_is_err=False).then_inc(gathered[r], 16)

        @block.vector
        def _(dve):
            link = Chain(dve, dve_c)
            nvar = [0]

            def bc(ap, shape, axis=2):
                return ap.unsqueeze(axis).to_broadcast(shape)

            def centre(g, c):
                ts = slice(c * TB, (c + 1) * TB)
                link(dve.tensor_reduce(stats[:, 0, ts], resid[:, ts, :], AX.X, ALU.add))
                link(dve.tensor_scalar(stats[:, 0, ts], stats[:, 0, ts], 1.0 / P, None, ALU.mult))
                dve.tensor_tensor(un[:, ts, :], resid[:, ts, :], bc(stats[:, 0, ts], [P, TB, P]), ALU.subtract).then_inc(sub_ready, 1)

            def variance(g, c, keep=False):
                ts = slice(c * TB, (c + 1) * TB)
                var = stats[:, 1, ts]
                dve.wait_ge(sq_ready, g * NB + c + 1)
                link(dve.tensor_reduce(var, sqn, AX.X, ALU.add))
                dve.sem_inc(sq_used, 1)
                link(dve.tensor_scalar(var, var, 1.0 / P, None, ALU.mult))
                if keep:
                    link(dve.tensor_copy(stats[:, 0, ts], var))
                nvar[0] += 1
                dve.tensor_scalar(var, var, EPS, None, ALU.add).then_inc(var_ready, 1)

            def scale(g, c, twice=False):
                ts = slice(c * TB, (c + 1) * TB)
                var = stats[:, 1, ts]
                dve.wait_ge(std_ready, nvar[0])
                link(dve.reciprocal(var, var))
                if twice:
                    link(dve.tensor_tensor(stats[:, 0, ts], stats[:, 0, ts], var, ALU.mult))
                    link(dve.tensor_tensor(stats[:, 0, ts], stats[:, 0, ts], var, ALU.mult))
                    nvar[0] += 1
                    dve.tensor_scalar(stats[:, 0, ts], stats[:, 0, ts], EPS, None, ALU.add).then_inc(var_ready, 1)
                    dve.wait_ge(std_ready, nvar[0])
                    link(dve.reciprocal(small[:, 0:TB], stats[:, 0, ts]))
                    link(dve.tensor_tensor(var, var, small[:, 0:TB], ALU.mult))
                dve.tensor_tensor(un[:, ts, :], un[:, ts, :], bc(var, [P, TB, P]), ALU.mult).then_inc(ln_ready, SB4)

            def twice_normal(c):
                variance(0, c, keep=True)
                scale(0, c, twice=True)

            def best(logits, first):
                for t in range(T):
                    ins = dve.max(topv[:, t, :], logits[:, t, :])
                link(ins)
                for t in range(T):
                    ins = dve.max_index(topx[:, t, :], topv[:, t, :], logits[:, t, :])
                link(ins)
                for s in range(2):
                    link(dve.tensor_copy(tops[:, s, :], topx[:, :, s]))
                dve.tensor_tensor(wts[:, 0, :], topv[:, :, 1], topv[:, :, 0], ALU.subtract).then_inc(tops_done, 1)
                dve.wait_ge(exp_ready, first)
                link(dve.tensor_scalar(wts[:, 1, :], wts[:, 0, :], 1.0, None, ALU.add))
                link(dve.reciprocal(wts[:, 1, :], wts[:, 1, :]))
                link(dve.tensor_tensor(wts[:, 0, :], wts[:, 0, :], wts[:, 1, :], ALU.mult))
                i8 = bc(iota[:, 0:8], [P, T, 8], 1)
                link(dve.tensor_tensor(gates[:, :, :], i8, bc(tops[:, 0, :], [P, T, 8]), ALU.is_equal))
                link(dve.tensor_tensor(gates[:, :, :], gates[:, :, :], bc(wts[:, 1, :], [P, T, 8]), ALU.mult))
                link(dve.tensor_tensor(logits, i8, bc(tops[:, 1, :], [P, T, 8]), ALU.is_equal))
                link(dve.tensor_tensor(logits, logits, bc(wts[:, 0, :], [P, T, 8]), ALU.mult))
                dve.tensor_tensor(gates[:, :, :], gates[:, :, :], logits, ALU.add).then_inc(gates_ready, 1)
                dve.wait_ge(gates_ready, first)

            dve.wait_ge(const, 7)
            link(dve.tensor_copy(iota[:, :], iota_i[:, :]))
            link(dve.tensor_copy(gid[:, :], gid_i[:, :]))
            link(dve.tensor_copy(rep, bc(iota_i[:, :], [P, P, B])))
            link(dve.tensor_copy(lt_b, lower[:, :]))
            link(dve.tensor_copy(on_b, ones[:, :]))
            link(dve.memset(cnt[:, :], 0.0))
            dve.sem_inc(tables_ready, 1)
            dve.wait_ge(edges_in, 16)
            link(dve.tensor_scalar(tmp, es[:, 1, :], 7, None, ALU.logical_shift_right))
            link(dve.tensor_scalar(valid, tmp, float(T), None, ALU.is_lt))
            dve.sem_inc(valid_ready, 1)
            link(dve.scalar_tensor_tensor(pcs[:, 0, :], tmp, 1.0, valid, ALU.add, ALU.mult))
            link(dve.tensor_scalar(tmp, es[:, 1, :], P - 1, None, ALU.bitwise_and))
            link(dve.tensor_tensor(pcs[:, 1, :], tmp, valid, ALU.mult))
            link(dve.tensor_scalar(es[:, 0, :], es[:, 0, :], float(N - 1), 0.0, ALU.min, ALU.max))
            link(dve.tensor_scalar(tmp, es[:, 0, :], 7, None, ALU.logical_shift_right))
            link(dve.tensor_tensor(pcs[:, 2, :], tmp, valid, ALU.mult))
            link(dve.tensor_scalar(tmp, es[:, 0, :], P - 1, None, ALU.bitwise_and))
            link(dve.tensor_tensor(pcs[:, 3, :], tmp, valid, ALU.mult))
            for k in range(EC // CH):
                ks = slice(k * CH, (k + 1) * CH)
                kw = slice(k * CH // B, (k + 1) * CH // B)
                before, total = ps[:, k % 2, :], ps[:, 2 + k % 2, :]
                dve.wait_ge(off_ready, k + 1)
                link(dve.tensor_tensor_scan(incl, zeros_b[:, 0:CH], total, 0.0 if k == 0 else vcount[:, 0:1], ALU.add, ALU.add))
                link(dve.tensor_copy(vcount[:, :], incl[:, CH - 1:CH]))
                link(dve.tensor_tensor(base, incl, total, ALU.subtract))
                link(dve.tensor_tensor(ci[:, :], base, before, ALU.add))
                dve.sem_inc(off_used, 1)
                link(dve.tensor_copy(wbi[:, kw], base.rearrange("p (n b) -> p n b", b=B)[:, :, 0]))
                link(dve.tensor_scalar(wbi[:, kw], wbi[:, kw], 7, None, ALU.logical_shift_right))
                link(dve.tensor_scalar(ci2[:, :], ci[:, :], 7, None, ALU.logical_shift_right))
                link(dve.tensor_tensor(wl[:, ks].rearrange("p (n b) -> p n b", b=B), ci2[:, :].rearrange("p (n b) -> p n b", b=B),
                                       bc(wbi[:, kw], [P, CH // B, B]), ALU.subtract))
                link(dve.tensor_scalar(ci[:, :], ci[:, :], P - 1, None, ALU.bitwise_and))
                link(dve.tensor_copy(qq[:, ks], ci[:, :]))
            link(dve.tensor_scalar(small[:, 0:1], vcount[:, :], float(W * P), 1.0, ALU.is_gt, ALU.add))
            for k in range(2, BLOCKS):
                link(dve.scalar_tensor_tensor(small[:, k - 1:k], vcount[:, :], float(k * W * P), small[:, k - 2:k - 1], ALU.is_gt, ALU.add))
            link(dve.tensor_copy(bcount[:, :], small[:, BLOCKS - 2:BLOCKS - 1]))
            dve.sem_inc(windows_ready, 1)

            def onehots(n, slot):
                cols = bass.ds(n * (G * B), G * B) if not isinstance(n, int) else slice(n * G * B, (n + 1) * G * B)
                qv = qq[:, cols].rearrange("p (g b) -> p g b", g=G).unsqueeze(2).to_broadcast([P, G, P, B])
                wv = wl[:, cols].rearrange("p (g b) -> p g b", g=G).unsqueeze(2).to_broadcast([P, G, WB, B])
                dve.tensor_tensor(ohq[:, slot], rep.unsqueeze(1).to_broadcast([P, G, P, B]), qv, ALU.is_equal)
                dve.tensor_tensor(woh[:, slot], rep[:, 0:WB, :].unsqueeze(1).to_broadcast([P, G, WB, B]), wv, ALU.is_equal).then_inc(win_oh, 1)
                dve.wait_ge(win_oh, n + 1)
                for g in range(G):
                    cg = bass.ds(n * (G * B) + g * B, B) if not isinstance(n, int) else slice(n * G * B + g * B, n * G * B + g * B + B)
                    ins = dve.tensor_tensor(rhs[:, slot, g], woh[:, slot, g].unsqueeze(1).to_broadcast([P, 4, WB, B]),
                                            pcs[:, :, cg].unsqueeze(2).to_broadcast([P, 4, WB, B]), ALU.mult)
                ins.then_inc(oh_made, 1)

            def take(n, slot):
                dve.wait_ge(moved, n + 2)
                dve.wait_ge(compacted, n * 2 + 2)
                dve.sem_inc(sorting, 1)
                dve.tensor_copy(wins[:, slot, :], ps[:, 4 + slot, 0:G * 4 * WB]).then_inc(taken, 1)

            onehots(0, 0)
            with dve.Fori(0, STEPS // 2 - 1) as i:
                for r in range(2):
                    dve.wait_ge(moved, i * 2 + (r + 1))
                    onehots(i * 2 + (r + 1), 1 - r)
                    take(i * 2 + r, r)
            dve.wait_ge(moved, STEPS - 1)
            onehots(STEPS - 1, 1)
            take(STEPS - 2, 0)
            take(STEPS - 1, 1)
            dve.wait_ge(compacted, 2 * STEPS + 4)

            dve.wait_ge(x_in, 16)
            link(dve.tensor_reduce(stats[:, 0, :], resid[:, :, :], AX.X, ALU.add))
            link(dve.tensor_scalar(stats[:, 0, :], stats[:, 0, :], 1.0 / P, None, ALU.mult))
            dve.sem_inc(mean_ready, 1)

            link(dve.memset(ones_b, 1.0))
            nb = dve.value_load(bcount[0:1, 0:1], min_val=1, max_val=BLOCKS)

            def sources(i):
                cb = bass.ds(i * W, W)
                return dve.scalar_tensor_tensor(lin.unsqueeze(1), ca[:, 2:3, cb], 128.0, ca[:, 3:4, cb], ALU.mult, ALU.add)

            def real_buckets(i):
                return dve.scalar_tensor_tensor(keyr.unsqueeze(1), lin.unsqueeze(1), float(N - 1), ca[:, 0:1, bass.ds(i * W, W)],
                                                ALU.is_lt, ALU.mult)

            with dve.Fori(0, nb) as i:
                sources(i).then_inc(blk_c, 1)
                dve.wait_ge(blk_c, i * 3 + 1)
                real_buckets(i).then_inc(blk_c, 1)
                dve.wait_ge(blk_c, i * 3 + 2)
                dve.tensor_tensor(keyc.unsqueeze(1), ca[:, 0:1, bass.ds(i * W, W)], keyr.unsqueeze(1), ALU.subtract).then_inc(blk_c, 1)
                dve.wait_ge(blk_c, i * 3 + 3)
                dve.sem_inc(sorting, 1)
                with dve.Fori(0, CSTEPS // 2) as j:
                    for r in range(2):
                        n = j * (2 * G * B) + r * G * B
                        dve.wait_ge(clamped, i * CSTEPS + (j * 2 + (r + 1)))
                        dv = ca[:, 1, bass.ds(i * W + n, G * B)].rearrange("p (g b) -> p g b", g=G).unsqueeze(2).to_broadcast([P, G, P, B])
                        kv = keyc[:, bass.ds(n, G * B)].rearrange("p (g b) -> p g b", g=G).unsqueeze(2).to_broadcast([P, G, T, B])
                        dve.tensor_tensor(ohq[:, r], rep.unsqueeze(1).to_broadcast([P, G, P, B]), dv, ALU.is_equal)
                        dve.tensor_tensor(coh[:, r], rep[:, 1:T + 1, :].unsqueeze(1).to_broadcast([P, G, T, B]), kv, ALU.is_equal).then_inc(coh_made, 1)
            dve.wait_ge(nclamp_ready, 1)
            link(dve.tensor_copy(nclamp[:, :], ps[:, 6, 0:T]))
            dve.sem_inc(nclamp_ready, 1)

            dve.wait_ge(x_in, 16)
            dve.wait_ge(small_in, 16 * SMALL)
            dve.wait_ge(squared, T)
            nvar[0] += 1
            dve.tensor_scalar(stats[:, 1, :], stats[:, 1, :], 1.0 / P, EPS, ALU.mult, ALU.add).then_inc(var_ready, 1)
            dve.wait_ge(row_summed, 2 * T)
            link(dve.tensor_tensor(dinv[:, :], deg2[:, :, 0], deg2[:, :, 1], ALU.add))
            link(dve.tensor_scalar(dinv[:, :], dinv[:, :], 1.0, None, ALU.add))
            link(dve.tensor_scalar(dmask[:, :], dinv[:, :], 0.0, None, ALU.is_gt))
            nvar[0] += 1
            dve.tensor_scalar(dinv[:, :], dinv[:, :], 1e-30, None, ALU.max).then_inc(var_ready, 1)
            dve.wait_ge(std_ready, nvar[0])
            link(dve.reciprocal(stats[:, 1, :], stats[:, 1, :]))
            link(dve.reciprocal(dinv[:, :], dinv[:, :]))
            link(dve.tensor_tensor(dinv[:, :], dinv[:, :], dmask[:, :], ALU.mult))
            link(dve.tensor_tensor(stats[:, 1, :], stats[:, 1, :], dinv[:, :], ALU.mult))
            dve.tensor_tensor(featp, featp, bc(stats[:, 1, :], [P, T, P]), ALU.mult).then_inc(feats0, 1)
            link(dve.tensor_tensor(resid[:, :, :], resid[:, :, :], bc(bias0, [P, T, P], 1), ALU.add))


            with dve.Fori(0, nb) as i:
                sources(i).then_inc(cnt_c, 1)
                dve.wait_ge(cnt_c, i * 3 + 1)
                real_buckets(i).then_inc(cnt_c, 1)
                dve.wait_ge(cnt_c, i * 3 + 2)
                dve.sem_inc(sorting, 1)
                with dve.Fori(0, T) as b:
                    dve.tensor_scalar(mk, keyr, iota[:, bass.ds(b + 1, 1)], 0.0, ALU.is_equal, ALU.add,
                                      accum_out=cnt1[:, bass.ds(b, 1)]).then_inc(counts, 1)
                    dve.wait_ge(counts, i * T + (b + 1))
                dve.tensor_tensor(cnt[:, :], cnt[:, :], cnt1[:, :], ALU.add).then_inc(cnt_c, 1)
                dve.wait_ge(cnt_c, i * 3 + 3)
            dve.sem_inc(counted, 1)
            dve.wait_ge(offs, 1)
            link(dve.tensor_copy(cnt[:, :], ps[:, 4, 0:T]))
            link(dve.tensor_copy(cnt1[:, :], ps[:, 5, 0:T]))
            dve.sem_inc(offs_taken, 1)
            link(dve.tensor_scalar(ngi[:, :], cnt1[:, :], 1.0 / GE, None, ALU.mult))
            link(dve.tensor_copy(gend[:, :], ngi[:, :]))
            link(dve.scalar_tensor_tensor(ngf[:, :], gend[:, :], float(GE), cnt1[:, :], ALU.mult, ALU.is_lt))
            link(dve.tensor_tensor(ngf[:, :], ngf[:, :], gend[:, :], ALU.add))
            link(dve.tensor_scalar(ngf[:, :], ngf[:, :], 1.0, None, ALU.max))
            link(dve.tensor_tensor_scan(gend[:, :], ones_b[:, 0:T], ngf[:, :], 0.0, ALU.mult, ALU.add))
            link(dve.tensor_tensor(cur[:, :], gend[:, :], ngf[:, :], ALU.subtract))
            link(dve.tensor_scalar(cur[:, :], cur[:, :], float(GE), -1.0, ALU.mult, ALU.add))
            link(dve.tensor_tensor(cur[:, :], cur[:, :], cnt[:, :], ALU.add))
            link(dve.tensor_scalar(gcount[:, :], gend[:, T - 1:T], float(GR - 1), None, ALU.add))
            link(dve.tensor_scalar(gcount[:, :], gcount[:, :], GR.bit_length() - 1, None, ALU.logical_shift_right))
            K = NGP // P
            link(dve.tensor_tensor(gcv, bc(gid[:, :], [P, K, T]), bc(gend[:, :], [P, K, T], 1), ALU.is_ge))
            link(dve.tensor_reduce(gbf[:, :], gcv, AX.X, ALU.add))
            dve.tensor_scalar(gbi[:, :], gbf[:, :], float(T - 1), None, ALU.min).then_inc(gbi_ready, 1)

            for k in range(NB):
                dve.wait_ge(lin_ready, k + 1)
                kb = (k % 2) * 4
                for t in range(TB):
                    g = k * TB + t
                    ins = dve.scalar_tensor_tensor(resid[:, g, :], ps[:, kb + t // 4, (t % 4) * P:(t % 4 + 1) * P],
                                                   dinv[:, g:g + 1], resid[:, g, :], ALU.mult, ALU.add)
                ins.then_inc(x1_ready, 1)
                if k:
                    dve.wait_ge(x1_ready, k + 1)
                if k == 1:
                    centre(0, 0)
                    centre(0, 1)
                    twice_normal(0)
                    twice_normal(1)
                if k > 1:
                    centre(0, k)
                    twice_normal(k)
                if k:
                    continue
                dve.sem_inc(blk_scattered, 1)
                with dve.Fori(0, nb) as i:
                    dve.wait_ge(blk_scattered, i + 1)
                    sources(i).then_inc(rank_c, 1)
                    dve.wait_ge(rank_c, i * (2 * T + 4) + 1)
                    real_buckets(i).then_inc(rank_c, 1)
                    dve.wait_ge(rank_c, i * (2 * T + 4) + 2)
                    dve.scalar_tensor_tensor(pay.unsqueeze(1), lin.unsqueeze(1), 256.0, ca[:, 1:2, bass.ds(i * W, W)], ALU.mult, ALU.add).then_inc(rank_c, 1)
                    dve.wait_ge(rank_c, i * (2 * T + 4) + 3)
                    dve.memset(pos, 1 << 30).then_inc(rank_c, 1)
                    dve.wait_ge(rank_c, i * (2 * T + 4) + 4)
                    dve.sem_inc(sorting, 1)
                    with dve.Fori(0, T) as b:
                        dve.tensor_scalar(mk, keyr, iota[:, bass.ds(b + 1, 1)], None, ALU.is_equal).then_inc(rank_c, 1)
                        dve.wait_ge(rank_c, i * (2 * T + 4) + (b * 2 + 5))
                        dve.tensor_tensor_scan(sc, ones_b, mk, cur[:, bass.ds(b, 1)], ALU.mult, ALU.add).then_inc(rank_c, 1)
                        dve.wait_ge(rank_c, i * (2 * T + 4) + (b * 2 + 6))
                        dve.tensor_scalar(cur[:, bass.ds(b, 1)], sc[:, W - 1:W], 0.0, None, ALU.add)
                        dve.copy_predicated(pos, mk.bitcast(U16), sc).then_inc(cur_moved, 1)
                        dve.wait_ge(cur_moved, i * T + (b + 1))
                    dve.sem_inc(pos_ready, 1)

            dve.wait_ge(x1_ready, NB)
            dve.wait_ge(w1_in, 32)
            dve.wait_ge(b1_done, 1)
            link(dve.tensor_tensor(b1a[:, :], b1a[:, :], ps[:, 7, 0:E0 * C0], ALU.add))
            dve.tensor_tensor(w1av, w1av, bc(lngb[:, 0, :], [P, E0, H0]), ALU.mult).then_inc(wa_ready, 1)
            dve.wait_ge(lg_ready, 1)
            link(dve.tensor_tensor(lgt, ps[:, 2, 0:T * E0].rearrange("p (t e) -> p t e", t=T), bc(stats[:, 0, :], [P, T, E0]), ALU.mult))
            link(dve.tensor_tensor(lgt, lgt, bc(brr, [P, T, E0], 1), ALU.add))
            best(lgt, 1)

            def combine(E, base_y, base_b, lo=0, hi=NBLK):
                with dve.Fori(lo, hi) as i:
                    link.enter(i, 1, lo)
                    bt = bass.ds(i * SB4, SB4)
                    dve.tensor_scalar(gst[:, :, :], gates[:, bt, :], 0.0, None, ALU.add).then_inc(gst_ready, 1)
                    for e in range(E):
                        dve.wait_ge(y_ready, i * E + (base_y + e + 3))
                        for t in range(SB4):
                            g = bass.ds(i * SB4 + t, 1)
                            ins = dve.scalar_tensor_tensor(resid[:, g, :], ps[:, 4 + e % 2, t * P:(t + 1) * P].unsqueeze(1),
                                                           gates[:, g, e], resid[:, g, :], ALU.mult, ALU.add)
                        ins.then_inc(y_added, 1)
                        dve.wait_ge(y_added, i * E + (base_y + e + 3))
                    dve.wait_ge(bt_ready, i + (base_b + 1))
                    link(dve.tensor_tensor(resid[:, bt, :], resid[:, bt, :],
                                           ps[:, 7, :].rearrange("p (t f) -> p t f", t=SB4), ALU.add))
                    link.leave(hi - lo, lo)

            dve.sem_inc(y_added, 2)
            for c in range(NB):
                b = c * NBLK // NB
                if c == 0:
                    combine(E0, 0, 0, 0, NBLK // NB)
                else:
                    combine(E0, 0, 0, b, b + 1)
                    variance(1, c - 1)
                    combine(E0, 0, 0, b + 1, b + 3)
                    scale(1, c - 1)
                    combine(E0, 0, 0, b + 3, b + NBLK // NB)
                centre(1, c)

            dve.wait_ge(wext_done, 1)
            link(dve.tensor_copy(wext[:, P:P + 2], ps[:, 6, 0:2]))
            dve.sem_inc(wext_ready, 1)
            link(dve.memset(feath[:, :, P:P + 1], 1.0))
            variance(1, NB - 1)
            scale(1, NB - 1)
            tmpw = wts[:, 0, 0:2 * HF].rearrange("p (s h e) -> p s h e", s=2, h=HEADS)
            wv = wgat[:, 0:HF].rearrange("p (h e) -> p h e", h=HEADS)
            for s in range(2):
                link(dve.tensor_tensor(tmpw[:, s], wv, attr[:, s], ALU.mult))
                link(dve.tensor_reduce(wgat[:, HF + s * HEADS:HF + (s + 1) * HEADS], tmpw[:, s], AX.X, ALU.add))
            dve.sem_inc(wgat_done, 1)
            dve.wait_ge(hx_copied, NBLK + 2)
            dve.tensor_reduce(small[:, 0:2], asd[:, :, :], AX.X, ALU.max).then_inc(mx_ready, 1)
            dve.wait_ge(mxt_ready, 1)
            link(dve.tensor_reduce(small[0:2, 4:5], ps[0:2, 2, 0:P], AX.X, ALU.max))
            dve.tensor_scalar(small[0:2, 8:10], ident[0:2, 0:2], small[0:2, 4:5], None, ALU.mult).then_inc(mxd_ready, 1)
            dve.wait_ge(mxb_ready, 1)
            link(dve.tensor_copy(small[:, 2:4], ps[:, 3, 0:2]))
            low, high, low8, low2, nhigh = [small[:, c:c + 1] for c in (5, 6, 7, 10, 11)]
            link(dve.tensor_tensor(low, small[:, 2:3], small[:, 3:4], ALU.add))
            link(dve.tensor_scalar(low, low, 64.0, None, ALU.is_le))
            link(dve.tensor_copy(low_i[:, :], low))
            link(dve.tensor_scalar(high, low, -1.0, 1.0, ALU.mult, ALU.add))
            link(dve.tensor_scalar(nhigh, high, -1.0, None, ALU.mult))
            link(dve.tensor_scalar(low8, low, 0.8, None, ALU.mult))
            link(dve.tensor_scalar(low2, low, -0.2, None, ALU.mult))
            link(dve.tensor_scalar(fac[:, 0, :], asd[:, 0, :], small[:, 2:3], None, ALU.subtract))
            link(dve.tensor_scalar(fac[:, 1, :], fac[:, 0, :], 0.2, None, ALU.mult))
            link(dve.tensor_scalar(asd[:, 1, :], asd[:, 1, :], small[:, 2:3], None, ALU.add))
            link(dve.tensor_scalar(asd[:, 0, :], asd[:, 1, :], 0.0, None, ALU.max))
            link(dve.tensor_scalar(fac[:, 2, :], asd[:, 1, :], 0.0, None, ALU.min))
            link(dve.tensor_scalar(fac[:, 2, :], fac[:, 2, :], high, None, ALU.mult))
            link(dve.scalar_tensor_tensor(fac[:, 2, :], asd[:, 1, :], low8, fac[:, 2, :], ALU.mult, ALU.add))
            link(dve.scalar_tensor_tensor(fac[:, 3, :], asd[:, 1, :], 0.2, asd[:, 0, :], ALU.mult, ALU.subtract))
            link(dve.tensor_scalar(fac[:, 4, :], asd[:, 0, :], nhigh, None, ALU.mult))
            link(dve.scalar_tensor_tensor(fac[:, 4, :], asd[:, 1, :], low2, fac[:, 4, :], ALU.mult, ALU.add))
            link(dve.tensor_scalar(fac[:, 4, :], fac[:, 4, :], 60.0, None, ALU.min))
            dve.sem_inc(fac_in, 1)
            dve.wait_ge(fac_ready, 1)
            link(dve.tensor_scalar(fac[:, 4, :], fac[:, 4, :], 1e-8, None, ALU.mult))
            dve.wait_ge(qt_ready, 1)
            dve.tensor_copy(qst, ps[:, 4, 0:P]).then_inc(qs_ready, 1)
            is_low = dve.to_reg(dve.value_load(low_i[0:1, 0:1], min_val=0, max_val=1))

            dve.sem_inc(e_ready, 2)
            dve.wait_ge(scattered, 1)
            TURN = NS6
            for k in range(NB):
                dve.wait_ge(q_in, 16 * (k + 1))

                def masked(n, loaded, r, s):
                    dve.wait_ge(a6_in[r], loaded)
                    dve.sem_inc(sorting, 1)
                    dve.scalar_tensor_tensor(at6[r], at6[r], 0.0, prod[s], ALU.is_gt, ALU.mult).then_inc(e_ready, 1)

                def fast(n, s, j):
                    dve.tensor_scalar(prod[s], qb[:, 0, :], fac[:, 0, j], fac[:, 1, j], ALU.mult, ALU.max).then_inc(p_ready, 1)

                def general(n, s, j):
                    dve.tensor_scalar(prod[s], qb[:, 0, :], fac[:, 0, j], None, ALU.mult).then_inc(vpos, 1)
                    dve.wait_ge(vpos, n + 1)
                    dve.scalar_tensor_tensor(prod[s], qb[:, 1, :], fac[:, 1, j], prod[s], ALU.mult, ALU.max).then_inc(p_ready, 1)

                def block(make, lo, hi):
                    def pair(n0, trip, m):
                        n = trip * TURN + n0
                        for s in range(2):
                            dve.wait_ge(e_ready, n + (s + 1))
                            make(n + s, s, bass.ds(trip * TURN + (m + s), 1))
                        for s in range(2):
                            dve.wait_ge(p_ready, n + (s + 1))
                            masked(n + s, trip * 16 + 16 * ((n0 + s) // NS6 + 1), (n0 + s) % NS6, s)

                    with dve.Fori(lo, hi) as i:
                        for m in range(0, TURN, 2):
                            pair(k * T + m, i, m)

                def turns(lo, hi):
                    with dve.If_ne(is_low, 0):
                        block(fast, lo, hi)
                    with dve.If_eq(is_low, 0):
                        block(general, lo, hi)

                steps = T // TURN
                if k == 0:
                    turns(0, steps)
                else:
                    turns(0, steps // 2)
                    dve.wait_ge(block_done, k)
                    centre(2, k - 1)
                    turns(steps // 2, steps * 3 // 4)
                    variance(2, k - 1)
                    turns(steps * 3 // 4, steps - 1)
                    scale(2, k - 1)
                    turns(steps - 1, steps)
                dve.wait_ge(att_ready, k + 1)
                for b, m in ((0, 5), (5, 1)):
                    w = 3 if m > 1 else 1
                    den = ps[:, b:b + m, 0:w * 129].rearrange("p b (t f) -> p b t f", f=129)[:, :, :, P]
                    ts = slice(3 * b, 3 * b + m * w)
                    link(dve.tensor_tensor(rden[:, ts].rearrange("p (b t) -> p b t", b=m), den,
                                           fac[:, 4, k * TB + 3 * b:k * TB + 3 * b + m * w].rearrange("p (b t) -> p b t", b=m), ALU.add))
                link(dve.reciprocal(rden[:, 0:TB], rden[:, 0:TB]))
                quot = quots[k]
                for b in range(6):
                    w = min(3, TB - 3 * b)
                    accv = ps[:, b, 0:w * 129].rearrange("p (t f) -> p t f", t=w)
                    ts = slice(3 * b, 3 * b + w)
                    ins = dve.tensor_tensor(quot[:, ts, :], accv[:, :, 0:P], bc(rden[:, ts], [P, w, P]), ALU.mult)
                ins.then_inc(eneg, 1)

            quot, qneg = quots[NB - 1], qnegs[NB - 1]
            dve.wait_ge(eneg, NB)
            dve.tensor_scalar(qneg, quot, 0.0, None, ALU.min).then_inc(neg_ready, 1)
            dve.wait_ge(neg_ready, NB)
            rs = resid[:, (NB - 1) * TB:NB * TB, :]
            link(dve.tensor_scalar(quot, quot, 0.0, -1.0, ALU.max, ALU.add))
            link(dve.tensor_tensor(rs, rs, quot, ALU.add))
            dve.wait_ge(x3_ready, NB)
            link(dve.tensor_tensor(rs, rs, qneg, ALU.add))

            centre(2, NB - 1)
            variance(2, NB - 1)
            scale(2, NB - 1)
            dve.wait_ge(gat_copied, NBLK + 2)
            dve.sem_inc(ntab_ready, 1)
            dve.tensor_reduce(small[:, 0:HEADS], ntab[:, :, HF:TW].rearrange("p t h -> p h t"), AX.X, ALU.max).then_inc(emx, 1)
            dve.wait_ge(emxt, 1)
            link(dve.tensor_reduce(small[0:HEADS, 4:5], ps[0:HEADS, 2, 0:P], AX.X, ALU.max))
            dve.tensor_scalar(small[0:HEADS, 8:8 + HEADS], ident[0:HEADS, 0:HEADS], small[0:HEADS, 4:5], None, ALU.mult).then_inc(emxd, 1)
            dve.wait_ge(emxb, 1)
            link(dve.tensor_copy(small[:, 12:16], ps[:, 3, 0:HEADS]))
            link(dve.tensor_copy(dtab[:, :, 0:HEADS], ntab[:, :, TW:TW + HEADS]))
            link(dve.tensor_tensor(ee[:, 0], ntab[:, :, TW:TW + HEADS], bc(small[:, 12:16], [P, T, HEADS], 1), ALU.add))
            link(dve.scalar_tensor_tensor(dtab[:, :, HEADS:2 * HEADS], ee[:, 0], 0.2, ee[:, 0], ALU.mult, ALU.max))
            link(dve.tensor_tensor(ee[:, 0], ntab[:, :, HF:TW], ntab[:, :, TW:TW + HEADS], ALU.add))
            dve.wait_ge(last_in, 16)
            link(dve.tensor_tensor(ee[:, 1], bc(last[:, HF:TW], [P, T, HEADS], 1), ntab[:, :, TW:TW + HEADS], ALU.add))
            for s in range(2):
                link(dve.scalar_tensor_tensor(ee[:, s], ee[:, s], 0.2, ee[:, s], ALU.mult, ALU.max))
                link(dve.tensor_tensor(ee[:, s], ee[:, s], dtab[:, :, HEADS:2 * HEADS], ALU.subtract))
            dve.sem_inc(self_in, 1)
            dve.wait_ge(self_exp, 1)
            link(dve.tensor_tensor(ee[:, 1], ee[:, 1], bc(nclamp[:, :], [P, T, HEADS]), ALU.mult))
            link(dve.tensor_tensor(acc[:, :, HF:TW], ee[:, 0], ee[:, 1], ALU.add))
            for h in range(HEADS):
                hs = slice(h * EX, (h + 1) * EX)
                link(dve.tensor_tensor(acc[:, :, hs], ntab[:, :, hs], ee[:, 0, :, h:h + 1].to_broadcast([P, T, EX]), ALU.mult))
                link(dve.tensor_tensor(ag[:, :, hs], bc(last[:, hs], [P, T, EX], 1), ee[:, 1, :, h:h + 1].to_broadcast([P, T, EX]), ALU.mult))
            link(dve.tensor_tensor(acc[:, :, 0:HF], acc[:, :, 0:HF], ag, ALU.add))
            link(dve.memset(gb[0:1, 0:1], 0))
            dve.sem_inc(vals_ready, GR)
            dve.wait_ge(gb_in, 16)
            trips = dve.value_load(gcount[0:1, 0:1], min_val=1, max_val=GTRIPS)

            def unpack(r, loaded, k):
                dve.wait_ge(pt_in[r], loaded)
                dve.tensor_scalar(srci[:, r, :], pt[:, r, :], 8, None, ALU.logical_shift_right)
                dve.tensor_scalar(dli[:, r, :], pt[:, r, :], 255, None, ALU.bitwise_and).then_inc(unpacked, 1)
                dve.wait_ge(unpacked, k + 1)
                dve.tensor_copy(dlf[:, r, :], dli[:, r, :]).then_inc(grp_c, 1)

            def onehot(s):
                dve.tensor_tensor(oh[:, s, :, :], bc(iota[:, :], [P, GRP, P], 1), bc(dlf[:, s, :], [P, GRP, P]),
                                  ALU.is_equal).then_inc(oh_ready, 1)

            def last_bucket(g):
                return dve.value_load(gb[0:1, bass.ds(g, 1)], min_val=0, max_val=T - 1)

            def take_sum(bk, g, slot, done):
                dve.wait_ge(sum_ready, g + 2)
                dve.tensor_tensor(acc[:, bass.ds(bk, 1), :], acc[:, bass.ds(bk, 1), :],
                                  ps[:, 6 + slot, 0:TW].unsqueeze(1), ALU.add).then_inc(grp_c, 1)
                dve.wait_ge(grp_c, done)

            for g in range(GR - 1):
                unpack(g, 16, g)
            dve.wait_ge(grp_c, GR - 1)
            dve.wait_ge(sum_ready, 2)
            onehot(0)
            with dve.Fori(0, trips) as i:
                for m in range(GR):
                    r = m % 2
                    k = i * (5 * GR) + (5 * m + GR - 1)
                    unpack((m + GR - 1) % GR, i * 16 + 16 * ((m + GR - 1) // GR + 1), i * GR + (m + GR - 1))
                    onehot((m + 1) % GR)
                    bk = last_bucket(i * GR + m)
                    dve.wait_ge(gathered[m], (i + 1) * 16 * GRP)
                    dve.wait_ge(dst_ready, i * GR + (m + 1))
                    pd = ps[:, 4 + r, 0:GRP * 8].rearrange("p (c k) -> p c k", k=8)
                    dve.tensor_tensor(zt, gt[:, m, :, HF:TW], pd[:, :, 0:HEADS], ALU.add).then_inc(grp_c, 1)
                    dve.wait_ge(grp_c, k + 2)
                    dve.scalar_tensor_tensor(zt, zt, 0.2, zt, ALU.mult, ALU.max).then_inc(grp_c, 1)
                    dve.wait_ge(grp_c, k + 3)
                    dve.tensor_tensor(zt, zt, pd[:, :, HEADS:2 * HEADS], ALU.subtract).then_inc(grp_c, 1)
                    dve.wait_ge(grp_c, k + 4)
                    dve.tensor_scalar(zt, zt, 0.0, None, ALU.min).then_inc(z_ready, 1)
                    take_sum(bk, i * GR + m, 1 - r, k + 5)
                    dve.wait_ge(ez_ready, i * GR + (m + 1))
                    dve.tensor_tensor(vals[:, r, :, 0:HF].rearrange("p c (h e) -> p c h e", h=HEADS),
                                      gt[:, m, :, 0:HF].rearrange("p c (h e) -> p c h e", h=HEADS),
                                      vals[:, r, :, HF:TW].unsqueeze(3).to_broadcast([P, GRP, HEADS, EX]),
                                      ALU.mult).then_inc(vals_ready, 1)
            take_sum(last_bucket(trips * GR), trips * GR, 1, trips * (5 * GR) + GR)

            link(dve.tensor_scalar(ee[:, 0], acc[:, :, HF:TW], 1e-16, None, ALU.add))
            link(dve.reciprocal(ee[:, 0], ee[:, 0]))
            for h in range(HEADS):
                link(dve.tensor_tensor(ag[:, :, h * EX:(h + 1) * EX], acc[:, :, h * EX:(h + 1) * EX],
                                       ee[:, 0, :, h:h + 1].to_broadcast([P, T, EX]), ALU.mult))
            link(dve.tensor_tensor(ag, ag, bc(bgat, [P, T, HF], 1), ALU.add))
            link(dve.tensor_reduce(lst[:, 0, :], ag, AX.X, ALU.add))
            link(dve.tensor_scalar(lst[:, 0, :], lst[:, 0, :], 1.0 / HF, None, ALU.mult))
            link(dve.tensor_tensor(ag, ag, bc(lst[:, 0, :], [P, T, HF]), ALU.subtract))
            link(dve.tensor_tensor(ag2, ag, ag, ALU.mult))
            link(dve.tensor_reduce(lst[:, 1, :], ag2, AX.X, ALU.add))
            nvar[0] += 1
            dve.tensor_scalar(lst[:, 1, :], lst[:, 1, :], 1.0 / HF, EPS, ALU.mult, ALU.add).then_inc(var_ready, 1)
            dve.wait_ge(std_ready, nvar[0])
            link(dve.reciprocal(lst[:, 1, :], lst[:, 1, :]))
            link(dve.tensor_tensor(ag, ag, bc(lst[:, 1, :], [P, T, HF]), ALU.mult))
            link(dve.tensor_tensor(ag, ag, bc(gam, [P, T, HF], 1), ALU.mult))
            link(dve.tensor_tensor(ag, ag, bc(bet, [P, T, HF], 1), ALU.add))
            link(dve.memset(lg8, -3e38))
            link(dve.tensor_reduce(lg8[:, :, 0:EX], ag.rearrange("p t (h e) -> p t e h", h=HEADS), AX.X, ALU.add))
            link(dve.tensor_scalar(lg8[:, :, 0:EX], lg8[:, :, 0:EX], 1.0 / HEADS, None, ALU.mult))
            best(lg8, 2)
            combine(E1, NBLK * E0, NBLK)
            dve.sem_inc(out_ready, 1)

        @block.tensor
        def _(pe):
            def clear(bank, n=BANK):
                return pe.matmul(ps[:, bank, 0:n], zeros_b[:, 0:P], zeros_b[:, 0:n], start=True, stop=False,
                                 skip_group_check=True)

            def close(bank, n=BANK):
                return pe.matmul(ps[:, bank, 0:n], zeros_b[:, 0:P], zeros_b[:, 0:n], start=False, stop=True,
                                 skip_group_check=True)

            pe.wait_ge(const, 7)
            pe.wait_ge(tables_ready, 1)
            pe.wait_ge(valid_ready, 1)
            for k in range(EC // CH):
                ks = slice(k * CH, (k + 1) * CH)
                if k >= 2:
                    pe.wait_ge(off_used, k - 1)
                pe.matmul(ps[:, k % 2, :], lt_b, valid[:, ks], start=True, stop=True)
                pe.matmul(ps[:, 2 + k % 2, :], on_b, valid[:, ks], start=True, stop=True).then_inc(off_ready, 1)
            pe.sem_inc(taken, 2)
            pe.sem_inc(moved, 1)
            with pe.Fori(0, STEPS // 2) as i:
                for r in range(2):
                    pe.wait_ge(oh_made, i * 2 + (r + 1))
                    pe.wait_ge(taken, i * 2 + (r + 1))
                    for g in range(G):
                        for b in range(B):
                            ins = pe.matmul(ps[:, 4 + r, g * 4 * WB:(g + 1) * 4 * WB], ohq[:, r, g, :, b],
                                            rhs[:, r, g, :, :, b].rearrange("p k w -> p (k w)"), start=(b == 0), stop=(b == B - 1))
                    ins.then_inc(moved, 1)
            clear(6, T)
            pe.sem_inc(clamped, 2)
            pe.wait_ge(coh_made, 1)
            nb = pe.value_load(bcount[0:1, 0:1], min_val=1, max_val=BLOCKS)
            with pe.Fori(0, nb) as i:
                with pe.Fori(0, CSTEPS // 2) as j:
                    for r in range(2):
                        pe.wait_ge(coh_made, i * CSTEPS + (j * 2 + (r + 1)))
                        for g in range(G):
                            for b in range(B):
                                ins = pe.matmul(ps[:, 6, 0:T], ohq[:, r, g, :, b], coh[:, r, g, :, b], start=False, stop=False,
                                                skip_group_check=True)
                        ins.then_inc(clamped, 1)
            close(6, T).then_inc(nclamp_ready, 1)
            pe.wait_ge(nclamp_ready, 2)

            pe.wait_ge(feats0, 1)
            pe.sem_inc(tile_used, NS2)
            pe.wait_ge(small_in, 16 * SMALL)
            for k in range(NB):
                kb = (k % 2) * 4
                if k >= 2:
                    pe.wait_ge(x1_ready, k - 1)
                if k == 1:
                    pe.wait_ge(counted, 1)
                    pe.matmul(ps[:, 4, 0:T], lower[:, :], cnt[:, :], start=True, stop=True)
                    pe.matmul(ps[:, 5, 0:T], ones[:, :], cnt[:, :], start=True, stop=True).then_inc(offs, 1)
                    pe.wait_ge(offs_taken, 1)
                for b in range(4):
                    clear(kb + b)
                with pe.Fori(0, T // NS2) as i:
                    for r in range(NS2):
                        pe.wait_ge(at_in[r], i * 16 + (k * (T // NS2) * 16 + 16))
                        pe.wait_ge(staged_x, i * NS2 + (k * T + r + 1))
                        for b in range(4):
                            ins = pe.matmul(ps[:, kb + b, :], xs[:, r, :], at2[r][:, b * BANK:(b + 1) * BANK],
                                            start=False, stop=False, skip_group_check=True)
                        ins.then_inc(tile_used, 1)
                for t in range(TB):
                    pe.matmul(ps[:, kb + t // 4, (t % 4) * P:(t % 4 + 1) * P], featp[:, k * TB + t, :], ident[:, :],
                              start=False, stop=False, skip_group_check=True)
                for b in range(4):
                    ins = close(kb + b)
                ins.then_inc(agg_ready, 1)
                pe.wait_ge(agg_copied, 4 * (k + 1))
                for t in range(TB):
                    ins = pe.matmul(ps[:, kb + t // 4, (t % 4) * P:(t % 4 + 1) * P], agg[:, t * P:(t + 1) * P],
                                    w0t[:, :], start=True, stop=True)
                ins.then_inc(lin_ready, 1)

            def transposes(g, product):
                for i in range(NBLK // 2):
                    for r in range(2):
                        n = 2 * i + r
                        pe.wait_ge(ln_ready, g * NBLK + n + 1)
                        for t in range(SB4):
                            ins = pe.transpose(ps[:, r, t * P:(t + 1) * P], un[:, n * SB4 + t, :], ident[:, :])
                        ins.then_inc(tr_ready, 1)
                    for r in range(2):
                        pe.wait_ge(tr_copied, g * NBLK + 2 * i + r + 1)
                        product(2 * i + r, r)

            def logits(n, r):
                for t in range(SB4):
                    c = (n * SB4 + t) * E0
                    ins = pe.matmul(ps[:, 2, c:c + E0], uT[r][:, t * P:(t + 1) * P], wr[:, :], start=True, stop=True)
                if n == NBLK - 1:
                    ins.then_inc(lg_ready, 1)

            pe.wait_ge(x1_ready, NB - 1)
            transposes(0, logits)
            pe.wait_ge(w1_in, 32)
            for e in range(E0):
                for h in range(C0):
                    ins = pe.matmul(ps[:, 7, e * C0 + h:e * C0 + h + 1], w1av[:, e, h * P:(h + 1) * P],
                                    lngb[:, 1, e:e + 1], start=True, stop=True)
            ins.then_inc(b1_done, 1)

            def experts(E, C, w1v, w2v, b2, base_y, base_b, base_h):
                def hidden(i, e):
                    at = i * BANK
                    for h in range(C):
                        pe.wait_ge(hid_ready, i * (E * C) + (base_h + C * e + h + 1))
                        bank = h if C == 4 else h + 2 * (e % 2)
                        pe.matmul(ps[:, bank, :], w1v[:, e, h * P:(h + 1) * P],
                                  featT[:, slice(at, at + BANK) if isinstance(i, int) else bass.ds(at, BANK)],
                                  start=True, stop=True).then_inc(h_ready, 1)

                def one_block(i, last):
                    for e in range(E):
                        if e + 1 < E:
                            hidden(i, e + 1)
                        elif not last:
                            hidden(i + 1, 0)
                        pe.wait_ge(hid_ready, i * (E * C) + (base_h + C * (e + 1) + 4))
                        pe.wait_ge(y_added, i * E + (base_y + e + 1))
                        for t in range(SB4):
                            for h in range(C):
                                ins = pe.matmul(ps[:, 4 + e % 2, t * P:(t + 1) * P], hid[e % 2][:, h, t * P:(t + 1) * P],
                                                w2v[:, e, h, :], start=(h == 0), stop=(h == C - 1))
                        ins.then_inc(y_ready, 1)
                        if e == 0:
                            pe.wait_ge(gst_ready, i + (base_b + 1))
                            for t in range(SB4):
                                ins = pe.transpose(ps[0:8, 6, t * P:(t + 1) * P], gst[:, t, :], ident[:, :])
                            ins.then_inc(gt_ready, 1)
                        if e == 2:
                            pe.wait_ge(gts_ready, i + (base_b + 1))
                            for t in range(SB4):
                                ins = pe.matmul(ps[:, 7, t * P:(t + 1) * P], gts[0:E, t * P:(t + 1) * P], b2[:, :], start=True, stop=True)
                            ins.then_inc(bt_ready, 1)

                hidden(0, 0)
                with pe.Fori(0, NBLK - 1) as i:
                    one_block(i, False)
                one_block(NBLK - 1, True)

            pe.sem_inc(y_ready, 2)
            pe.wait_ge(wa_ready, 1)
            experts(E0, C0, w1av, w2av, b2a, 0, 0, 0)

            pe.wait_ge(small_in, 16 * SMALL)
            pe.matmul(ps[:, 6, 0:2], wg[:, :], att[:, :], start=True, stop=True).then_inc(wext_done, 1)
            pe.wait_ge(wext_ready, 1)

            def hidden_scores(n, r):
                pe.wait_ge(hx_copied, n + 1)
                for t in range(SB4):
                    ins = pe.matmul(ps[:, 2 + 2 * r + t // 2, (t % 2) * 256:(t % 2) * 256 + P + 2], uT[r][:, t * P:(t + 1) * P],
                                    wext[:, :], start=True, stop=True)
                ins.then_inc(hx_ready, 1)

            pe.sem_inc(hx_copied, 2)
            pe.wait_ge(y_added, NBLK * E0 + 2)
            transposes(1, hidden_scores)
            pe.wait_ge(hx_copied, NBLK + 2)
            pe.wait_ge(mx_ready, 1)
            pe.transpose(ps[0:2, 2, 0:P], small[:, 0:2], ident[:, :]).then_inc(mxt_ready, 1)
            pe.wait_ge(mxd_ready, 1)
            pe.matmul(ps[:, 3, 0:2], ones[0:2, :], small[0:2, 8:10], start=True, stop=True).then_inc(mxb_ready, 1)
            pe.wait_ge(fac_ready, 1)
            pe.transpose(ps[:, 4, 0:P], fac[:, 2:4, :].rearrange("p k t -> p (k t)"), ident[:, :]).then_inc(qt_ready, 1)
            pe.wait_ge(qs_ready, 1)

            for k in range(NB):
                if k:
                    pe.wait_ge(eneg, k)
                for b in range(6):
                    clear(b, 129 * min(3, TB - 3 * b))

                def tile6(n, r, j):
                    pe.wait_ge(e_ready, n + 3)
                    for t in range(TB):
                        ins = pe.matmul(ps[:, t // 3, (t % 3) * 129:(t % 3 + 1) * 129], at6[r][:, t * P:(t + 1) * P],
                                        feath[:, j, 0:129], start=False, stop=False, skip_group_check=True)
                    ins.then_inc(e_used, 1)

                with pe.Fori(0, T // NS6) as i:
                    for m in range(NS6):
                        tile6(i * NS6 + (k * T + m), m, bass.ds(i * NS6 + m, 1))
                for b in range(6):
                    ins = close(b, 129 * min(3, TB - 3 * b))
                ins.then_inc(att_ready, 1)

            pe.wait_ge(wgat_done, 1)

            def features(n, r):
                pe.wait_ge(gat_copied, n + 1)
                for t in range(SB4):
                    ins = pe.matmul(ps[:, 2 + r, t * 24:(t + 1) * 24], uT[r][:, t * P:(t + 1) * P], wgat[:, :], start=True, stop=True)
                ins.then_inc(gat_ready, 1)

            pe.sem_inc(gat_copied, 2)
            pe.wait_ge(eneg, NB)
            transposes(2, features)
            pe.wait_ge(gat_copied, NBLK + 2)
            pe.wait_ge(emx, 1)
            pe.transpose(ps[0:HEADS, 2, 0:P], small[:, 0:HEADS], ident[:, :]).then_inc(emxt, 1)
            pe.wait_ge(emxd, 1)
            pe.matmul(ps[:, 3, 0:HEADS], ones[0:HEADS, :], small[0:HEADS, 8:8 + HEADS], start=True, stop=True).then_inc(emxb, 1)
            pe.wait_ge(vals_ready, GR)
            pe.wait_ge(gb_in, 16)
            trips = pe.value_load(gcount[0:1, 0:1], min_val=1, max_val=GTRIPS)

            def dst_side(s, r, g, need):
                bk = pe.value_load(gb[0:1, bass.ds(g + 1, 1)] if not isinstance(g, int) else gb[0:1, g + 1:g + 2], min_val=0, max_val=T - 1)
                pe.wait_ge(oh_ready, need)
                for q in range(GRP):
                    ins = pe.transpose(ps[:, 2 * r + q // 4, (q % 4) * P:(q % 4 + 1) * P], oh[:, s, q, :], ident[:, :])
                ins.then_inc(ohp_ready, 1)
                pe.wait_ge(oht_ready, need)
                for q in range(GRP):
                    ins = pe.matmul(ps[:, 4 + r, q * 8:(q + 1) * 8], oht[:, r, q, :], dtab[:, bass.ds(bk, 1), :],
                                    start=True, stop=True)
                ins.then_inc(dst_ready, 1)

            pe.matmul(ps[:, 7, 0:TW], zeros_b[:, 0:P], zeros_b[:, 0:TW], start=True, stop=True).then_inc(sum_ready, 2)
            dst_side(0, 0, 0, 1)
            with pe.Fori(0, trips) as i:
                for m in range(GR):
                    r = m % 2
                    dst_side((m + 1) % GR, 1 - r, i * GR + (m + 1), i * GR + (m + 2))
                    pe.wait_ge(vals_ready, i * GR + (m + 1 + GR))
                    for q in range(GRP):
                        ins = pe.matmul(ps[:, 6 + r, 0:TW], oh[:, m, q, :], vals[:, r, q, :], start=(q == 0), stop=(q == GRP - 1))
                    ins.then_inc(sum_ready, 1)

            pe.wait_ge(w1b_in, 32)
            experts(E1, C1, w1bv, w2bv, b2b, NBLK * E0, NBLK, NBLK * E0 * C0)

        @block.scalar
        def _(act):
            def root(ap, n, trip=None):
                act.wait_ge(var_ready, n if trip is None else trip + n)
                act.activation(ap, ap, ACT.Sqrt).then_inc(std_ready, 1)

            with act.Fori(0, 2 * T // 6) as i:
                for k in range(6):
                    r = k % NS1
                    act.wait_ge(arow_in[r], i * 32 + (k // NS1 * 16 + 16))
                    act.activation(arow[r], arow[r], ACT.Copy,
                                   accum_out=deg2[:, bass.ds(i * 3 + k // 2, 1), k % 2]).then_inc(row_summed, 1)
            for n in range(6 * (2 * T // 6), 2 * T):
                r = n % NS1
                act.wait_ge(arow_in[r], 16 * (n // NS1 + 1))
                act.activation(arow[r], arow[r], ACT.Copy, accum_out=deg2[:, n // 2, n % 2:n % 2 + 1]).then_inc(row_summed, 1)
            act.wait_ge(x_centred, 1)
            with act.Fori(0, T) as i:
                act.activation(lnsq, featp[:, bass.ds(i, 1), :], ACT.Square, accum_out=stats[:, 1, bass.ds(i, 1)]).then_inc(squared, 1)
                act.wait_ge(squared, i + 1)
            root(stats[:, 1, :], 1)
            root(dinv[:, :], 2)
            nv = [2]

            def square(g, c):
                act.wait_ge(sub_ready, g * NB + c + 1)
                if g * NB + c:
                    act.wait_ge(sq_used, g * NB + c)
                act.activation(sqn, un[:, c * TB:(c + 1) * TB, :], ACT.Square).then_inc(sq_ready, 1)

            def roots(g, c):
                ts = slice(c * TB, (c + 1) * TB)
                nv[0] += 1
                root(stats[:, 1, ts], nv[0])
                if g == 0:
                    nv[0] += 1
                    root(stats[:, 0, ts], nv[0])

            def blocks(c, copies):
                with act.Fori(c * (TB // SB4 // 2), (c + 1) * (TB // SB4 // 2)) as i:
                    copies(i)

            act.wait_ge(feats0, 1)
            for k in range(NB):
                def stage(lo, hi):
                    with act.Fori(lo, hi) as i:
                        for r in range(NS2):
                            act.wait_ge(tile_used, i * NS2 + (k * T + r + 1))
                            act.sem_inc(slot_taken, 1)
                            act.activation(xs[:, r, :].unsqueeze(1), featp[:, bass.ds(i * NS2 + r, 1), :], ACT.Copy).then_inc(staged_x, 1)

                half = T // NS2 // 2
                stage(0, half)
                for c in {2: (0, 1), 3: (2,)}.get(k, ()):
                    square(0, c)
                    roots(0, c)
                stage(half, 2 * half)
                act.wait_ge(agg_ready, k + 1)
                kb = (k % 2) * 4
                for b in range(4):
                    act.activation(agg[:, b * BANK:(b + 1) * BANK], ps[:, kb + b, :], ACT.Copy).then_inc(agg_copied, 1)

            def to_experts(g):
                def copies(i):
                    for r in range(2):
                        act.wait_ge(tr_ready, i * 2 + (g * NBLK + r + 1))
                        act.activation(uT[r], ps[:, r, :], ACT.Copy)
                        act.activation(featT[:, bass.ds(i * (2 * BANK) + r * BANK, BANK)], ps[:, r, :], ACT.Copy).then_inc(tr_copied, 1)
                    if g:
                        for r in range(2):
                            act.wait_ge(gat_ready, i * 2 + (r + 1))
                            act.sem_inc(slot_taken, 1)
                            act.activation(ntab[:, bass.ds(i * (2 * SB4) + r * SB4, SB4), :],
                                           ps[:, 2 + r, 0:SB4 * 24].rearrange("p (t k) -> p t k", t=SB4), ACT.Copy).then_inc(gat_copied, 1)
                return copies

            def last_quarter(g, copies):
                blocks(0, copies)
                square(g, NB - 1)
                roots(g, NB - 1)
                for c in range(1, NB):
                    blocks(c, copies)

            last_quarter(0, to_experts(0))
            act.wait_ge(tops_done, 1)
            act.activation(wts[:, 0, :], wts[:, 0, :], ACT.Exp).then_inc(exp_ready, 1)

            def gelus(E, C, b1, base_y, base_b, base_h, lo=0, hi=NBLK):
                with act.Fori(lo, hi) as i:
                    for e in range(E):
                        for h in range(C):
                            act.wait_ge(h_ready, i * (E * C) + (base_h + e * C + h + 1))
                            if h == 0:
                                act.wait_ge(y_ready, i * E + (base_y + e + 1))
                            bank = h if C == 4 else h + 2 * (e % 2)
                            act.activation(hid[e % 2][:, h, :], ps[:, bank, :], ACT.Gelu,
                                           bias=b1[:, e * C + h:e * C + h + 1]).then_inc(hid_ready, 1)
                        if e == 2:
                            act.wait_ge(gt_ready, i + (base_b + 1))
                            act.activation(gts[:, :], ps[0:8, 6, :], ACT.Copy).then_inc(gts_ready, 1)

            act.sem_inc(hid_ready, 4)
            act.wait_ge(wa_ready, 1)
            for c in range(NB):
                b = c * NBLK // NB
                if c == 0:
                    gelus(E0, C0, b1a, 0, 0, 0, 0, NBLK // NB)
                else:
                    gelus(E0, C0, b1a, 0, 0, 0, b, b + 1)
                    square(1, c - 1)
                    gelus(E0, C0, b1a, 0, 0, 0, b + 1, b + 3)
                    roots(1, c - 1)
                    gelus(E0, C0, b1a, 0, 0, 0, b + 3, b + NBLK // NB)

            def to_attention(i):
                for r in range(2):
                    act.wait_ge(tr_ready, i * 2 + (NBLK + r + 1))
                    act.activation(uT[r], ps[:, r, :], ACT.Copy).then_inc(tr_copied, 1)
                for r in range(2):
                    bt = bass.ds(i * (2 * SB4) + r * SB4, SB4)
                    hv = ps[:, 2 + 2 * r:4 + 2 * r, :].rearrange("p b (t w) -> p (b t) w", t=2)
                    act.wait_ge(hx_ready, i * 2 + (r + 1))
                    act.sem_inc(slot_taken, 1)
                    act.activation(feath[:, bt, 0:P], hv[:, :, 0:P], ACT.Copy)
                    act.activation(asd[:, :, bt].rearrange("p s t -> p t s"), hv[:, :, P:P + 2], ACT.Copy).then_inc(hx_copied, 1)

            last_quarter(1, to_attention)
            act.wait_ge(fac_in, 1)
            act.activation(fac[:, :, :], fac[:, :, :], ACT.Exp).then_inc(fac_ready, 1)
            act.wait_ge(q_out, 16)
            qrows = q_d.rearrange("(k t) p -> k (t p)", k=2)

            def elu(k):
                act.wait_ge(neg_ready, k + 1)
                act.activation(qnegs[k], qnegs[k], ACT.Exp).then_inc(x3_ready, 1)

            for k in range(NB):
                if k:
                    act.wait_ge(p_ready, k * T)
                act.dma_start(qb[:, :, :], qrows[:, k * IB:(k + 1) * IB].unsqueeze(0).to_broadcast([P, 2, IB])).then_inc(q_in, 16)
                act.wait_ge(q_in, 16 * (k + 1))
                if k:
                    elu(k - 1)
                    square(2, k - 1)
                    roots(2, k - 1)
            elu(NB - 1)
            last_quarter(2, to_experts(2))
            act.wait_ge(self_in, 1)
            act.activation(ee, ee, ACT.Exp).then_inc(self_exp, 1)
            act.wait_ge(gb_in, 16)
            trips = act.value_load(gcount[0:1, 0:1], min_val=1, max_val=GTRIPS)

            def turn(r, need):
                act.wait_ge(ohp_ready, need)
                flat = ps[:, 2 * r:2 * r + 2, :].rearrange("p b n -> p (b n)")[:, 0:GRP * P]
                act.activation(oht[:, r, :, :].rearrange("p c n -> p (c n)"), flat, ACT.Copy).then_inc(oht_ready, 1)

            turn(0, 1)
            with act.Fori(0, trips) as i:
                for m in range(GR):
                    r = m % 2
                    turn(1 - r, i * GR + (m + 2))
                    act.wait_ge(z_ready, i * GR + (m + 1))
                    act.wait_ge(sum_ready, i * GR + (m + 1))
                    act.activation(vals[:, r, :, HF:TW], zt, ACT.Exp).then_inc(ez_ready, 1)
            nv[0] += 1
            root(lst[:, 1, :], nv[0])
            act.wait_ge(tops_done, 2)
            act.activation(wts[:, 0, :], wts[:, 0, :], ACT.Exp).then_inc(exp_ready, 1)
            gelus(E1, C1, b1b, NBLK * E0, NBLK, NBLK * E0 * C0)


_ORDER = ["x", "adj", "adjT", "edge_index", "W0T", "b0", "Wr", "br", "lngb", "W1a", "b1a", "W2a", "b2a",
          "Wg", "WgT", "attn", "W_gat", "att_src", "att_dst", "b_gat", "ln_gamma", "ln_beta",
          "W1b", "b1b", "W2b", "b2b"]


def kernel(x, adj, L0_gnn_W, L0_gnn_b, L0_ffn_Wr, L0_ffn_br, L0_ffn_ln_g, L0_ffn_ln_b, L0_ffn_W1, L0_ffn_b1,
           L0_ffn_W2, L0_ffn_b2, L1_gnn_W, L1_gnn_attn_src, L1_gnn_attn_dst, L1_ffn_W_gat, L1_ffn_att_src,
           L1_ffn_att_dst, L1_ffn_b_gat, L1_ffn_ln_gamma, L1_ffn_ln_beta, L1_ffn_W1, L1_ffn_b1, L1_ffn_W2,
           L1_ffn_b2, L1_ffn_edge_index):
    import numpy as np
    import concourse.bacc as bacc
    from concourse.bass_utils import run_bass_kernel_spmd

    A = np.ascontiguousarray
    n = x.shape[0]

    def cols(b):
        b = np.asarray(b)
        return A(b.reshape(b.shape[0], -1, 128).transpose(2, 0, 1).reshape(128, -1))

    def down(w):
        w = np.asarray(w)
        return A(w.reshape(w.shape[0], -1, 128, w.shape[2]).transpose(2, 0, 1, 3))

    adj = np.asarray(adj)
    arrays = {
        "x": A(x), "adj": A(adj), "adjT": A(adj.reshape(4, n // 4, n).transpose(0, 2, 1)),
        "edge_index": A(L1_ffn_edge_index),
        "W0T": A(np.asarray(L0_gnn_W).T), "b0": A(L0_gnn_b), "Wr": A(L0_ffn_Wr), "br": A(L0_ffn_br),
        "lngb": A(np.stack([np.asarray(L0_ffn_ln_g).T, np.asarray(L0_ffn_ln_b).T], axis=1)),
        "W1a": A(np.asarray(L0_ffn_W1).transpose(1, 0, 2)), "b1a": cols(L0_ffn_b1), "W2a": down(L0_ffn_W2), "b2a": A(L0_ffn_b2),
        "Wg": A(L1_gnn_W), "WgT": A(np.asarray(L1_gnn_W).T),
        "attn": A(np.concatenate([np.asarray(L1_gnn_attn_src), np.asarray(L1_gnn_attn_dst)]).T),
        "W_gat": A(L1_ffn_W_gat), "att_src": A(np.asarray(L1_ffn_att_src).reshape(-1)),
        "att_dst": A(np.asarray(L1_ffn_att_dst).reshape(-1)), "b_gat": A(L1_ffn_b_gat),
        "ln_gamma": A(L1_ffn_ln_gamma), "ln_beta": A(L1_ffn_ln_beta),
        "W1b": A(np.asarray(L1_ffn_W1).transpose(1, 0, 2)), "b1b": cols(L1_ffn_b1), "W2b": down(L1_ffn_W2), "b2b": A(L1_ffn_b2),
    }
    nc = bacc.Bacc("TRN2", target_bir_lowering=False, num_devices=1)
    d = {k: nc.dram_tensor(f"in_{k}", arrays[k].shape, mybir.dt.from_np(arrays[k].dtype), kind="ExternalInput").ap()
         for k in _ORDER}
    out = nc.dram_tensor("out_0", (n, 128), F32, kind="ExternalOutput").ap()
    build(nc, d, out)
    r = run_bass_kernel_spmd(nc, [{f"in_{k}": arrays[k] for k in _ORDER}], core_ids=[0])
    return r.results[0]["out_0"]
```
